# Optimizing a Trainium2 kernel written in Bass

```python
import numpy as np
import jax
import jax.numpy as jnp

def _softmax(x, axis=-1):
    return jax.nn.softmax(x, axis=axis)

def _gelu(x):
    return jax.nn.gelu(x, approximate=True)

def _silu(x):
    return jax.nn.silu(x)

def _sigmoid(x):
    return jax.nn.sigmoid(x)

def _layernorm(x, axis=-1, eps=1e-05):
    m = jnp.mean(x, axis=axis, keepdims=True)
    v = jnp.var(x, axis=axis, keepdims=True)
    return (x - m) / jnp.sqrt(v + eps)

def _scatter_add(tgt, idx, src, axis=0):
    return tgt.at[idx].add(src)

def _segment_sum(src, seg, n):
    return jax.ops.segment_sum(src, seg, n)
kernel_name = 'mk_decoder_preln_d2_seqx_r8_a4bdd4'

def setup_inputs(seed: int=0):
    np.random.seed(seed)
    _w = jnp.asarray

    def _rec_inputs():
        import jax
        import jax.numpy as jnp
        _rk = jax.random.key(seed)
        x = -0.000125 + 0.9999 * jax.random.normal(jax.random.fold_in(_rk, 1), (128, 64, 128), jnp.float32)
        _lenS = 64 - jax.random.randint(jax.random.fold_in(_rk, 7), (128,), 0, max(1, 64 // 4) + 1, jnp.int32)
        _lenS2 = 64 - jax.random.randint(jax.random.fold_in(_rk, 8), (128,), 0, max(1, 64 // 4) + 1, jnp.int32)
        _ctx_1024P = jax.random.normal(jax.random.fold_in(_rk, 11), (128, 16, 128), jnp.float32)
        _ctx_1024c = jax.random.dirichlet(jax.random.fold_in(_rk, 511), 0.3 * jnp.ones((16,), jnp.float32), (128, 64))
        _ctx_1024t = jnp.einsum('bsk,bkd->bsd', _ctx_1024c, _ctx_1024P)
        _ctx_1024t = _ctx_1024t * jax.lax.rsqrt(jnp.mean(jnp.square(_ctx_1024t)) + 1e-12) * 0.953939
        ctx_1024 = -1.52775e-05 + 0.999936 * (_ctx_1024t + 0.3 * jax.random.normal(jax.random.fold_in(_rk, 611), (128, 64, 128), jnp.float32))
        _validS = jnp.arange(64)[None, :] < _lenS[:, None]
        _validS2 = jnp.arange(64)[None, :] < _lenS2[:, None]
        _causal = jnp.tril(jnp.ones((64, 64), dtype=bool))
        mask_BxSxS2_ff0 = jnp.where(jnp.ones((128, 64, 64), dtype=bool), 0.0, -1000000000.0).astype(jnp.float32)
        return (x, ctx_1024, mask_BxSxS2_ff0)
    x, ctx_1024, mask_BxSxS2_ff0 = _rec_inputs()

    def _L0_attn_setup():
        import jax, jax.numpy as jnp
        import numpy as np
        import math
        NUM_HEADS = 16
        TPMS_WEIGHT = 0.3
        TWO_PI = 2.0 * math.pi

        def _tpms_mask(L, phase, threshold, temperature):
            pos = jnp.arange(L, dtype=jnp.float32) / L * TWO_PI
            pq = pos[None, :, None] + phase[:, 0][:, None, None]
            pk = pos[None, None, :] + phase[:, 1][:, None, None]
            pz = (pos[None, :, None] + pos[None, None, :]) * 0.5 + phase[:, 2][:, None, None]
            t = jax.lax.stop_gradient(threshold)
            val = jnp.sin(pq) * jnp.cos(pk) + jnp.sin(pk) * jnp.cos(pz) + jnp.sin(pz) * jnp.cos(pq) - t
            return jax.nn.sigmoid(val / (temperature + 1e-06))
        key = jax.random.key(seed)
        ks = jax.random.split(key, 8)
        B, L, H = (2, 256, 128)
        nh = NUM_HEADS
        std = 0.02
        x = jax.random.normal(ks[0], (B, L, H), dtype=jnp.float32)
        Wq = jax.random.normal(ks[1], (H, H), dtype=jnp.float32) * std
        Wk = jax.random.normal(ks[2], (H, H), dtype=jnp.float32) * std
        Wv = jax.random.normal(ks[3], (H, H), dtype=jnp.float32) * std
        Wo = jax.random.normal(ks[4], (H, H), dtype=jnp.float32) * std
        bq = jnp.zeros((H,), jnp.float32)
        bk = jnp.zeros((H,), jnp.float32)
        bv = jnp.zeros((H,), jnp.float32)
        bo = jnp.zeros((H,), jnp.float32)
        phase = jax.random.normal(ks[5], (nh, 3), dtype=jnp.float32) * 0.5
        threshold = jnp.array(0.0, jnp.float32)
        temperature = jnp.array(1.0, jnp.float32)
        return {'x': x, 'Wq': Wq, 'bq': bq, 'Wk': Wk, 'bk': bk, 'Wv': Wv, 'bv': bv, 'Wo': Wo, 'bo': bo, 'phase': phase, 'threshold': threshold, 'temperature': temperature}
    _L0_attn_all = _L0_attn_setup()
    _L0_attn_in = {k: v for k, v in _L0_attn_all.items() if k in ('Wq', 'bq', 'Wk', 'bk', 'Wv', 'bv', 'Wo', 'bo', 'phase', 'threshold', 'temperature')}
    del _L0_attn_all

    def _L0_xattn_setup():
        import jax, jax.numpy as jnp
        import numpy as np
        DECAY = 0.9
        key = jax.random.key(seed)
        k1, k2, k3 = jax.random.split(key, 3)
        B, S, D = (8, 512, 128)
        q = jax.random.normal(k1, (B, S, D), dtype=jnp.float32)
        k = jax.random.normal(k2, (B, S, D), dtype=jnp.float32)
        v = jax.random.normal(k3, (B, S, D), dtype=jnp.float32)
        return {'q': q, 'k': k, 'v': v}
    _L0_xattn_all = _L0_xattn_setup()
    _L0_xattn_in = {k: v for k, v in _L0_xattn_all.items() if k in ()}
    del _L0_xattn_all

    def _L0_ffn_setup():
        import jax, jax.numpy as jnp
        import numpy as np
        E = 8
        TOP_K = 2
        ROUTE_SCALE = 1.0
        ALPHA = 1.702
        LIMIT = 7.0
        D = 128
        F = 128
        B, S = (2, 128)

        def swiglu(h):
            g = jnp.minimum(h[..., ::2], LIMIT)
            l = jnp.clip(h[..., 1::2], -LIMIT, LIMIT)
            return g * jax.nn.sigmoid(ALPHA * g) * (l + 1.0)
        if __name__ == '__main__':
            out = reference(**setup_inputs())
            print(out.shape, out.dtype)
        key = jax.random.key(seed)
        ks = jax.random.split(key, 16)
        sd = 1.0 / np.sqrt(D)
        sf = 1.0 / np.sqrt(F)
        return {'x': jax.random.normal(ks[0], (B, S, D), jnp.float32), 'gate_w': jax.random.normal(ks[1], (E, D), jnp.float32) * sd, 'gate_b': jax.random.normal(ks[2], (E,), jnp.float32) * 0.01, 'w1': jax.random.normal(ks[3], (E, 2 * F, D), jnp.float32) * sd, 'b1': jax.random.normal(ks[4], (E, 2 * F), jnp.float32) * 0.01, 'w3': jax.random.normal(ks[5], (E, 2 * F, D), jnp.float32) * sd, 'b3': jax.random.normal(ks[6], (E, 2 * F), jnp.float32) * 0.01, 'w2': jax.random.normal(ks[7], (E, D, F), jnp.float32) * sf, 'b2': jax.random.normal(ks[8], (E, D), jnp.float32) * 0.01, 'sw1': jax.random.normal(ks[9], (2 * F, D), jnp.float32) * sd, 'sb1': jax.random.normal(ks[10], (2 * F,), jnp.float32) * 0.01, 'sw3': jax.random.normal(ks[11], (2 * F, D), jnp.float32) * sd, 'sb3': jax.random.normal(ks[12], (2 * F,), jnp.float32) * 0.01, 'sw2': jax.random.normal(ks[13], (D, F), jnp.float32) * sf, 'sb2': jax.random.normal(ks[14], (D,), jnp.float32) * 0.01}
    _L0_ffn_all = _L0_ffn_setup()
    _L0_ffn_in = {k: v for k, v in _L0_ffn_all.items() if k in ('gate_w', 'gate_b', 'w1', 'b1', 'w3', 'b3', 'w2', 'b2', 'sw1', 'sb1', 'sw3', 'sb3', 'sw2', 'sb2')}
    del _L0_ffn_all

    def _L1_attn_setup():
        import jax, jax.numpy as jnp
        import numpy as np
        import math
        N_HEAD = 16
        LATENT_RANK = 64
        key = jax.random.key(seed)
        ks = jax.random.split(key, 8)
        B, T, C, H, R = (4, 256, 128, N_HEAD, LATENT_RANK)
        std = 0.02
        return {'hidden_states': jax.random.normal(ks[0], (B, T, C), jnp.float32), 'basis_w': jax.random.normal(ks[1], (R, C), jnp.float32) * std, 'core': jax.random.normal(ks[2], (R, R), jnp.float32) * std, 'head_residual': jax.random.normal(ks[3], (H, R, R), jnp.float32) * (std / 10.0), 'v_w': jax.random.normal(ks[4], (C, C), jnp.float32) * std, 'v_b': jnp.zeros((C,), jnp.float32), 'o_w': jax.random.normal(ks[5], (C, C), jnp.float32) * std, 'o_b': jnp.zeros((C,), jnp.float32)}
    _L1_attn_all = _L1_attn_setup()
    _L1_attn_in = {k: v for k, v in _L1_attn_all.items() if k in ('basis_w', 'core', 'head_residual', 'v_w', 'v_b', 'o_w', 'o_b')}
    del _L1_attn_all

    def _L1_xattn_setup():
        import jax, jax.numpy as jnp
        import numpy as np
        DIM = 128
        CTX_DIM = 128
        HEADS = 16
        DIM_HEAD = 64
        INNER = HEADS * DIM_HEAD
        FF_INNER = 4 * DIM
        EPS = 1e-05

        def layer_norm(x, g, b):
            mu = jnp.mean(x, axis=-1, keepdims=True)
            var = jnp.var(x, axis=-1, keepdims=True)
            return (x - mu) * jax.lax.rsqrt(var + EPS) * g + b
        key = jax.random.key(seed)
        ks = jax.random.split(key, 10)
        b, n, j = (2, 256, 256)
        x = jax.random.normal(ks[0], (b, n, DIM), dtype=jnp.float32)
        context = jax.random.normal(ks[1], (b, j, CTX_DIM), dtype=jnp.float32)
        mask = jnp.zeros((b, n, j), dtype=jnp.float32)
        s = 0.02
        Wq = jax.random.normal(ks[2], (DIM, INNER), dtype=jnp.float32) * s
        Wkv = jax.random.normal(ks[3], (CTX_DIM, 2 * DIM_HEAD), dtype=jnp.float32) * s
        Wout = jax.random.normal(ks[4], (INNER, DIM), dtype=jnp.float32) * s
        W1 = jax.random.normal(ks[5], (DIM, 2 * FF_INNER), dtype=jnp.float32) * s
        W2 = jax.random.normal(ks[6], (FF_INNER, DIM), dtype=jnp.float32) * s
        ln_g = jnp.ones((DIM,), jnp.float32)
        ln_b = jnp.zeros((DIM,), jnp.float32)
        cln_g = jnp.ones((CTX_DIM,), jnp.float32)
        cln_b = jnp.zeros((CTX_DIM,), jnp.float32)
        return {'x': x, 'context': context, 'mask': mask, 'ln_g': ln_g, 'ln_b': ln_b, 'cln_g': cln_g, 'cln_b': cln_b, 'Wq': Wq, 'Wkv': Wkv, 'Wout': Wout, 'W1': W1, 'W2': W2}
    _L1_xattn_all = _L1_xattn_setup()
    _L1_xattn_in = {k: v for k, v in _L1_xattn_all.items() if k in ('ln_g', 'ln_b', 'cln_g', 'cln_b', 'Wq', 'Wkv', 'Wout', 'W1', 'W2')}
    del _L1_xattn_all

    def _L1_ffn_setup():
        import jax, jax.numpy as jnp
        import numpy as np
        TOP_K = 2
        key = jax.random.key(seed)
        k1, k2, k3, k4 = jax.random.split(key, 4)
        B, T, D, H, E = (2, 256, 128, 256, 8)
        x = jax.random.normal(k1, (B, T, D), dtype=jnp.float32)
        w12 = jax.random.normal(k2, (E, 2 * H, D), dtype=jnp.float32) * D ** (-0.5)
        w3 = jax.random.normal(k3, (E, D, H), dtype=jnp.float32) * H ** (-0.5)
        gate_w = jax.random.normal(k4, (E, D), dtype=jnp.float32) * D ** (-0.5)
        return {'x': x, 'w12': w12, 'w3': w3, 'gate_w': gate_w}
    _L1_ffn_all = _L1_ffn_setup()
    _L1_ffn_in = {k: v for k, v in _L1_ffn_all.items() if k in ('w12', 'w3', 'gate_w')}
    del _L1_ffn_all
    return {'x': x, 'ctx_1024': ctx_1024, 'mask_BxSxS2_ff0': mask_BxSxS2_ff0, 'L0_attn_Wq': _L0_attn_in['Wq'], 'L0_attn_bq': _L0_attn_in['bq'], 'L0_attn_Wk': _L0_attn_in['Wk'], 'L0_attn_bk': _L0_attn_in['bk'], 'L0_attn_Wv': _L0_attn_in['Wv'], 'L0_attn_bv': _L0_attn_in['bv'], 'L0_attn_Wo': _L0_attn_in['Wo'], 'L0_attn_bo': _L0_attn_in['bo'], 'L0_attn_phase': _L0_attn_in['phase'], 'L0_attn_threshold': _L0_attn_in['threshold'], 'L0_attn_temperature': _L0_attn_in['temperature'], 'L0_ffn_gate_w': _L0_ffn_in['gate_w'], 'L0_ffn_gate_b': _L0_ffn_in['gate_b'], 'L0_ffn_w1': _L0_ffn_in['w1'], 'L0_ffn_b1': _L0_ffn_in['b1'], 'L0_ffn_w3': _L0_ffn_in['w3'], 'L0_ffn_b3': _L0_ffn_in['b3'], 'L0_ffn_w2': _L0_ffn_in['w2'], 'L0_ffn_b2': _L0_ffn_in['b2'], 'L0_ffn_sw1': _L0_ffn_in['sw1'], 'L0_ffn_sb1': _L0_ffn_in['sb1'], 'L0_ffn_sw3': _L0_ffn_in['sw3'], 'L0_ffn_sb3': _L0_ffn_in['sb3'], 'L0_ffn_sw2': _L0_ffn_in['sw2'], 'L0_ffn_sb2': _L0_ffn_in['sb2'], 'L1_attn_basis_w': _L1_attn_in['basis_w'], 'L1_attn_core': _L1_attn_in['core'], 'L1_attn_head_residual': _L1_attn_in['head_residual'], 'L1_attn_v_w': _L1_attn_in['v_w'], 'L1_attn_v_b': _L1_attn_in['v_b'], 'L1_attn_o_w': _L1_attn_in['o_w'], 'L1_attn_o_b': _L1_attn_in['o_b'], 'L1_xattn_ln_g': _L1_xattn_in['ln_g'], 'L1_xattn_ln_b': _L1_xattn_in['ln_b'], 'L1_xattn_cln_g': _L1_xattn_in['cln_g'], 'L1_xattn_cln_b': _L1_xattn_in['cln_b'], 'L1_xattn_Wq': _L1_xattn_in['Wq'], 'L1_xattn_Wkv': _L1_xattn_in['Wkv'], 'L1_xattn_Wout': _L1_xattn_in['Wout'], 'L1_xattn_W1': _L1_xattn_in['W1'], 'L1_xattn_W2': _L1_xattn_in['W2'], 'L1_ffn_w12': _L1_ffn_in['w12'], 'L1_ffn_w3': _L1_ffn_in['w3'], 'L1_ffn_gate_w': _L1_ffn_in['gate_w']}

def reference(x, ctx_1024, mask_BxSxS2_ff0, L0_attn_Wq, L0_attn_bq, L0_attn_Wk, L0_attn_bk, L0_attn_Wv, L0_attn_bv, L0_attn_Wo, L0_attn_bo, L0_attn_phase, L0_attn_threshold, L0_attn_temperature, L0_ffn_gate_w, L0_ffn_gate_b, L0_ffn_w1, L0_ffn_b1, L0_ffn_w3, L0_ffn_b3, L0_ffn_w2, L0_ffn_b2, L0_ffn_sw1, L0_ffn_sb1, L0_ffn_sw3, L0_ffn_sb3, L0_ffn_sw2, L0_ffn_sb2, L1_attn_basis_w, L1_attn_core, L1_attn_head_residual, L1_attn_v_w, L1_attn_v_b, L1_attn_o_w, L1_attn_o_b, L1_xattn_ln_g, L1_xattn_ln_b, L1_xattn_cln_g, L1_xattn_cln_b, L1_xattn_Wq, L1_xattn_Wkv, L1_xattn_Wout, L1_xattn_W1, L1_xattn_W2, L1_ffn_w12, L1_ffn_w3, L1_ffn_gate_w):
    import jax
    import jax.numpy as jnp

    def _L0_attn_ref(x, Wq, bq, Wk, bk, Wv, bv, Wo, bo, phase, threshold, temperature):
        import jax, jax.numpy as jnp
        import numpy as np
        import math
        NUM_HEADS = 16
        TPMS_WEIGHT = 0.3
        TWO_PI = 2.0 * math.pi

        def _tpms_mask(L, phase, threshold, temperature):
            pos = jnp.arange(L, dtype=jnp.float32) / L * TWO_PI
            pq = pos[None, :, None] + phase[:, 0][:, None, None]
            pk = pos[None, None, :] + phase[:, 1][:, None, None]
            pz = (pos[None, :, None] + pos[None, None, :]) * 0.5 + phase[:, 2][:, None, None]
            t = jax.lax.stop_gradient(threshold)
            val = jnp.sin(pq) * jnp.cos(pk) + jnp.sin(pk) * jnp.cos(pz) + jnp.sin(pz) * jnp.cos(pq) - t
            return jax.nn.sigmoid(val / (temperature + 1e-06))
        B, L, H = x.shape
        nh = NUM_HEADS
        hd = H // nh
        scale = math.sqrt(hd)
        Q = (x @ Wq + bq).reshape(B, L, nh, hd).transpose(0, 2, 1, 3)
        K = (x @ Wk + bk).reshape(B, L, nh, hd).transpose(0, 2, 1, 3)
        V = (x @ Wv + bv).reshape(B, L, nh, hd).transpose(0, 2, 1, 3)
        scores = jnp.einsum('bhqd,bhkd->bhqk', Q, K) / scale
        mask = _tpms_mask(L, phase, threshold, temperature)
        scores = scores + TPMS_WEIGHT * jnp.log(mask + 1e-06)[None]
        attn = jax.nn.softmax(scores, axis=-1)
        out = jnp.einsum('bhqk,bhkd->bhqd', attn, V)
        out = out.transpose(0, 2, 1, 3).reshape(B, L, H)
        return out @ Wo + bo

    def _L0_xattn_ref(q, k, v):
        import jax, jax.numpy as jnp
        import numpy as np
        DECAY = 0.9
        kv = jnp.swapaxes(k * v, 0, 1)

        def step(r, kv_t):
            r = DECAY * r + kv_t
            return (r, r)
        r0 = jnp.zeros(q.shape[:1] + q.shape[2:], dtype=q.dtype)
        _, rs = jax.lax.scan(step, r0, kv)
        return q * jnp.swapaxes(rs, 0, 1)

    def _L0_ffn_ref(x, gate_w, gate_b, w1, b1, w3, b3, w2, b2, sw1, sb1, sw3, sb3, sw2, sb2):
        import jax, jax.numpy as jnp
        import numpy as np
        E = 8
        TOP_K = 2
        ROUTE_SCALE = 1.0
        ALPHA = 1.702
        LIMIT = 7.0
        D = 128
        F = 128
        B, S = (2, 128)

        def swiglu(h):
            g = jnp.minimum(h[..., ::2], LIMIT)
            l = jnp.clip(h[..., 1::2], -LIMIT, LIMIT)
            return g * jax.nn.sigmoid(ALPHA * g) * (l + 1.0)
        if __name__ == '__main__':
            out = reference(**setup_inputs())
            print(out.shape, out.dtype)
        inp_shape = x.shape
        xt = x.reshape(-1, D)
        logits = xt @ gate_w.T
        scores = jax.nn.softmax(logits.astype(jnp.float32), axis=-1)
        biased = scores + gate_b.astype(jnp.float32)
        idx = jax.lax.top_k(biased, TOP_K)[1]
        weights = (jnp.take_along_axis(scores, idx, axis=-1) * ROUTE_SCALE).astype(x.dtype)
        cw = jnp.sum(jax.nn.one_hot(idx, E, dtype=x.dtype) * weights[..., None], axis=1)
        h1 = jnp.einsum('td,efd->etf', xt, w1) + b1[:, None, :]
        h3 = jnp.einsum('td,efd->etf', xt, w3) + b3[:, None, :]
        a = swiglu(h1 * h3)
        y = jnp.einsum('etf,edf->etd', a, w2) + b2[:, None, :]
        routed = jnp.einsum('te,etd->td', cw, y)
        sh = swiglu((xt @ sw1.T + sb1) * (xt @ sw3.T + sb3))
        shared = sh @ sw2.T + sb2
        return (routed + shared).reshape(inp_shape)

    def _L1_attn_ref(hidden_states, basis_w, core, head_residual, v_w, v_b, o_w, o_b):
        import jax, jax.numpy as jnp
        import numpy as np
        import math
        N_HEAD = 16
        LATENT_RANK = 64
        B, T, C = hidden_states.shape
        H = N_HEAD
        R = LATENT_RANK
        head_dim = C // H
        latent = jnp.einsum('btc,rc->btr', hidden_states, basis_w)
        core_sym = 0.5 * (core + core.T)
        centered = head_residual - head_residual.mean(axis=0, keepdims=True)
        head_mats = core_sym[None] / float(H) + centered
        lt = jnp.einsum('btr,hrs->bhts', latent, head_mats)
        att = jnp.einsum('bhts,bus->bhtu', lt, latent) * (1.0 / math.sqrt(R))
        causal = jnp.tril(jnp.ones((T, T), jnp.bool_))
        att = jnp.where(causal[None, None], att, jnp.float32(-jnp.inf))
        att = jax.nn.softmax(att, axis=-1)
        v = (hidden_states @ v_w.T + v_b).reshape(B, T, H, head_dim).transpose(0, 2, 1, 3)
        y = att @ v
        y = y.transpose(0, 2, 1, 3).reshape(B, T, C)
        y = y @ o_w.T + o_b
        return y

    def _L1_xattn_ref(x, context, mask, ln_g, ln_b, cln_g, cln_b, Wq, Wkv, Wout, W1, W2):
        import jax, jax.numpy as jnp
        import numpy as np
        DIM = 128
        CTX_DIM = 128
        HEADS = 16
        DIM_HEAD = 64
        INNER = HEADS * DIM_HEAD
        FF_INNER = 4 * DIM
        EPS = 1e-05

        def layer_norm(x, g, b):
            mu = jnp.mean(x, axis=-1, keepdims=True)
            var = jnp.var(x, axis=-1, keepdims=True)
            return (x - mu) * jax.lax.rsqrt(var + EPS) * g + b
        scale = DIM_HEAD ** (-0.5)
        xn = layer_norm(x, ln_g, ln_b)
        cn = layer_norm(context, cln_g, cln_b)
        b, n, _ = xn.shape
        q = (xn @ Wq).reshape(b, n, HEADS, DIM_HEAD).transpose(0, 2, 1, 3) * scale
        kv = cn @ Wkv
        k, v = jnp.split(kv, 2, axis=-1)
        sim = jnp.einsum('bhid,bjd->bhij', q, k) + mask[:, None, :, :]
        attn = jax.nn.softmax(sim, axis=-1)
        out = jnp.einsum('bhij,bjd->bhid', attn, v)
        out = out.transpose(0, 2, 1, 3).reshape(b, n, INNER) @ Wout
        h = xn @ W1
        val, gate = jnp.split(h, 2, axis=-1)
        out = out + jax.nn.silu(gate) * val @ W2
        return out

    def _L1_ffn_ref(x, w12, w3, gate_w):
        import jax, jax.numpy as jnp
        import numpy as np
        TOP_K = 2
        E = gate_w.shape[0]
        H = w3.shape[-1]
        scores = jnp.einsum('btd,ed->bte', x, gate_w)
        topk_scores, topk_idx = jax.lax.top_k(scores, TOP_K)
        topk_probs = jax.nn.softmax(topk_scores, axis=-1)
        total_probs = jnp.sum(jax.nn.one_hot(topk_idx, E, dtype=topk_probs.dtype) * topk_probs[..., None], axis=-2)
        h12 = jnp.einsum('btd,ehd->bteh', x, w12)
        h1, h2 = (h12[..., :H], h12[..., H:])
        hidden = jax.nn.silu(h1) * h2
        expert_out = jnp.einsum('bteh,edh->bted', hidden, w3)
        y = jnp.sum(total_probs[..., None] * expert_out, axis=-2)
        return y
    x = x + _L0_attn_ref(_layernorm(x, axis=-1), L0_attn_Wq, L0_attn_bq, L0_attn_Wk, L0_attn_bk, L0_attn_Wv, L0_attn_bv, L0_attn_Wo, L0_attn_bo, L0_attn_phase, L0_attn_threshold, L0_attn_temperature)
    x = x + _L0_xattn_ref(_layernorm(x, axis=-1), ctx_1024, ctx_1024)
    x = x + _L0_ffn_ref(_layernorm(x, axis=-1), L0_ffn_gate_w, L0_ffn_gate_b, L0_ffn_w1, L0_ffn_b1, L0_ffn_w3, L0_ffn_b3, L0_ffn_w2, L0_ffn_b2, L0_ffn_sw1, L0_ffn_sb1, L0_ffn_sw3, L0_ffn_sb3, L0_ffn_sw2, L0_ffn_sb2)
    x = x + _L1_attn_ref(_layernorm(x, axis=-1), L1_attn_basis_w, L1_attn_core, L1_attn_head_residual, L1_attn_v_w, L1_attn_v_b, L1_attn_o_w, L1_attn_o_b)
    x = x + _L1_xattn_ref(_layernorm(x, axis=-1), ctx_1024, mask_BxSxS2_ff0, L1_xattn_ln_g, L1_xattn_ln_b, L1_xattn_cln_g, L1_xattn_cln_b, L1_xattn_Wq, L1_xattn_Wkv, L1_xattn_Wout, L1_xattn_W1, L1_xattn_W2)
    x = x + _L1_ffn_ref(_layernorm(x, axis=-1), L1_ffn_w12, L1_ffn_w3, L1_ffn_gate_w)
    return x

_drawn_inputs = setup_inputs


def setup_inputs(seed=0):
    import zlib

    import numpy as np

    out = dict(_drawn_inputs(seed))
    spreads = {'L0_attn_bq': (0.0, 0.8),
     'L0_attn_bk': (0.0, 2.0),
     'L0_attn_bv': (0.0, 0.36),
     'L0_attn_bo': (0.0, 0.1),
     'L1_attn_v_b': (0.0, 0.8),
     'L1_attn_o_b': (0.0, 0.8),
     'L1_xattn_ln_g': (1.0, 0.6),
     'L1_xattn_ln_b': (0.0, 0.8),
     'L1_xattn_cln_g': (1.0, 0.6),
     'L1_xattn_cln_b': (0.0, 0.8)}
    factors = {'L0_attn_Wq': 8.0,
     'L0_attn_Wk': 8.0,
     'L0_attn_Wv': 8.0,
     'L0_attn_Wo': 2.681,
     'L0_attn_phase': 8.0,
     'L0_ffn_gate_b': 28.232,
     'L0_ffn_b1': 64.0,
     'L0_ffn_b3': 64.0,
     'L0_ffn_b2': 64.0,
     'L0_ffn_sb1': 37.895,
     'L0_ffn_sb3': 41.306,
     'L0_ffn_sb2': 42.986,
     'L1_attn_basis_w': 8.0,
     'L1_attn_core': 8.0,
     'L1_attn_head_residual': 8.0,
     'L1_attn_v_w': 8.0,
     'L1_attn_o_w': 8.0,
     'L1_xattn_Wq': 8.0,
     'L1_xattn_Wkv': 7.344,
     'L1_xattn_Wout': 7.436,
     'L1_xattn_W1': 8.0,
     'L1_xattn_W2': 8.0,
     'L1_ffn_w12': 3.237,
     'L1_ffn_w3': 3.197,
     'L1_ffn_gate_w': 3.742}
    for name, (base, spread) in spreads.items():
        noise = np.random.default_rng([zlib.crc32(name.encode()), seed]).standard_normal(out[name].shape)
        drawn = base * np.exp(spread * noise) if base else spread * noise
        out[name] = jnp.asarray(drawn.astype(out[name].dtype))
    for name, factor in factors.items():
        out[name] = (out[name] * factor).astype(out[name].dtype)
    return out
```

```python
import math
from contextlib import ExitStack, contextmanager

import concourse.bass as bass
from concourse import mybir

F32 = mybir.dt.float32
ALU = mybir.AluOpType
ACT = mybir.ActivationFunctionType
AX = mybir.AxisListType

B, S, D = 128, 64, 128
TOK = B * S
P = 128
TILE = 2 * S
NT = TOK // TILE
ST = 512
NS = TOK // ST
JT = ST // TILE
H = 16
HD = D // H
HK = H * S
EPS = 1e-5


def wait(eng, sem, value):
    if not (isinstance(value, int) and value <= 0):
        eng.wait_ge(sem, value)


def at_most(value, limit):
    return min(value, limit) if isinstance(value, int) else value


def apart(eng, sem):
    eng.sem_inc(sem, 1)


def over_steps(eng, n, *stages):
    deepest = max(lag for lag, _ in stages)
    first = deepest + 2 + (deepest % 2)

    def step(k):
        for lag, fn in stages:
            if 0 <= k - lag < n:
                fn(k - lag, (k - lag) % 2, (k - lag) // 2)

    for k in range(first):
        step(k)
    with eng.Fori(first // 2, n // 2) as j:
        for p in range(2):
            for lag, fn in stages:
                fn(j * 2 + (p - lag), (p - lag) % 2, j + (p - lag) // 2)
    for k in range(n, n + deepest):
        step(k)


def rows_of(dram, i, size):
    return dram[bass.ds(i * size, size), :].rearrange("(j p) d -> p j d", p=P)


@contextmanager
def phase(nc, name):
    taken = []

    def sem(part):
        taken.append(nc.alloc_semaphore(name=f"{name}_{part}"))
        return taken[-1]

    with ExitStack() as ctx:
        def sb(part, shape):
            return ctx.enter_context(nc.sbuf_tensor(f"{name}_{part}", shape, F32))

        def ps(part, shape):
            return ctx.enter_context(nc.psum_tensor(f"{name}_{part}", shape, F32))

        def sems(*parts):
            return [sem(part) for part in parts]

        def pair(part):
            return [sem(f"{part}{u}") for u in range(2)]

        yield sb, ps, sem, sems, pair, lambda: ctx.enter_context(nc.Block())
    nc.clear_and_free_semaphores(taken)
    nc.all_engine_barrier()


def layer_norm(sb, sems, name, n=JT):
    stats, moments = sb(f"{name}_stats", [P, n, 6]), sb(f"{name}_moments", [P, n, 2])
    var_eps, rstd, power = (sb(f"{name}_{x}", [P, n]) for x in ("var_eps", "rstd", "power"))
    stats_done, moments_done, eps_added, rstd_done, power_set, apart_dve, apart_pool = sems(*(
        f"{name}_{x}" for x in ("stats_done", "moments_done", "eps_added", "rstd_done", "power_set", "apart_dve",
                                "apart_pool")))

    def set_up(pool):
        pool.memset(power[:, :], -0.5).then_inc(power_set, 1)
        pool.wait_ge(power_set, 1)

    def measure(dve, rows, i):
        for j in range(n):
            last = dve.bn_stats(stats[:, j, :], rows[:, j, :])
        last.then_inc(stats_done, 1)
        dve.wait_ge(stats_done, i + 1)
        apart(dve, apart_dve)
        for j in range(n):
            last = dve.bn_aggr(moments[:, j, :], stats[:, j, :])
        last.then_inc(moments_done, 1)

    def invert(pool, i):
        pool.wait_ge(moments_done, i + 1)
        apart(pool, apart_pool)
        pool.tensor_scalar(var_eps[:, :], moments[:, :, 1], EPS, 0.0, ALU.add, ALU.add).then_inc(eps_added, 1)
        pool.wait_ge(eps_added, i + 1)
        pool.tensor_tensor(rstd[:, :], var_eps[:, :], power[:, :], ALU.pow).then_inc(rstd_done, 1)

    def apply(dve, out, rows, i, done):
        dve.wait_ge(rstd_done, i + 1)
        for j in range(n):
            last = dve.tensor_scalar(out[:, j, :], rows[:, j, :], moments[:, j, 0:1], rstd[:, j:j + 1],
                                     ALU.subtract, ALU.mult)
        last.then_inc(done, 1)

    return set_up, measure, invert, apply


def project(nc, io, layer):
    with phase(nc, f"project{layer}") as (sb, ps, sem, sems, pair, open_block):
        R = D if layer == 0 else io["latent"]
        wq, wk, wv, ident = (sb(n, [P, w]) for n, w in (("wq", P), ("wk", R), ("wv", P), ("ident", P)))
        bq, bqs, bk = (sb(n, [P, 1]) for n in ("bq", "bqs", "bk"))
        rows = sb("rows", [P, 2, JT, D])
        xn = sb("xn", [P, 2, JT, D])
        xnT = sb("xnT", [P, 2, ST])
        q, k, v = (sb(n, [P, 2, ST]) for n in ("q", "k", "v"))
        tp, qp, kp, vp = (ps(n, [P, 2, ST]) for n in ("tp", "qp", "kp", "vp"))
        set_up, measure, invert, apply = layer_norm(sb, sems, "ln")
        x_in, stored = pair("x_in"), pair("stored")
        w_in, bias_scaled, xn_ready, t_done, xnT_ready, q_done, k_done, v_done, q_ready, k_ready, v_ready = sems(
            "w_in", "bias_scaled", "xn_ready", "t_done", "xnT_ready", "q_done", "k_done", "v_done",
            "q_ready", "k_ready", "v_ready")
        scale = HD ** -0.5
        block = open_block()
        if layer == 0:
            source, weights = io["x"], ((wq, io["L0_attn_Wq"]), (wk, io["L0_attn_Wk"]), (wv, io["L0_attn_Wv"]), (ident, io["ident"]),
                                     (bq, io["L0_attn_bq"]), (bk, io["L0_attn_bk"]))
            across, across_ready = q, q_ready
        else:
            source, weights = io["x3"], ((wk, io["basis_T"]), (wv, io["L1_attn_v_wT"]), (ident, io["ident"]))
            across, across_ready = xnT, xnT_ready
        WEIGHTS = len(weights) * 16

        @block.sync
        def _(sp):
            for dst, src in weights:
                sp.dma_start(dst[:, :], src[:, :]).then_inc(w_in, 16)

            def load(i, u, n):
                wait(sp, xn_ready, i - 1)
                sp.dma_start(rows[:, u, :, :], rows_of(source, i, ST)).then_inc(x_in[u], 16)

            def store(i, u, n):
                sp.wait_ge(across_ready, i + 1)
                sp.dma_start((io["QT"] if layer == 0 else io["xnT"])[:, bass.ds(i * ST, ST)],
                             across[:, u, :]).then_inc(stored[u], 16)
                sp.wait_ge(k_ready, i + 1)
                sp.dma_start((io["KT"] if layer == 0 else io["latT"])[:, bass.ds(i * ST, ST)],
                             k[0:R, u, :]).then_inc(stored[u], 16)
                sp.wait_ge(v_ready, i + 1)
                sp.dma_start(rows_of(io["V"], i, ST), v[:, u, :].rearrange("p (j d) -> p j d", d=D)).then_inc(stored[u], 16)

            over_steps(sp, NS, (0, load), (2, store))
            for u in range(2):
                sp.wait_ge(stored[u], 48 * (NS // 2))

        @block.vector
        def _(dve):
            def normalise(i, u, n):
                dve.wait_ge(x_in[u], n * 16 + 16)
                measure(dve, rows[:, u], i)
                wait(dve, t_done, i - 1)
                apply(dve, xn[:, u], rows[:, u], i, xn_ready)

            def evacuate(i, u, n):
                wait(dve, stored[u], n * 48)
                dve.wait_ge(k_done, i + 1)
                if layer == 0:
                    dve.tensor_scalar(k[:, u, :], kp[:, u, :], bk[:, 0:1], None, ALU.add).then_inc(k_ready, 1)
                else:
                    dve.tensor_copy(k[0:R, u, :], kp[0:R, u, :]).then_inc(k_ready, 1)
                dve.wait_ge(v_done, i + 1)
                dve.tensor_copy(v[:, u, :], vp[:, u, :]).then_inc(v_ready, 1)

            if layer == 0:
                dve.wait_ge(w_in, WEIGHTS)
                dve.tensor_scalar(bqs[:, :], bq[:, :], scale, None, ALU.mult).then_inc(bias_scaled, 1)
            over_steps(dve, NS, (0, normalise), (1, evacuate))

        @block.gpsimd
        def _(pool):
            set_up(pool)
            over_steps(pool, NS, (0, lambda i, u, n: invert(pool, i)))

        @block.tensor
        def _(pe):
            def transpose(i, u, n):
                pe.wait_ge(xn_ready, i + 1)
                wait(pe, xnT_ready, i - 1)
                for j in range(JT):
                    last = pe.transpose(tp[:, u, j * P:(j + 1) * P], xn[:, u, j, :], ident[:, :])
                last.then_inc(t_done, 1)

            def products(i, u, n):
                pe.wait_ge(xnT_ready, i + 1)
                if layer == 0:
                    wait(pe, q_ready, i - 1)
                    pe.matmul(qp[:, u, :], wq[:, :], xnT[:, u, :], start=True, stop=True).then_inc(q_done, 1)
                wait(pe, k_ready, i - 1)
                pe.matmul(kp[0:R, u, :], wk[:, :], xnT[:, u, :], start=True, stop=True).then_inc(k_done, 1)
                wait(pe, v_ready, i - 1)
                for j in range(JT):
                    last = pe.matmul(vp[:, u, j * P:(j + 1) * P], xnT[:, u, j * P:(j + 1) * P], wv[:, :],
                                     start=True, stop=True)
                last.then_inc(v_done, 1)

            pe.wait_ge(w_in, WEIGHTS)
            over_steps(pe, NS, (0, transpose), (1, products))

        @block.scalar
        def _(act):
            def evacuate_transpose(i, u, n):
                act.wait_ge(t_done, i + 1)
                wait(act, v_done, i - 1)
                if layer == 1:
                    wait(act, stored[u], n * 48)
                act.activation(xnT[:, u, :], tp[:, u, :], ACT.Copy).then_inc(xnT_ready, 1)

            def evacuate_q(i, u, n):
                act.wait_ge(q_done, i + 1)
                wait(act, stored[u], n * 48)
                act.activation(q[:, u, :], qp[:, u, :], ACT.Identity, bias=bqs[:, 0:1], scale=scale).then_inc(q_ready, 1)

            if layer == 0:
                act.wait_ge(bias_scaled, 1)
                over_steps(act, NS, (0, evacuate_transpose), (1, evacuate_q))
            else:
                over_steps(act, NS, (0, evacuate_transpose))


def tpms_bias(nc, io):
    with phase(nc, "tpms") as (sb, ps, sem, sems, pair, open_block):
        offsets = sb("offsets", [P, H, 3])
        thr, tmp = sb("thr", [P, 1]), sb("tmp", [P, 1])
        inv = sb("inv", [P, 1])
        pos_q, pos_k, pos_z = sb("pos_q", [P, 1]), sb("pos_k", [P, S]), sb("pos_z", [P, S])
        pq = sb("pq", [P, 2, H])
        pk, pz = sb("pk", [P, 2, H, S]), sb("pz", [P, 2, H, S])
        turns_q, turns_k = sb("turns_q", [P, 2, H]), sb("turns_k", [P, 2, H, S])
        val, part = sb("val", [P, H, S]), sb("part", [P, H, S])
        in_done, step, sines = sems("in_done", "step", "sines")
        block = open_block()
        MAGIC = 1.5 * 2.0 ** 23
        TURN_HIGH = 6.28125
        TURN_LOW = 2 * math.pi - TURN_HIGH
        angles = (pq, pk, pz)
        STEPS = 27

        @block.sync
        def _(sp):
            for dst, src in ((offsets[:, :, :], io["L0_attn_phase"].partition_broadcast(P)),
                             (thr[:, :], io["L0_attn_threshold"].partition_broadcast(P)),
                             (tmp[:, :], io["L0_attn_temperature"].partition_broadcast(P)),
                             (pos_q[:, :], io["pos_q"][:, :]), (pos_k[:, :], io["pos_k"][:, :]), (pos_z[:, :], io["pos_z"][:, :])):
                sp.dma_start(dst, src).then_inc(in_done, 16)
            sp.wait_ge(step, STEPS)
            sp.dma_start(io["bias0"][:, :], val[:, :, :].rearrange("p h s -> p (h s)")).then_inc(in_done, 16)
            sp.wait_ge(in_done, 7 * 16)

        @block.vector
        def _(dve):
            count = [0]

            def then(instruction):
                count[0] += 1
                instruction.then_inc(step, 1)
                dve.wait_ge(step, count[0])

            dve.wait_ge(in_done, 6 * 16)
            heads = lambda t: t[:, None, :].broadcast_to([P, H, S])
            keys = lambda n: offsets[:, :, n:n + 1].broadcast_to([P, H, S])
            dve.tensor_scalar(pq[:, 0, :], offsets[:, :, 0], pos_q[:, 0:1], None, ALU.add)
            dve.tensor_tensor(pk[:, 0], keys(1), heads(pos_k), ALU.add)
            then(dve.tensor_tensor(pz[:, 0], keys(2), heads(pos_z), ALU.add))
            for a in angles:
                last = dve.tensor_scalar(a[:, 1], a[:, 0], math.pi / 2, None, ALU.add)
            then(last)
            for a, t in ((pq, turns_q), (pk, turns_k), (pz, turns_k)):
                then(dve.tensor_scalar(t[:], a[:], 1 / (2 * math.pi), MAGIC, ALU.mult, ALU.add))
                then(dve.tensor_scalar(t[:], t[:], MAGIC, None, ALU.subtract))
                then(dve.scalar_tensor_tensor(out=a[:], in0=t[:], scalar=-TURN_HIGH, in1=a[:], op0=ALU.mult, op1=ALU.add))
                then(dve.scalar_tensor_tensor(out=a[:], in0=t[:], scalar=-TURN_LOW, in1=a[:], op0=ALU.mult, op1=ALU.add))
                then(dve.tensor_scalar(a[:], a[:], math.pi, -math.pi, ALU.min, ALU.max))
            then(dve.tensor_scalar(inv[:, :], tmp[:, :], 1e-6, None, ALU.add))
            then(dve.reciprocal(inv[:, :], inv[:, :]))
            dve.wait_ge(sines, 1)
            query = lambda n: pq[:, n, :, None].broadcast_to([P, H, S])
            then(dve.tensor_tensor(val[:], query(0), pk[:, 1], ALU.mult))
            then(dve.tensor_tensor(part[:], pk[:, 0], pz[:, 1], ALU.mult))
            then(dve.tensor_tensor(val[:], val[:], part[:], ALU.add))
            then(dve.tensor_tensor(part[:], query(1), pz[:, 0], ALU.mult))
            then(dve.tensor_tensor(val[:], val[:], part[:], ALU.add))
            then(dve.tensor_scalar(val[:], val[:], thr[:, 0:1], None, ALU.subtract))
            dve.wait_ge(sines, 2)
            then(dve.tensor_scalar(val[:], val[:], 1e-6, None, ALU.add))
            dve.wait_ge(sines, 3)
            then(dve.tensor_scalar(val[:], val[:], 0.3, None, ALU.mult))
            assert count[0] == STEPS

        @block.scalar
        def _(act):
            act.wait_ge(step, 19)
            for a in angles:
                last = act.activation(a[:], a[:], ACT.Sin)
            last.then_inc(sines, 1)
            act.wait_ge(step, 25)
            act.activation(val[:], val[:], ACT.Sigmoid, scale=inv[:, 0:1]).then_inc(sines, 1)
            act.wait_ge(step, 26)
            act.activation(val[:], val[:], ACT.Ln).then_inc(sines, 1)


def narrow_attention(nc, io, name, first):
    with phase(nc, name) as (sb, ps, sem, sems, pair, open_block):
        HP = H // 2
        W = HD + 1
        ident, bias = sb("ident", [P, P]), sb("bias", [P, HK])
        copy_mask = sb("copy_mask", [P, 2])
        qin = sb("qin", [P, 2, TILE])
        vin = sb("vin", [P, 2, 2, D])
        vblock = sb("vblock", [P, 2, 2, HP, 2 * W])
        scored, e, pt = (sb(n, [P, 2, HK]) for n in ("scored", "e", "pt"))
        top, inv = sb("top", [P, 2, H]), sb("inv", [P, 2, H])
        out = sb("out", [P, 2, D])
        if first:
            kin = sb("kin", [P, 2, TILE])
            kblock = sb("kblock", [P, 2, H, TILE])
            head_mask = sb("head_mask", [P, H])
        else:
            kblock = sb("kblock", [P, 2, 2, TILE])
            lat_w = sb("lat_w", [P, HK])
            qT = sb("qT", [P, 2, HP, TILE])
            q_ps = ps("q_ps", [P, HP, TILE])
        s_ps, pt_ps = ps("s_ps", [P, HK]), ps("pt_ps", [P, HK])
        o_ps = ps("o_ps", [P, ST])
        q_in, k_in, v_in, out_stored = (pair(x) for x in ("q_in", "k_in", "v_in", "out_stored"))
        w_in, cleared, kblock_ready, vblock_ready, q_done, q_ready, s_done, biased, topped, shifted, e_ready, \
            pt_done, pt_ready, o_done, inverted, out_ready, apart_pool = sems(
                "w_in", "cleared", "kblock_ready", "vblock_ready", "q_done", "q_ready", "s_done", "biased", "topped",
                "shifted", "e_ready", "pt_done", "pt_ready", "o_done", "inverted", "out_ready", "apart_pool")
        block = open_block()
        Q_LOADS = 16 * (1 if first else 3)
        WEIGHTS = 16 * 4

        def values(t):
            return o_ps[:, 0:HP * 2 * W].rearrange("p (h w) -> p h w", w=W)

        @block.sync
        def _(sp):
            sp.dma_start(ident[:, :], io["ident"][:, :]).then_inc(w_in, 16)
            sp.dma_start(copy_mask[:, :], io["copy_mask"][:, :]).then_inc(w_in, 16)
            sp.dma_start(bias[:, :], (io["bias0"] if first else io["causal"])[:, :]).then_inc(w_in, 16)
            if first:
                sp.dma_start(head_mask[:, :], io["head_mask"][:, :]).then_inc(w_in, 16)
            else:
                sp.dma_start(lat_w[:, :], io["lat_w"][:, :]).then_inc(w_in, 16)
            sp.wait_ge(cleared, 1)

            def load_queries(i, u, n):
                at = bass.ds(i * TILE, TILE)
                wait(sp, s_done, i - 1)
                sp.dma_start(qin[:, u, :], (io["QT"] if first else io["xnT"])[:, at]).then_inc(q_in[u], 16)
                if not first:
                    for c in range(2):
                        sp.dma_start(kblock[c * S:(c + 1) * S, u, c, :], io["latT"][:, at]).then_inc(q_in[u], 16)

            def load_keys(i, u, n):
                wait(sp, kblock_ready, i - 1)
                sp.dma_start(kin[:, u, :], io["KT"][:, bass.ds(i * TILE, TILE)]).then_inc(k_in[u], 16)

            def load_values(i, u, n):
                wait(sp, vblock_ready, i - 1)
                for c in range(2):
                    sp.dma_start(vin[c * S:(c + 1) * S, u], io["V"][bass.ds(i * TILE, TILE), :]
                                 .rearrange("(b k) d -> k b d", b=2)).then_inc(v_in[u], 16)

            def store(i, u, n):
                sp.wait_ge(out_ready, i + 1)
                sp.dma_start(io["AO"][bass.ds(i * TILE, TILE), :], out[:, u, :]).then_inc(out_stored[u], 16)

            if first:
                over_steps(sp, NT, (0, load_keys), (1, load_queries), (2, load_values), (4, store))
            else:
                over_steps(sp, NT, (0, load_queries), (1, load_values), (4, store))
            for u in range(2):
                sp.wait_ge(out_stored[u], 16 * (NT // 2))

        @block.gpsimd
        def _(pool):
            if not first:
                pool.memset(kblock[:, :, :, :], 0.0)
            pool.memset(vblock[:, :, :, :, :], 0.0).then_inc(cleared, 1)
            pool.wait_ge(cleared, 1)
            for c in range(2):
                last = pool.memset(vblock[c * S:(c + 1) * S, :, :, :, c * W + HD:c * W + W], 1.0)
            last.then_inc(cleared, 1)
            pool.wait_ge(w_in, WEIGHTS)

            pool.wait_ge(cleared, 2)

            def spread_keys(i, u, n):
                pool.wait_ge(k_in[u], n * 16 + 16)
                wait(pool, s_done, i - 1)
                apart(pool, apart_pool)
                for h in range(H):
                    last = pool.tensor_scalar(kblock[:, u, h, :], kin[:, u, :], head_mask[:, h:h + 1], 0.0,
                                              ALU.mult, ALU.add)
                last.then_inc(kblock_ready, 1)

            def spread_values(i, u, n):
                pool.wait_ge(v_in[u], n * 32 + 32)
                wait(pool, o_done, i - 1)
                apart(pool, apart_pool)
                for b in range(2):
                    for c in range(2):
                        heads = vin[:, u, b, :].rearrange("p (g c d) -> p g c d", c=2, d=HD)[:, :, c, :]
                        last = pool.tensor_scalar(vblock[:, u, b, :, c * W:c * W + HD], heads, copy_mask[:, c:c + 1], 0.0,
                                                  ALU.mult, ALU.add)
                last.then_inc(vblock_ready, 1)

            if first:
                over_steps(pool, NT, (0, spread_keys), (1, spread_values))
            else:
                over_steps(pool, NT, (0, spread_values))

        @block.tensor
        def _(pe):
            def queries(i, u, n):
                pe.wait_ge(q_in[u], n * Q_LOADS + Q_LOADS)
                wait(pe, q_ready, i)
                for g in range(HP):
                    last = pe.matmul(q_ps[:, g, :], lat_w[:, g * P:(g + 1) * P], qin[:, u, :], start=True, stop=True)
                last.then_inc(q_done, 1)

            def scores(i, u, n):
                if first:
                    pe.wait_ge(q_in[u], n * Q_LOADS + Q_LOADS)
                    pe.wait_ge(kblock_ready, i + 1)
                else:
                    pe.wait_ge(q_ready, i + 1)
                wait(pe, biased, i)
                if first:
                    for half in range(2):
                        for b in range(2):
                            last = pe.matmul(
                                s_ps[b * S:(b + 1) * S, half * ST:(half + 1) * ST],
                                qin[:, u, b * S:(b + 1) * S],
                                kblock[:, u, half * HP:(half + 1) * HP, b * S:(b + 1) * S],
                                start=True, stop=True, tile_position=(0, b * S))
                else:
                    for g in range(HP):
                        for b in range(2):
                            last = pe.matmul(
                                s_ps[b * S:(b + 1) * S, g * P:(g + 1) * P],
                                qT[:, u, g, b * S:(b + 1) * S],
                                kblock[:, u, :, b * S:(b + 1) * S],
                                start=True, stop=True, tile_position=(0, b * S))
                last.then_inc(s_done, 1)

            def weigh(i, u, n):
                pe.wait_ge(pt_ready, i + 1)
                pe.wait_ge(vblock_ready, i + 1)
                wait(pe, out_ready, i)
                for g in range(HP):
                    for b in range(2):
                        last = pe.matmul(
                            o_ps[b * S:(b + 1) * S, g * 2 * W:(g + 1) * 2 * W],
                            pt[:, u, g * P + b * S:g * P + (b + 1) * S],
                            vblock[:, u, b, g, :],
                            start=True, stop=True, tile_position=(0, b * S))
                last.then_inc(o_done, 1)

            def turn(i, u, n):
                pe.wait_ge(e_ready, i + 1)
                wait(pe, pt_ready, i)
                for g in range(HP):
                    last = pe.transpose(pt_ps[:, g * P:(g + 1) * P], e[:, u, g * P:(g + 1) * P], ident[:, :])
                last.then_inc(pt_done, 1)

            pe.wait_ge(w_in, WEIGHTS)
            pe.wait_ge(cleared, 2)
            if first:
                over_steps(pe, NT, (0, scores), (2, weigh), (1, turn))
            else:
                over_steps(pe, NT, (0, queries), (1, scores), (3, weigh), (2, turn))

        @block.vector
        def _(dve):
            def soften(i, u, n):
                dve.wait_ge(s_done, i + 1)
                wait(dve, e_ready, i - 1)
                dve.tensor_tensor(scored[:, u, :], s_ps[:, :], bias[:, :], ALU.add).then_inc(biased, 1)
                dve.wait_ge(biased, i + 1)
                by_head = scored[:, u, :].rearrange("p (h k) -> p h k", k=S)
                dve.tensor_reduce(top[:, u, :], by_head, axis=AX.X, op=ALU.max).then_inc(topped, 1)
                dve.wait_ge(topped, i + 1)
                dve.tensor_tensor(by_head, by_head, top[:, u, :, None].broadcast_to([P, H, S]),
                                  ALU.subtract).then_inc(shifted, 1)

            def normalise(i, u, n):
                dve.wait_ge(o_done, i + 1)
                wait(dve, out_stored[u], n * 16)
                dve.reciprocal(inv[:, u, :], values(o_ps)[:, :, HD]).then_inc(inverted, 1)
                dve.wait_ge(inverted, i + 1)
                dve.tensor_tensor(out[:, u, :].rearrange("p (h d) -> p h d", d=HD), values(o_ps)[:, :, 0:HD],
                                  inv[:, u, :, None].broadcast_to([P, H, HD]), ALU.mult).then_inc(out_ready, 1)

            dve.wait_ge(w_in, WEIGHTS)
            over_steps(dve, NT, (0, soften), (2, normalise))

        @block.scalar
        def _(act):
            def evacuate_queries(i, u, n):
                act.wait_ge(q_done, i + 1)
                wait(act, s_done, i - 1)
                act.activation(qT[:, u], q_ps[:, :, :], ACT.Copy).then_inc(q_ready, 1)

            def exponentials(i, u, n):
                act.wait_ge(shifted, i + 1)
                wait(act, pt_done, i - 1)
                act.activation(e[:, u, :], scored[:, u, :], ACT.Exp).then_inc(e_ready, 1)

            def evacuate_turned(i, u, n):
                act.wait_ge(pt_done, i + 1)
                wait(act, o_done, i - 1)
                act.activation(pt[:, u, :], pt_ps[:, :], ACT.Copy).then_inc(pt_ready, 1)

            if first:
                over_steps(act, NT, (2, evacuate_turned), (1, exponentials))
            else:
                over_steps(act, NT, (3, evacuate_turned), (0, evacuate_queries), (2, exponentials))


def latent_weights(nc, io):
    with phase(nc, "latents") as (sb, ps, sem, sems, pair, open_block):
        R = io["latent"]
        scale = R ** -0.5
        basis, core, core_t = sb("basis", [R, D]), sb("core", [R, R]), sb("core_t", [R, R])
        heads = sb("heads", [R, H, R])
        mean = sb("mean", [R, R])
        w = sb("w", [P, H * R])
        w_ps = ps("w_ps", [P, H * R])
        loaded, step, product_done, w_ready, stored = sems("loaded", "step", "product_done", "w_ready", "stored")
        block = open_block()
        STEPS = 6

        @block.sync
        def _(sp):
            sp.dma_start(basis[:, :], io["L1_attn_basis_w"][:, :]).then_inc(loaded, 16)
            sp.dma_start(core[:, :], io["L1_attn_core"][:, :]).then_inc(loaded, 16)
            sp.dma_start(core_t[:, :], io["core_T"][:, :]).then_inc(loaded, 16)
            sp.dma_start(heads[:, :, :], io["L1_attn_head_residual"].rearrange("h r s -> r h s")).then_inc(loaded, 16)
            sp.wait_ge(w_ready, 1)
            sp.dma_start(io["lat_w"][:, :], w[:, :]).then_inc(stored, 16)
            sp.wait_ge(stored, 16)

        @block.vector
        def _(dve):
            count = [0]

            def then(instruction):
                count[0] += 1
                instruction.then_inc(step, 1)
                dve.wait_ge(step, count[0])

            dve.wait_ge(loaded, 64)
            then(dve.tensor_reduce(mean[:, :], heads[:, :, :].rearrange("r h s -> r s h"), axis=AX.X, op=ALU.add))
            then(dve.tensor_tensor(core[:, :], core[:, :], core_t[:, :], ALU.add))
            then(dve.tensor_scalar(core[:, :], core[:, :], 0.5, None, ALU.mult))
            then(dve.tensor_tensor(core[:, :], core[:, :], mean[:, :], ALU.subtract))
            then(dve.scalar_tensor_tensor(out=heads[:, :, :], in0=core[:, None, :].broadcast_to([R, H, R]),
                                          scalar=1.0 / H, in1=heads[:, :, :], op0=ALU.mult, op1=ALU.add))
            then(dve.tensor_scalar(heads[:, :, :], heads[:, :, :], scale, None, ALU.mult))
            assert count[0] == STEPS
            dve.wait_ge(product_done, 1)
            dve.tensor_copy(w[:, :], w_ps[:, :]).then_inc(w_ready, 1)

        @block.tensor
        def _(pe):
            pe.wait_ge(step, STEPS)
            for half in range(2):
                last = pe.matmul(w_ps[:, half * ST:(half + 1) * ST], basis[:, :], heads[:, half * 8:half * 8 + 8, :],
                                 start=True, stop=True)
            last.then_inc(product_done, 1)


def close_attention(nc, io, layer):
    with phase(nc, f"close{layer}") as (sb, ps, sem, sems, pair, open_block):
        ident, w = sb("ident", [P, P]), sb("w", [P, D])
        bv, bv_wide, brow, bo = sb("bv", [P, 1]), sb("bv_wide", [P, P]), sb("brow", [P, D]), sb("bo", [P, D])
        ao, rows, x1, out = (sb(n, [P, 2, JT, D]) for n in ("ao", "rows", "x1", "out"))
        aoT = sb("aoT", [P, 2, ST])
        t_ps, y_ps, r_ps = (ps(n, [P, 2, ST]) for n in ("t_ps", "y_ps", "r_ps"))
        b_ps = ps("b_ps", [P, D])
        ctxT, square, r = (sb(n, [P, 2, ST]) for n in ("ctxT", "square", "r"))
        decay = sb("decay", [P, ST])
        xn = sb("xn", [P, 2, JT, D])
        set_up, measure, invert, apply = layer_norm(sb, sems, "ln")
        tile_in, stored = pair("tile_in"), pair("stored")
        w_in, wide_ready, brow_done, brow_ready, t_done, t_ready, y_done, x1_ready, squared, r_ready, r_done, xn_ready, \
            multiplied, out_ready, biased, apart_sp = sems(
                "w_in", "wide_ready", "brow_done", "brow_ready", "t_done", "t_ready", "y_done", "x1_ready", "squared",
                "r_ready", "r_done", "xn_ready", "multiplied", "out_ready", "biased", "apart_sp")
        block = open_block()
        if layer == 0:
            source, target = io["x"], io["x2"]
            weights = ((w, io["L0_attn_Wo"]), (bv, io["L0_attn_bv"]), (bo, io["L0_attn_bo"].partition_broadcast(P)),
                       (ident, io["ident"]), (decay, io["decay"]))
        else:
            source, target = io["x3"], io["x4"]
            weights = ((w, io["L1_attn_o_wT"]), (bv, io["L1_attn_v_b"]), (bo, io["L1_attn_o_b"].partition_broadcast(P)),
                       (ident, io["ident"]))
        WEIGHTS = 16 * len(weights)
        LOADS = 48 if layer == 0 else 32
        final, final_ready = (out, out_ready) if layer == 0 else (x1, x1_ready)

        @block.sync
        def _(sp):
            for dst, src in weights:
                sp.dma_start(dst[:, :], src if dst is bo else src[:, :]).then_inc(w_in, 16)

            def load(i, u, n):
                wait(sp, t_done, i - 1)
                sp.dma_start(ao[:, u], rows_of(io["AO"], i, ST)).then_inc(tile_in[u], 16)
                wait(sp, x1_ready, i - 1)
                sp.dma_start(rows[:, u], rows_of(source, i, ST)).then_inc(tile_in[u], 16)
                if layer == 0:
                    wait(sp, squared, i - 1)
                    apart(sp, apart_sp)
                    sp.dma_start(ctxT[:, u, :], io["ctxT"][:, bass.ds(i * ST, ST)]).then_inc(tile_in[u], 16)

            def store(i, u, n):
                sp.wait_ge(final_ready, i + 1)
                sp.dma_start(rows_of(target, i, ST), final[:, u]).then_inc(stored[u], 16)

            over_steps(sp, NS, (0, load), (2, store))
            for u in range(2):
                sp.wait_ge(stored[u], 16 * (NS // 2))

        @block.gpsimd
        def _(pool):
            if layer == 0:
                set_up(pool)

            def square_context(i, u, n):
                pool.wait_ge(tile_in[u], n * LOADS + LOADS)
                wait(pool, r_ready, i - 1)
                pool.tensor_tensor(square[:, u, :], ctxT[:, u, :], ctxT[:, u, :], ALU.mult).then_inc(squared, 1)

            def add_bias(i, u, n):
                pool.wait_ge(tile_in[u], n * LOADS + LOADS)
                pool.wait_ge(brow_ready, 1)
                pool.tensor_tensor(rows[:, u], rows[:, u], brow[:, None, :].broadcast_to([P, JT, D]),
                                   ALU.add).then_inc(biased, 1)

            if layer == 0:
                over_steps(pool, NS, (0, square_context), (0, add_bias), (1, lambda i, u, n: invert(pool, i)))
            else:
                over_steps(pool, NS, (0, add_bias))

        @block.vector
        def _(dve):
            dve.wait_ge(w_in, WEIGHTS)
            dve.tensor_copy(bv_wide[:, :], bv[:, 0:1].broadcast_to([P, P])).then_inc(wide_ready, 1)
            dve.wait_ge(brow_done, 1)
            dve.tensor_tensor(brow[:, :], b_ps[:, :], bo[:, :], ALU.add).then_inc(brow_ready, 1)

            def running(i, u, n):
                dve.wait_ge(squared, i + 1)
                wait(dve, r_done, i - 1)
                dve.tensor_tensor_scan(r[:, u, :], decay[:, :], square[:, u, :], 0.0, ALU.mult, ALU.add).then_inc(r_ready, 1)

            def residual(i, u, n):
                dve.wait_ge(y_done, i + 1)
                dve.wait_ge(biased, i + 1)
                if layer == 1:
                    wait(dve, stored[u], n * 16)
                dve.tensor_tensor(x1[:, u], y_ps[:, u, :].rearrange("p (j d) -> p j d", d=D), rows[:, u],
                                  ALU.add).then_inc(x1_ready, 1)

            def cross(i, u, n):
                dve.wait_ge(x1_ready, i + 1)
                measure(dve, x1[:, u], i)
                apply(dve, xn[:, u], x1[:, u], i, xn_ready)
                dve.wait_ge(xn_ready, i + 1)
                dve.wait_ge(r_done, i + 1)
                wait(dve, stored[u], n * 16)
                dve.tensor_tensor(xn[:, u], r_ps[:, u, :].rearrange("p (j d) -> p j d", d=D), xn[:, u],
                                  ALU.mult).then_inc(multiplied, 1)
                dve.wait_ge(multiplied, i + 1)
                dve.tensor_tensor(out[:, u], x1[:, u], xn[:, u], ALU.add).then_inc(out_ready, 1)

            if layer == 0:
                over_steps(dve, NS, (0, running), (1, residual), (1, cross))
            else:
                over_steps(dve, NS, (0, residual))

        @block.tensor
        def _(pe):
            pe.wait_ge(wide_ready, 1)
            pe.matmul(b_ps[:, :], bv_wide[:, :], w[:, :], start=True, stop=True).then_inc(brow_done, 1)

            def turn(i, u, n):
                pe.wait_ge(tile_in[u], n * LOADS + LOADS)
                wait(pe, t_ready, i - 1)
                for j in range(JT):
                    last = pe.transpose(t_ps[:, u, j * P:(j + 1) * P], ao[:, u, j, :], ident[:, :])
                last.then_inc(t_done, 1)
                if layer == 0:
                    pe.wait_ge(r_ready, i + 1)
                    wait(pe, multiplied, i - 1)
                    for j in range(JT):
                        last = pe.transpose(r_ps[:, u, j * P:(j + 1) * P], r[:, u, j * P:(j + 1) * P], ident[:, :])
                    last.then_inc(r_done, 1)

            def product(i, u, n):
                pe.wait_ge(t_ready, i + 1)
                wait(pe, x1_ready, i - 1)
                for j in range(JT):
                    last = pe.matmul(y_ps[:, u, j * P:(j + 1) * P], aoT[:, u, j * P:(j + 1) * P], w[:, :],
                                     start=True, stop=True)
                last.then_inc(y_done, 1)

            over_steps(pe, NS, (0, turn), (1, product))

        @block.scalar
        def _(act):
            def evacuate(i, u, n):
                act.wait_ge(t_done, i + 1)
                wait(act, y_done, i - 1)
                act.activation(aoT[:, u, :], t_ps[:, u, :], ACT.Copy).then_inc(t_ready, 1)

            over_steps(act, NS, (0, evacuate))


def chain_of(eng, sem, steps, alone):
    at = [0, 0]

    def start(i):
        at[:] = [0, i * steps]

    def then(instruction, before=False):
        at[0] += 1
        assert at[0] <= steps
        instruction.then_inc(sem, 1)
        eng.wait_ge(sem, at[1] + at[0])
        if before:
            apart(eng, alone)

    return start, then


def moe(nc, io, layer):
    with phase(nc, f"moe{layer}") as (sb, ps, sem, sems, pair, open_block):
        E = 8
        EX = E + 1 if layer == 0 else E
        Y = EX + 1 if layer == 0 else E
        C = 1 if layer == 0 else 2
        LIMIT, ALPHA = 7.0, 1.702
        ident = sb("ident", [P, P])
        gate = sb("gate", [P, E])
        up = sb("up", [P, EX, 4, P])
        down = sb("down", [P, EX, C, D])
        not_first = sb("not_first", [P, JT * E])
        if layer == 0:
            gate_b, up_b, down_b = sb("gate_b", [P, E]), sb("up_b", [P, EX, 4]), sb("down_b", [P, D])
            weights = ((ident[:, :], io["ident"][:, :]), (gate[:, :], io["gate0_T"][:, :]), (up[:, :, :, :], io["up0"][:, :, :, :]),
                       (down[:, :, 0, :], io["down0"][:, :, :]), (not_first[:, :], io["not_first"][:, :]),
                       (gate_b[:, :], io["gate0_b"].partition_broadcast(P)), (up_b[:, :, :], io["up0_b"][:, :, :]),
                       (down_b[0:EX, :], io["down0_b"][:, :]))
            source, target = io["x2"], io["x3"]
        else:
            weights = ((ident[:, :], io["ident"][:, :]), (gate[:, :], io["gate1_T"][:, :]), (up[:, :, :, :], io["up1"][:, :, :, :]),
                       (down[:, :, :, :], io["down1"][:, :, :, :]), (not_first[:, :], io["not_first"][:, :]))
            source, target = io["x6"], io["out"]
        WEIGHTS = 16 * len(weights)
        rows, xn, acc = (sb(n, [P, 2, JT, D]) for n in ("rows", "xn", "acc"))
        xnT = sb("xnT", [P, 2, ST])
        mx, total, share, above_n = (sb(n, [P, JT]) for n in ("mx", "total", "share", "above_n"))
        shifted, ex, score, biased, best, above, level, rank, picked = (
            sb(n, [P, JT, E]) for n in ("shifted", "ex", "score", "biased", "best", "above", "level", "rank", "picked"))
        cw = sb("cw", [P, 2, JT, P])
        cwT = sb("cwT", [P, ST])
        first = sb("first", [P, 2, 2, ST])
        prod = sb("prod", [P, 2, 2, ST])
        tanh, gated = sb("tanh", [P, 2, ST]), sb("gated", [P, 2, ST])
        hidden = sb("hidden", [P, 2, C, ST])
        t_ps, c_ps = ps("t_ps", [P, ST]), ps("c_ps", [P, ST])
        h_ps, y_ps = ps("h_ps", [P, 4, ST]), ps("y_ps", [P, 2, ST])
        set_up, measure, invert, apply = layer_norm(sb, sems, "ln")
        x_in, acc_in, stored = pair("x_in"), pair("acc_in"), pair("stored")
        w_in, cw_set, xn_ready, t_done, t_ready, logits_done, route, exped, h_done, first_ready, product_ready, \
            gate_clamped, tanh_ready, linear_clamped, linear_ready, gated_ready, hidden_ready, y_done, added, c_done, \
            c_ready, cw_ready, apart_sp, apart_pool, apart_dve = sems(
                "w_in", "cw_set", "xn_ready", "t_done", "t_ready", "logits_done", "route", "exped", "h_done",
                "first_ready", "product_ready", "gate_clamped", "tanh_ready", "linear_clamped", "linear_ready",
                "gated_ready", "hidden_ready", "y_done", "added", "c_done", "c_ready", "cw_ready", "apart_sp",
                "apart_pool", "apart_dve")
        block = open_block()
        ROUTE = 14 if layer == 0 else 13
        EXP_INPUT = 2 if layer == 0 else 10
        LOGITS_READ = 2 if layer == 0 else 1
        wide = lambda t: t[:, :, None].broadcast_to([P, JT, E])

        def across(e):
            made = [(1, EX - 1)] if e == 0 else [(0, e - 1)]
            out = [(1, EX - 2)] if e == 0 else [(1, y) for y in range(EX - 1, Y)] if e == 1 else [(0, e - 2)]
            return made, out

        @block.sync
        def _(sp):
            for dst, src in weights:
                sp.dma_start(dst, src).then_inc(w_in, 16)

            def load(i, u, n):
                wait(sp, xn_ready, i - 1)
                sp.dma_start(rows[:, u], rows_of(source, i, ST)).then_inc(x_in[u], 16)

            def load_residual(i, u, n):
                wait(sp, stored[u], n * 16)
                sp.dma_start(acc[:, u], rows_of(source, i, ST)).then_inc(acc_in[u], 16)

            def store(i, u, n):
                sp.wait_ge(added, i * Y + Y)
                sp.dma_start(rows_of(target, i, ST), acc[:, u]).then_inc(stored[u], 16)

            over_steps(sp, NS, (0, load), (3, store), (1, load_residual))
            for u in range(2):
                sp.wait_ge(stored[u], 16 * (NS // 2))

        @block.gpsimd
        def _(pool):
            pool.memset(cw[:, :, :, :], 0.0).then_inc(cw_set, 1)
            pool.wait_ge(cw_set, 1)
            pool.memset(cw[:, :, :, E:E + 1], 1.0).then_inc(cw_set, 1)
            set_up(pool)

            def clamp(i, u, n):
                for e in range(EX):
                    m, pm = i * EX + e, (u * EX + e) % 2
                    linear = prod[:, pm, 1, :]
                    pool.wait_ge(product_ready, 2 * m + 2)
                    apart(pool, apart_pool)
                    pool.tensor_scalar(linear, linear, LIMIT, -LIMIT, ALU.min, ALU.max).then_inc(linear_clamped, 1)
                    pool.wait_ge(linear_clamped, m + 1)
                    apart(pool, apart_pool)
                    pool.tensor_scalar(linear, linear, 0.5, 0.5, ALU.mult, ALU.add).then_inc(linear_ready, 1)

            if layer == 0:
                over_steps(pool, NS, (0, lambda i, u, n: invert(pool, i)), (2, clamp))
            else:
                over_steps(pool, NS, (0, lambda i, u, n: invert(pool, i)))

        @block.tensor
        def _(pe):
            def front(i, u, n):
                pe.wait_ge(xn_ready, i + 1)
                wait(pe, route, (i - 1) * ROUTE + LOGITS_READ)
                for j in range(JT):
                    last = pe.transpose(t_ps[:, j * P:(j + 1) * P], xn[:, u, j, :], ident[:, :])
                last.then_inc(t_done, 1)
                pe.wait_ge(t_ready, i + 1)
                for j in range(JT):
                    last = pe.matmul(t_ps[:, j * E:(j + 1) * E], xnT[:, u, j * P:(j + 1) * P], gate[:, :],
                                     start=True, stop=True)
                last.then_inc(logits_done, 1)

            def outputs(i, u, e):
                m, pm = i * EX + e, (u * EX + e) % 2
                wait(pe, added, i * Y + e - 1)
                if e == EX:
                    pe.wait_ge(c_ready, i + 1)
                else:
                    pe.wait_ge(hidden_ready, m + 1)
                for j in range(JT):
                    at = slice(j * P, (j + 1) * P)
                    if e == EX:
                        last = pe.matmul(y_ps[:, e % 2, at], cwT[0:EX, at], down_b[0:EX, :], start=True, stop=True)
                    else:
                        for c in range(C):
                            last = pe.matmul(y_ps[:, e % 2, at], hidden[:, pm, c, at], down[:, e, c, :],
                                             start=(c == 0), stop=(c == C - 1))
                last.then_inc(y_done, 1)

            def body(i, u, n):
                for e in range(EX):
                    m = i * EX + e
                    for bank in range(4):
                        if bank % 2 == 0:
                            wait(pe, first_ready, 2 * m + bank // 2 - 1)
                            wait(pe, product_ready, 2 * m + bank // 2 - 1)
                        pe.matmul(h_ps[:, bank, :], up[:, e, bank, :], xnT[:, u, :], start=True, stop=True)\
                            .then_inc(h_done, 1)
                    for back, y in across(e)[1]:
                        if not (back and isinstance(i, int) and i == 0):
                            outputs(i - back, (u - back) % 2, y)
                    if e == 4 and layer == 0:
                        pe.wait_ge(cw_ready, i + 1)
                        wait(pe, c_ready, i)
                        for j in range(JT):
                            last = pe.transpose(c_ps[:, j * P:(j + 1) * P], cw[:, u, j, :], ident[:, :])
                        last.then_inc(c_done, 1)

            pe.wait_ge(w_in, WEIGHTS)
            over_steps(pe, NS, (1, front), (2, body))
            for y in range(EX - 2, Y):
                outputs(NS - 1, (NS - 1) % 2, y)

        @block.scalar
        def _(act):
            def front(i, u, n):
                act.wait_ge(t_done, i + 1)
                wait(act, h_done, (i - 1) * EX * 4)
                act.activation(xnT[:, u, :], t_ps[:, :], ACT.Copy).then_inc(t_ready, 1)

            def exponentials(i, u, n):
                act.wait_ge(route, i * ROUTE + EXP_INPUT)
                act.activation(ex[:, :, :], shifted[:, :, :], ACT.Exp).then_inc(exped, 1)

            def body(i, u, n):
                for e in range(EX):
                    m, pm = i * EX + e, (u * EX + e) % 2
                    for half in range(2):
                        act.wait_ge(h_done, 4 * m + 2 * half + 1)
                        wait(act, product_ready, 2 * m + half - 3)
                        if layer == 0:
                            act.activation(first[:, pm, half, :], h_ps[:, 2 * half, :], ACT.Identity,
                                           bias=up_b[:, e, 2 * half:2 * half + 1]).then_inc(first_ready, 1)
                        else:
                            act.activation(first[:, pm, half, :], h_ps[:, 2 * half, :], ACT.Silu).then_inc(first_ready, 1)
                    if layer == 0:
                        act.wait_ge(gate_clamped, m + 1)
                        wait(act, gated_ready, m - 1)
                        act.activation(tanh[:, pm, :], prod[:, pm, 0, :], ACT.Tanh, scale=ALPHA / 2).then_inc(tanh_ready, 1)
                    if e == 4 and layer == 0:
                        act.wait_ge(c_done, i + 1)
                        wait(act, y_done, i * Y)
                        act.activation(cwT[:, :], c_ps[:, :], ACT.Copy).then_inc(c_ready, 1)

            act.wait_ge(w_in, WEIGHTS)
            over_steps(act, NS, (1, front), (2, body), (1, exponentials))

        @block.vector
        def _(dve):
            start_chain, then = chain_of(dve, route, ROUTE, apart_dve)

            def normalise(i, u, n):
                dve.wait_ge(x_in[u], n * 16 + 16)
                measure(dve, rows[:, u], i)
                wait(dve, t_done, i - 1)
                apply(dve, xn[:, u], rows[:, u], i, xn_ready)

            def route_weights(i, u, n):
                start_chain(i)
                logits = t_ps[:, 0:JT * E].rearrange("p (j e) -> p j e", e=E)
                dve.wait_ge(logits_done, i + 1)
                if layer == 0:
                    then(dve.tensor_reduce(mx[:, :], logits, axis=AX.X, op=ALU.max))
                    then(dve.tensor_tensor(shifted[:, :, :], logits, wide(mx), ALU.subtract))
                    dve.wait_ge(exped, i + 1)
                    then(dve.tensor_reduce(total[:, :], ex[:, :, :], axis=AX.X, op=ALU.add))
                    then(dve.reciprocal(share[:, :], total[:, :]))
                    then(dve.tensor_tensor(score[:, :, :], ex[:, :, :], wide(share), ALU.mult))
                    then(dve.tensor_tensor(biased[:, :, :], score[:, :, :], gate_b[:, None, :].broadcast_to([P, JT, E]),
                                           ALU.add), before=True)
                else:
                    then(dve.tensor_copy(biased[:, :, :], logits), before=True)
                for j in range(JT):
                    last = dve.max(best[:, j, :], biased[:, j, :])
                then(last)
                second = best[:, :, 1:2].broadcast_to([P, JT, E])
                then(dve.tensor_tensor(above[:, :, :], biased[:, :, :], second, ALU.is_gt))
                then(dve.tensor_tensor(level[:, :, :], biased[:, :, :], second, ALU.is_equal))
                then(dve.tensor_reduce(above_n[:, :], above[:, :, :], axis=AX.X, op=ALU.add))
                then(dve.tensor_tensor_scan(rank[:, :, :].rearrange("p j e -> p (j e)"), not_first[:, :],
                                            level[:, :, :].rearrange("p j e -> p (j e)"), 0.0, ALU.mult, ALU.add))
                then(dve.tensor_tensor(rank[:, :, :], rank[:, :, :], wide(above_n), ALU.add))
                then(dve.scalar_tensor_tensor(out=level[:, :, :], in0=rank[:, :, :], scalar=2.0, in1=level[:, :, :],
                                              op0=ALU.is_le, op1=ALU.mult))
                then(dve.tensor_tensor(picked[:, :, :], above[:, :, :], level[:, :, :], ALU.add))
                dve.wait_ge(cw_set, 2)
                if layer == 0:
                    dve.tensor_tensor(cw[:, u, :, 0:E], picked[:, :, :], score[:, :, :], ALU.mult).then_inc(cw_ready, 1)
                else:
                    then(dve.tensor_tensor(shifted[:, :, :], biased[:, :, :], best[:, :, 0:1].broadcast_to([P, JT, E]),
                                           ALU.subtract))
                    dve.wait_ge(exped, i + 1)
                    then(dve.tensor_tensor(ex[:, :, :], ex[:, :, :], picked[:, :, :], ALU.mult))
                    then(dve.tensor_reduce(total[:, :], ex[:, :, :], axis=AX.X, op=ALU.add))
                    then(dve.reciprocal(share[:, :], total[:, :]))
                    dve.tensor_tensor(cw[:, u, :, 0:E], ex[:, :, :], wide(share), ALU.mult).then_inc(cw_ready, 1)

            def products(i, u, e):
                m, pm = i * EX + e, (u * EX + e) % 2
                for half in range(2):
                    dve.wait_ge(first_ready, 2 * m + half + 1)
                    dve.wait_ge(h_done, 4 * m + 2 * half + 2)
                    if layer == 0:
                        dve.scalar_tensor_tensor(
                            out=prod[:, pm, half, :], in0=h_ps[:, 2 * half + 1, :], scalar=up_b[:, e, 2 * half + 1:2 * half + 2],
                            in1=first[:, pm, half, :], op0=ALU.add, op1=ALU.mult).then_inc(product_ready, 1)
                        if half == 0:
                            dve.wait_ge(product_ready, 2 * m + 1)
                            dve.tensor_scalar(prod[:, pm, 0, :], prod[:, pm, 0, :], LIMIT, None, ALU.min)\
                                .then_inc(gate_clamped, 1)
                    else:
                        wait(dve, y_done, m - 1)
                        last = dve.tensor_tensor(hidden[:, pm, half, :], h_ps[:, 2 * half + 1, :], first[:, pm, half, :], ALU.mult)
                        last.then_inc(product_ready, 1)
                if layer == 1:
                    dve.wait_ge(product_ready, 2 * m + 2)
                    dve.sem_inc(hidden_ready, 1)

            def hiddens(i, u, e):
                m, pm = i * EX + e, (u * EX + e) % 2
                dve.wait_ge(tanh_ready, m + 1)
                dve.scalar_tensor_tensor(out=gated[:, pm, :], in0=tanh[:, pm, :], scalar=1.0, in1=prod[:, pm, 0, :],
                                         op0=ALU.add, op1=ALU.mult).then_inc(gated_ready, 1)
                dve.wait_ge(gated_ready, m + 1)
                dve.wait_ge(linear_ready, m + 1)
                wait(dve, y_done, i * Y + e - 1 if e >= 2 else (i - 1) * Y + EX + e - 1)
                dve.tensor_tensor(hidden[:, pm, 0, :], gated[:, pm, :], prod[:, pm, 1, :], ALU.mult).then_inc(hidden_ready, 1)

            def add(i, u, e, n=NS // 2 - 1):
                dve.wait_ge(y_done, i * Y + e + 1)
                if e == 0:
                    dve.wait_ge(acc_in[u], n * 16 + 16)
                    dve.wait_ge(cw_ready, i + 1)
                else:
                    dve.wait_ge(added, i * Y + e)
                if e == EX:
                    dve.tensor_tensor(acc[:, u], y_ps[:, e % 2, :].rearrange("p (j d) -> p j d", d=D), acc[:, u],
                                      ALU.add).then_inc(added, 1)
                    return
                for j in range(JT):
                    last = dve.scalar_tensor_tensor(
                        out=acc[:, u, j, :], in0=y_ps[:, e % 2, j * P:(j + 1) * P], scalar=cw[:, u, j, e:e + 1],
                        in1=acc[:, u, j, :], op0=ALU.mult, op1=ALU.add)
                last.then_inc(added, 1)

            def body(i, u, n):
                for e in range(EX):
                    products(i, u, e)
                    made, out = across(e)
                    start = isinstance(i, int) and i == 0
                    if layer == 0:
                        for back, x in made:
                            if not (back and start):
                                hiddens(i - back, (u - back) % 2, x)
                    for back, y in out:
                        if not (back and start):
                            add(i - back, (u - back) % 2, y, n)

            dve.wait_ge(w_in, WEIGHTS)
            over_steps(dve, NS, (0, normalise), (2, body), (1, route_weights))
            if layer == 0:
                hiddens(NS - 1, (NS - 1) % 2, EX - 1)
            for y in range(EX - 2, Y):
                add(NS - 1, (NS - 1) % 2, y)


def context_and_gated(nc, io):
    with phase(nc, "gated") as (sb, ps, sem, sems, pair, open_block):
        C, KV = 4, 64
        ident = sb("ident", [P, P])
        gain, offset, cgain, coffset = (sb(n, [P, 1]) for n in ("gain", "offset", "cgain", "coffset"))
        wkv, w1, w2 = sb("wkv", [P, 2 * KV]), sb("w1", [P, 2 * C * P]), sb("w2", [P, C, D])
        rows, ctx, xn, xn2, cn, out = (sb(n, [P, 2, JT, D]) for n in ("rows", "ctx", "xn", "xn2", "cn", "out"))
        xnT, cnT = sb("xnT", [P, 2, ST]), sb("cnT", [P, 2, ST])
        key, value = sb("key", [KV, 2, ST]), sb("value", [P, 2, JT, KV])
        silu, hidden = sb("silu", [P, 2, ST]), sb("hidden", [P, C, ST])
        t_ps, c_ps, k_ps = (ps(n, [P, ST]) for n in ("t_ps", "c_ps", "k_ps"))
        v_ps = c_ps
        h_ps = ps("h_ps", [P, 2, 2, ST])
        y_ps = ps("y_ps", [P, ST])
        norm, norm2, cnorm = (layer_norm(sb, sems, n) for n in ("ln", "ln2", "cln"))
        x_in, ctx_in, x_stored, kv_stored = (pair(n) for n in ("x_in", "ctx_in", "x_stored", "kv_stored"))
        w_in, xn_ready, xn2_ready, cn_ready, t_done, t_ready, c_done, c_ready, k_done, k_ready, v_done, v_ready, \
            h_done, silu_ready, hidden_ready, y_done, out_ready, apart_sp = sems(
                "w_in", "xn_ready", "xn2_ready", "cn_ready", "t_done", "t_ready", "c_done", "c_ready", "k_done",
                "k_ready", "v_done", "v_ready", "h_done", "silu_ready", "hidden_ready", "y_done", "out_ready", "apart_sp")
        block = open_block()
        weights = ((ident[:, :], io["ident"][:, :]), (gain[:, :], io["L1_xattn_ln_g"][:, :]), (offset[:, :], io["L1_xattn_ln_b"][:, :]),
                   (cgain[:, :], io["L1_xattn_cln_g"][:, :]), (coffset[:, :], io["L1_xattn_cln_b"][:, :]),
                   (wkv[:, :], io["xkv"][:, :]), (w1[:, :], io["xw1"][:, :]), (w2[:, :, :], io["xw2"][:, :, :]))
        WEIGHTS = 16 * len(weights)

        @block.sync
        def _(sp):
            for dst, src in weights:
                sp.dma_start(dst, src).then_inc(w_in, 16)

            def load(i, u, n):
                wait(sp, out_ready, i - 1)
                sp.dma_start(rows[:, u], rows_of(io["x4"], i, ST)).then_inc(x_in[u], 16)
                wait(sp, cn_ready, i - 1)
                sp.dma_start(ctx[:, u], rows_of(io["ctx"], i, ST)).then_inc(ctx_in[u], 16)

            def store(i, u, n):
                at = bass.ds(i * ST, ST)
                sp.wait_ge(t_ready, i + 1)
                sp.dma_start(io["xnT"][:, at], xnT[:, u, :]).then_inc(x_stored[u], 16)
                sp.wait_ge(k_ready, i + 1)
                sp.dma_start(io["kT"][:, at], key[:, u, :]).then_inc(kv_stored[u], 16)
                sp.wait_ge(v_ready, i + 1)
                sp.dma_start(rows_of(io["v"], i, ST), value[:, u]).then_inc(kv_stored[u], 16)
                sp.wait_ge(out_ready, i + 1)
                sp.dma_start(rows_of(io["x5"], i, ST), out[:, u]).then_inc(x_stored[u], 16)

            over_steps(sp, NS, (0, load), (2, store))
            for u in range(2):
                sp.wait_ge(x_stored[u], 32 * (NS // 2))
                sp.wait_ge(kv_stored[u], 32 * (NS // 2))

        @block.gpsimd
        def _(pool):
            for each in (norm, norm2, cnorm):
                each[0](pool)
            over_steps(pool, NS, *((0, lambda i, u, n, each=each: each[2](pool, i)) for each in (norm, cnorm, norm2)))

        @block.vector
        def _(dve):
            def normalise(i, u, n):
                dve.wait_ge(x_in[u], n * 16 + 16)
                norm[1](dve, rows[:, u], i)
                dve.wait_ge(ctx_in[u], n * 16 + 16)
                cnorm[1](dve, ctx[:, u], i)
                norm[3](dve, xn[:, u], rows[:, u], i, xn_ready)
                dve.wait_ge(xn_ready, i + 1)
                norm2[1](dve, xn[:, u], i)
                wait(dve, c_done, i - 1)
                cnorm[3](dve, cn[:, u], ctx[:, u], i, cn_ready)
                wait(dve, t_done, i - 1)
                norm2[3](dve, xn2[:, u], xn[:, u], i, xn2_ready)

            def keys_and_values(i, u, n):
                dve.wait_ge(k_done, i + 1)
                wait(dve, kv_stored[u], n * 32)
                dve.tensor_copy(key[:, u, :], k_ps[0:KV, :]).then_inc(k_ready, 1)
                dve.wait_ge(v_done, i + 1)
                dve.tensor_copy(value[:, u], v_ps[:, 0:JT * KV].rearrange("p (j d) -> p j d", d=KV)).then_inc(v_ready, 1)

            def feed_forward(i, u, n):
                for c in range(C):
                    dve.wait_ge(h_done, 2 * (i * C + c) + 2)
                    dve.wait_ge(silu_ready, i * C + c + 1)
                    if c == 0:
                        wait(dve, y_done, i)
                    dve.tensor_tensor(hidden[:, c, :], silu[:, c % 2, :], h_ps[:, c % 2, 1, :], ALU.mult)\
                        .then_inc(hidden_ready, 1)
                dve.wait_ge(y_done, i + 1)
                wait(dve, x_stored[u], n * 32)
                dve.tensor_tensor(out[:, u], y_ps[:, :].rearrange("p (j d) -> p j d", d=D), rows[:, u], ALU.add)\
                    .then_inc(out_ready, 1)

            over_steps(dve, NS, (0, normalise), (1, keys_and_values), (1, feed_forward))

        @block.tensor
        def _(pe):
            def turn(i, u, n):
                pe.wait_ge(cn_ready, i + 1)
                wait(pe, v_ready, i)
                for j in range(JT):
                    last = pe.transpose(c_ps[:, j * P:(j + 1) * P], cn[:, u, j, :], ident[:, :])
                last.then_inc(c_done, 1)
                pe.wait_ge(xn2_ready, i + 1)
                wait(pe, t_ready, i)
                for j in range(JT):
                    last = pe.transpose(t_ps[:, j * P:(j + 1) * P], xn2[:, u, j, :], ident[:, :])
                last.then_inc(t_done, 1)

            def keys_and_values(i, u, n):
                pe.wait_ge(c_ready, i + 1)
                wait(pe, k_ready, i)
                pe.matmul(k_ps[0:KV, :], wkv[:, 0:KV], cnT[:, u, :], start=True, stop=True).then_inc(k_done, 1)
                for j in range(JT):
                    last = pe.matmul(v_ps[:, j * KV:(j + 1) * KV], cnT[:, u, j * P:(j + 1) * P], wkv[:, KV:2 * KV],
                                     start=True, stop=True)
                last.then_inc(v_done, 1)

            def feed_forward(i, u, n):
                pe.wait_ge(t_ready, i + 1)
                for c in range(C):
                    wait(pe, silu_ready, i * C + c - 1)
                    wait(pe, hidden_ready, i * C + c - 1)
                    for part in range(2):
                        f = (1 - part) * C + c
                        pe.matmul(h_ps[:, c % 2, part, :], w1[:, f * P:(f + 1) * P], xnT[:, u, :], start=True, stop=True)\
                            .then_inc(h_done, 1)

            def down(i, u, n):
                pe.wait_ge(hidden_ready, i * C + C)
                wait(pe, out_ready, i)
                for j in range(JT):
                    at = slice(j * P, (j + 1) * P)
                    for c in range(C):
                        last = pe.matmul(y_ps[:, at], hidden[:, c, at], w2[:, c, :], start=(c == 0), stop=(c == C - 1))
                last.then_inc(y_done, 1)

            pe.wait_ge(w_in, WEIGHTS)
            over_steps(pe, NS, (1, feed_forward), (0, turn), (0, keys_and_values), (1, down))

        @block.scalar
        def _(act):
            def evacuate_turned(i, u, n):
                act.wait_ge(c_done, i + 1)
                wait(act, v_done, i - 1)
                act.activation(cnT[:, u, :], c_ps[:, :], ACT.Identity, bias=coffset[:, 0:1], scale=cgain[:, 0:1])\
                    .then_inc(c_ready, 1)
                act.wait_ge(t_done, i + 1)
                wait(act, h_done, (i - 1) * 2 * C)
                wait(act, x_stored[u], n * 32)
                act.activation(xnT[:, u, :], t_ps[:, :], ACT.Identity, bias=offset[:, 0:1], scale=gain[:, 0:1])\
                    .then_inc(t_ready, 1)

            def gates(i, u, n):
                for c in range(C):
                    act.wait_ge(h_done, 2 * (i * C + c) + 1)
                    wait(act, hidden_ready, i * C + c - 1)
                    act.activation(silu[:, c % 2, :], h_ps[:, c % 2, 0, :], ACT.Silu).then_inc(silu_ready, 1)

            act.wait_ge(w_in, WEIGHTS)
            over_steps(act, NS, (1, gates), (0, evacuate_turned))


def wide_attention(nc, io):
    with phase(nc, "wide") as (sb, ps, sem, sems, pair, open_block):
        HP, KV = H // 2, 64
        ident, wq, wo = sb("ident", [P, P]), sb("wq", [P, HP, P]), sb("wo", [P, HP, D])
        qin = sb("qin", [P, 2, TILE])
        kblock = sb("kblock", [P, 2, 2, TILE])
        vblock = sb("vblock", [P, 2, 2, 2, KV])
        mask = sb("mask", [P, 2, S])
        rows, fin = sb("rows", [P, 2, D]), sb("fin", [P, 2, D])
        qT, oT = sb("qT", [P, 2, HP, TILE]), sb("oT", [P, HP, TILE])
        scored, e, pt, out = (sb(n, [P, 2, HK]) for n in ("scored", "e", "pt", "out"))
        shifted = sb("shifted", [P, 2, HK])
        top, total, inv = (sb(n, [P, 2, H]) for n in ("top", "total", "inv"))
        a_ps, s_ps, t_ps, o_ps = (ps(n, [P, HK]) for n in ("a_ps", "s_ps", "t_ps", "o_ps"))
        q_in, v_in, m_in, x_in, stored = (pair(x) for x in ("q_in", "v_in", "m_in", "x_in", "stored"))
        w_in, cleared, q_done, q_ready, s_done, masked, topped, shifted_ready, e_ready, pt_done, pt_ready, o_done, summed, \
            inverted, out_ready, ot_done, ot_ready, y_done, fin_ready = sems(
                "w_in", "cleared", "q_done", "q_ready", "s_done", "masked", "topped", "shifted_ready", "e_ready",
                "pt_done", "pt_ready", "o_done", "summed", "inverted", "out_ready", "ot_done", "ot_ready", "y_done",
                "fin_ready")
        block = open_block()
        scale = KV ** -0.5
        by_head = lambda t: t.rearrange("p (h k) -> p h k", k=S)
        wide = lambda t: t[:, :, None].broadcast_to([P, H, S])

        @block.sync
        def _(sp):
            sp.dma_start(ident[:, :], io["ident"][:, :]).then_inc(w_in, 16)
            sp.dma_start(wq[:, :, :], io["xq"][:, :, :]).then_inc(w_in, 16)
            sp.dma_start(wo[:, :, :], io["xout"][:, :, :]).then_inc(w_in, 16)
            sp.wait_ge(cleared, 1)

            def load_queries(i, u, n):
                at = bass.ds(i * TILE, TILE)
                wait(sp, s_done, i - 1)
                sp.dma_start(qin[:, u, :], io["xnT"][:, at]).then_inc(q_in[u], 16)
                for c in range(2):
                    sp.dma_start(kblock[c * S:(c + 1) * S, u, c, :], io["kT"][:, at]).then_inc(q_in[u], 16)

            def load_mask(i, u, n):
                wait(sp, masked, i - 1)
                sp.dma_start(mask[:, u, :], io["mask"][bass.ds(i * TILE, TILE), :]).then_inc(m_in[u], 16)

            def load_values(i, u, n):
                wait(sp, o_done, i - 1)
                for c in range(2):
                    sp.dma_start(vblock[c * S:(c + 1) * S, u, :, c, :], io["v"][bass.ds(i * TILE, TILE), :]
                                 .rearrange("(b k) d -> k b d", b=2)).then_inc(v_in[u], 16)

            def load_residual(i, u, n):
                wait(sp, fin_ready, i - 1)
                sp.dma_start(rows[:, u, :], io["x5"][bass.ds(i * TILE, TILE), :]).then_inc(x_in[u], 16)

            def store(i, u, n):
                sp.wait_ge(fin_ready, i + 1)
                sp.dma_start(io["x6"][bass.ds(i * TILE, TILE), :], fin[:, u, :]).then_inc(stored[u], 16)

            over_steps(sp, NT, (0, load_queries), (0, load_mask), (2, load_values), (3, load_residual), (5, store))
            for u in range(2):
                sp.wait_ge(stored[u], 16 * (NT // 2))

        @block.gpsimd
        def _(pool):
            pool.memset(kblock[:, :, :, :], 0.0)
            pool.memset(vblock[:, :, :, :, :], 0.0).then_inc(cleared, 1)

            def shift(i, u, n):
                pool.wait_ge(topped, i + 1)
                wait(pool, e_ready, i - 1)
                pool.tensor_tensor(by_head(shifted[:, u, :]), by_head(scored[:, u, :]), wide(top[:, u, :]),
                                   ALU.subtract).then_inc(shifted_ready, 1)

            over_steps(pool, NT, (0, shift))

        @block.tensor
        def _(pe):
            def queries(i, u, n):
                pe.wait_ge(q_in[u], n * 48 + 48)
                wait(pe, q_ready, i)
                wait(pe, fin_ready, i - 4)
                for g in range(HP):
                    last = pe.matmul(a_ps[:, g * P:(g + 1) * P], wq[:, g, :], qin[:, u, :], start=True, stop=True)
                last.then_inc(q_done, 1)

            def turn_outputs(i, u, n):
                pe.wait_ge(out_ready, i + 1)
                wait(pe, pt_ready, at_most(i + 2, NT))
                for g in range(HP):
                    last = pe.transpose(t_ps[:, g * P:(g + 1) * P], out[:, u, g * P:(g + 1) * P], ident[:, :])
                last.then_inc(ot_done, 1)

            def scores(i, u, n):
                pe.wait_ge(q_ready, i + 1)
                wait(pe, masked, i)
                for g in range(HP):
                    for b in range(2):
                        last = pe.matmul(s_ps[b * S:(b + 1) * S, g * P:(g + 1) * P], qT[:, u, g, b * S:(b + 1) * S],
                                         kblock[:, u, :, b * S:(b + 1) * S], start=True, stop=True,
                                         tile_position=(0, b * S))
                last.then_inc(s_done, 1)

            def project(i, u, n):
                pe.wait_ge(ot_ready, i + 1)
                wait(pe, q_ready, at_most(i + 5, NT))
                for g in range(HP):
                    last = pe.matmul(a_ps[:, 0:D], oT[:, g, :], wo[:, g, :], start=(g == 0), stop=(g == HP - 1))
                last.then_inc(y_done, 1)

            def weigh(i, u, n):
                pe.wait_ge(pt_ready, i + 1)
                pe.wait_ge(v_in[u], n * 32 + 32)
                wait(pe, out_ready, i)
                for g in range(HP):
                    for b in range(2):
                        last = pe.matmul(o_ps[b * S:(b + 1) * S, g * P:(g + 1) * P],
                                         pt[:, u, g * P + b * S:g * P + (b + 1) * S],
                                         vblock[:, u, b, :, :], start=True, stop=True, tile_position=(0, b * S))
                last.then_inc(o_done, 1)

            def turn_weights(i, u, n):
                pe.wait_ge(e_ready, i + 1)
                wait(pe, ot_ready, i - 1)
                for g in range(HP):
                    last = pe.transpose(t_ps[:, g * P:(g + 1) * P], e[:, u, g * P:(g + 1) * P], ident[:, :])
                last.then_inc(pt_done, 1)

            pe.wait_ge(w_in, 48)
            over_steps(pe, NT, (0, queries), (4, turn_outputs), (1, scores), (4, project), (3, weigh), (2, turn_weights))

        @block.vector
        def _(dve):
            def soften(i, u, n):
                dve.wait_ge(s_done, i + 1)
                dve.wait_ge(m_in[u], n * 16 + 16)
                wait(dve, shifted_ready, i - 1)
                dve.tensor_tensor(by_head(scored[:, u, :]), by_head(s_ps[:, :]),
                                  mask[:, u, None, :].broadcast_to([P, H, S]), ALU.add).then_inc(masked, 1)
                dve.wait_ge(masked, i + 1)
                dve.tensor_reduce(top[:, u, :], by_head(scored[:, u, :]), axis=AX.X, op=ALU.max).then_inc(topped, 1)

            def sums(i, u, n):
                dve.wait_ge(e_ready, i + 1)
                dve.tensor_reduce(total[:, u, :], by_head(e[:, u, :]), axis=AX.X, op=ALU.add).then_inc(summed, 1)
                dve.wait_ge(summed, i + 1)
                dve.reciprocal(inv[:, u, :], total[:, u, :]).then_inc(inverted, 1)

            def normalise(i, u, n):
                dve.wait_ge(inverted, i + 1)
                dve.wait_ge(o_done, i + 1)
                wait(dve, ot_done, i - 1)
                dve.tensor_tensor(by_head(out[:, u, :]), by_head(o_ps[:, :]), wide(inv[:, u, :]), ALU.mult)\
                    .then_inc(out_ready, 1)

            def residual(i, u, n):
                dve.wait_ge(y_done, i + 1)
                dve.wait_ge(x_in[u], n * 16 + 16)
                wait(dve, stored[u], n * 16)
                dve.tensor_tensor(fin[:, u, :], a_ps[:, 0:D], rows[:, u, :], ALU.add).then_inc(fin_ready, 1)

            over_steps(dve, NT, (0, soften), (1, sums), (3, residual), (2, normalise))

        @block.scalar
        def _(act):
            def evacuate_weights(i, u, n):
                act.wait_ge(pt_done, i + 1)
                wait(act, o_done, i - 1)
                act.activation(pt[:, u, :], t_ps[:, :], ACT.Copy).then_inc(pt_ready, 1)

            def evacuate_queries(i, u, n):
                act.wait_ge(q_done, i + 1)
                wait(act, s_done, i - 1)
                act.activation(qT[:, u], a_ps[:, :].rearrange("p (g t) -> p g t", t=TILE), ACT.Copy, scale=scale)\
                    .then_inc(q_ready, 1)

            def evacuate_outputs(i, u, n):
                act.wait_ge(ot_done, i + 1)
                wait(act, y_done, i)
                act.activation(oT[:, :, :], t_ps[:, :].rearrange("p (g t) -> p g t", t=TILE), ACT.Copy).then_inc(ot_ready, 1)

            def exponentials(i, u, n):
                act.wait_ge(shifted_ready, i + 1)
                wait(act, pt_done, i - 1)
                wait(act, summed, i - 1)
                act.activation(e[:, u, :], shifted[:, u, :], ACT.Exp).then_inc(e_ready, 1)

            over_steps(act, NT, (3, evacuate_weights), (0, evacuate_queries), (4, evacuate_outputs), (2, exponentials))


SCRATCH = {
    "QT": (D, TOK), "KT": (D, TOK), "V": (TOK, D), "AO": (TOK, D), "bias0": (P, HK), "xnT": (D, TOK),
    "latT": (64, TOK), "lat_w": (P, HK), "x2": (TOK, D), "x3": (TOK, D), "x4": (TOK, D), "x5": (TOK, D),
    "x6": (TOK, D), "kT": (64, TOK), "v": (TOK, 64),
}


def build(nc, io, upto=99):
    io["latent"] = 64
    phases = [lambda: tpms_bias(nc, io), lambda: latent_weights(nc, io), lambda: project(nc, io, 0),
              lambda: narrow_attention(nc, io, "attn0", True), lambda: close_attention(nc, io, 0),
              lambda: moe(nc, io, 0), lambda: project(nc, io, 1),
              lambda: narrow_attention(nc, io, "attn1", False), lambda: close_attention(nc, io, 1),
              lambda: context_and_gated(nc, io), lambda: wide_attention(nc, io), lambda: moe(nc, io, 1)]
    for part in phases[:upto]:
        part()


def constants():
    import numpy as np

    f = np.float32
    token = np.arange(TILE) % S
    pos = (np.arange(S, dtype=f) / f(S) * f(2.0 * math.pi)).astype(f)
    head = np.arange(P)[:, None] // HD == np.arange(H)[None, :]
    seen = token[:, None] >= np.arange(S)[None, :]
    decay = np.where(np.arange(ST) % S == 0, 0.0, 0.9).astype(f)
    first_expert = np.where(np.arange(JT * 8) % 8 == 0, 0.0, 1.0).astype(f)
    return {
        "ident": np.eye(P, dtype=f),
        "pos_q": pos[token][:, None],
        "pos_k": np.broadcast_to(pos, (P, S)),
        "pos_z": ((pos[token][:, None] + pos[None, :]) * f(0.5)).astype(f),
        "head_mask": head.astype(f),
        "copy_mask": (np.arange(P)[:, None] // S == np.arange(2)[None, :]).astype(f),
        "causal": np.tile(np.where(seen, 0.0, -1e30).astype(f), (1, H)),
        "decay": np.broadcast_to(decay, (P, ST)),
        "not_first": np.broadcast_to(first_expert, (P, JT * 8)),
    }


def layouts(x):
    import numpy as np

    col = lambda a: a.reshape(-1, 1)
    both = lambda routed, shared: np.concatenate([g(routed), g(shared)[None]], 0)
    w13 = lambda *n: both(*n).reshape(9, P, 2, D).transpose(3, 0, 2, 1)
    b13 = lambda *n: both(*n).reshape(9, P, 2).transpose(1, 0, 2)
    g = lambda n: x[n]
    return {
        "x": g("x").reshape(TOK, D),
        "ctx": g("ctx_1024").reshape(TOK, D),
        "ctxT": g("ctx_1024").reshape(TOK, D).T,
        "mask": g("mask_BxSxS2_ff0").reshape(TOK, S),
        **{n: g(n) for n in ("L0_attn_Wq", "L0_attn_Wk", "L0_attn_Wv", "L0_attn_Wo", "L0_attn_bo", "L0_attn_phase",
                             "L1_attn_basis_w", "L1_attn_core", "L1_attn_head_residual", "L1_attn_o_b")},
        **{n: col(g(n)) for n in ("L0_attn_bq", "L0_attn_bk", "L0_attn_bv", "L1_attn_v_b", "L1_xattn_ln_g",
                                  "L1_xattn_ln_b", "L1_xattn_cln_g", "L1_xattn_cln_b")},
        "L0_attn_threshold": g("L0_attn_threshold").reshape(1),
        "L0_attn_temperature": g("L0_attn_temperature").reshape(1),
        "basis_T": g("L1_attn_basis_w").T,
        "core_T": g("L1_attn_core").T,
        "L1_attn_v_wT": g("L1_attn_v_w").T,
        "L1_attn_o_wT": g("L1_attn_o_w").T,
        "gate0_T": g("L0_ffn_gate_w").T,
        "gate0_b": g("L0_ffn_gate_b"),
        "up0": np.stack([w13("L0_ffn_w1", "L0_ffn_sw1"), w13("L0_ffn_w3", "L0_ffn_sw3")], 3).reshape(D, 9, 4, P),
        "up0_b": np.stack([b13("L0_ffn_b1", "L0_ffn_sb1"), b13("L0_ffn_b3", "L0_ffn_sb3")], 3).reshape(P, 9, 4),
        "down0": both("L0_ffn_w2", "L0_ffn_sw2").transpose(2, 0, 1),
        "down0_b": both("L0_ffn_b2", "L0_ffn_sb2"),
        "xq": g("L1_xattn_Wq").reshape(D, 8, P),
        "xkv": g("L1_xattn_Wkv"),
        "xout": g("L1_xattn_Wout").reshape(8, P, D).transpose(1, 0, 2),
        "xw1": g("L1_xattn_W1"),
        "xw2": g("L1_xattn_W2").reshape(4, P, D).transpose(1, 0, 2),
        "gate1_T": g("L1_ffn_gate_w").T,
        "up1": g("L1_ffn_w12").reshape(8, 2, 2, P, D).transpose(4, 0, 2, 1, 3).reshape(D, 8, 4, P),
        "down1": g("L1_ffn_w3").reshape(8, D, 2, P).transpose(3, 0, 2, 1),
    }


def kernel(**inputs):
    import numpy as np
    import concourse.bacc as bacc
    from concourse.bass_utils import run_bass_kernel_spmd

    nc = bacc.Bacc("TRN2", target_bir_lowering=False, num_devices=1)
    arrays, io = {}, {}
    for name, a in {**constants(), **layouts({k: np.asarray(v) for k, v in inputs.items()})}.items():
        arrays[f"in_{name}"] = np.ascontiguousarray(a)
        dram = nc.dram_tensor(f"in_{name}", a.shape, mybir.dt.from_np(a.dtype), kind="ExternalInput").ap()
        io[name] = dram
    for name, shape in SCRATCH.items():
        io[name] = nc.dram_tensor(f"scratch_{name}", shape, F32, kind="Internal").ap()
    io["out"] = nc.dram_tensor("out", (TOK, D), F32, kind="ExternalOutput").ap()
    build(nc, io)
    result = run_bass_kernel_spmd(nc, [arrays], core_ids=[0])
    return result.results[0]["out"].reshape(B, S, D)
```

```python
import math
from contextlib import ExitStack, contextmanager

import concourse.bass as bass
from concourse import mybir

F32 = mybir.dt.float32
F32R = mybir.dt.float32r
ALU = mybir.AluOpType
ACT = mybir.ActivationFunctionType
AX = mybir.AxisListType

B, S, D = 128, 64, 128
TOK = B * S
P = 128
TILE = 2 * S
NT = TOK // TILE
ST = 512
NS = TOK // ST
JT = ST // TILE
H = 16
HD = D // H
HK = H * S
EPS = 1e-5


def wait(eng, sem, value):
    if not (isinstance(value, int) and value <= 0):
        eng.wait_ge(sem, value)


def at_most(value, limit):
    return min(value, limit) if isinstance(value, int) else value


def apart(eng, sem):
    eng.sem_inc(sem, 1)


def over_steps(eng, n, *stages):
    deepest = max(lag for lag, _ in stages)
    first = deepest + 2 + (deepest % 2)

    def step(k):
        for lag, fn in stages:
            if 0 <= k - lag < n:
                fn(k - lag, (k - lag) % 2, (k - lag) // 2)

    for k in range(first):
        step(k)
    with eng.Fori(first // 2, n // 2) as j:
        for p in range(2):
            for lag, fn in stages:
                fn(j * 2 + (p - lag), (p - lag) % 2, j + (p - lag) // 2)
    for k in range(n, n + deepest):
        step(k)


def rows_of(dram, i, size):
    return dram[bass.ds(i * size, size), :].rearrange("(j p) d -> p j d", p=P)


def product_of_parts(pe, out, weights, moving):
    (w_high, w_low), (m_high, m_low) = weights, moving
    pe.matmul(out, w_high, m_high, start=True, stop=False)
    pe.matmul(out, w_high, m_low, start=False, stop=False)
    return pe.matmul(out, w_low, m_high, start=False, stop=True)


@contextmanager
def phase(nc, name):
    taken = []

    def sem(part):
        taken.append(nc.alloc_semaphore(name=f"{name}_{part}"))
        return taken[-1]

    with ExitStack() as ctx:
        def sb(part, shape, dtype=F32):
            return ctx.enter_context(nc.sbuf_tensor(f"{name}_{part}", shape, dtype))

        def ps(part, shape):
            return ctx.enter_context(nc.psum_tensor(f"{name}_{part}", shape, F32))

        def sems(*parts):
            return [sem(part) for part in parts]

        def pair(part):
            return [sem(f"{part}{u}") for u in range(2)]

        yield sb, ps, sem, sems, pair, lambda: ctx.enter_context(nc.Block())
    nc.clear_and_free_semaphores(taken)
    nc.all_engine_barrier()


def layer_norm(sb, sems, name, n=JT):
    stats, moments = sb(f"{name}_stats", [P, n, 6]), sb(f"{name}_moments", [P, n, 2])
    var_eps, rstd, power = (sb(f"{name}_{x}", [P, n]) for x in ("var_eps", "rstd", "power"))
    stats_done, moments_done, eps_added, rstd_done, power_set, apart_dve, apart_pool = sems(*(
        f"{name}_{x}" for x in ("stats_done", "moments_done", "eps_added", "rstd_done", "power_set", "apart_dve",
                                "apart_pool")))

    def set_up(pool):
        pool.memset(power[:, :], -0.5).then_inc(power_set, 1)
        pool.wait_ge(power_set, 1)

    def measure(dve, rows, i):
        for j in range(n):
            last = dve.bn_stats(stats[:, j, :], rows[:, j, :])
        last.then_inc(stats_done, 1)
        dve.wait_ge(stats_done, i + 1)
        apart(dve, apart_dve)
        for j in range(n):
            last = dve.bn_aggr(moments[:, j, :], stats[:, j, :])
        last.then_inc(moments_done, 1)

    def invert(pool, i):
        pool.wait_ge(moments_done, i + 1)
        apart(pool, apart_pool)
        pool.tensor_scalar(var_eps[:, :], moments[:, :, 1], EPS, 0.0, ALU.add, ALU.add).then_inc(eps_added, 1)
        pool.wait_ge(eps_added, i + 1)
        pool.tensor_tensor(rstd[:, :], var_eps[:, :], power[:, :], ALU.pow).then_inc(rstd_done, 1)

    def apply(dve, out, rows, i, done):
        dve.wait_ge(rstd_done, i + 1)
        for j in range(n):
            last = dve.tensor_scalar(out[:, j, :], rows[:, j, :], moments[:, j, 0:1], rstd[:, j:j + 1],
                                     ALU.subtract, ALU.mult)
        last.then_inc(done, 1)

    return set_up, measure, invert, apply


def project(nc, io, layer):
    with phase(nc, f"project{layer}") as (sb, ps, sem, sems, pair, open_block):
        R = D if layer == 0 else io["latent"]
        wq, wk, wv, ident = (sb(n, [P, w]) for n, w in (("wq", P), ("wk", R), ("wv", P), ("ident", P)))
        bq, bqs, bk = (sb(n, [P, 1]) for n in ("bq", "bqs", "bk"))
        rows = sb("rows", [P, 2, JT, D])
        xn = sb("xn", [P, 2, JT, D])
        xnT = sb("xnT", [P, 2, ST])
        q, k, v = (sb(n, [P, 2, ST]) for n in ("q", "k", "v"))
        tp, qp, kp, vp = (ps(n, [P, 2, ST]) for n in ("tp", "qp", "kp", "vp"))
        set_up, measure, invert, apply = layer_norm(sb, sems, "ln")
        x_in, across_stored, stored = pair("x_in"), pair("across_stored"), pair("stored")
        w_in, bias_scaled, xn_ready, t_done, xnT_ready, q_done, k_done, v_done, q_ready, k_ready, v_ready = sems(
            "w_in", "bias_scaled", "xn_ready", "t_done", "xnT_ready", "q_done", "k_done", "v_done",
            "q_ready", "k_ready", "v_ready")
        scale = HD ** -0.5
        block = open_block()
        if layer == 0:
            source, weights = io["x"], ((wq, io["L0_attn_Wq"]), (wk, io["L0_attn_Wk"]), (wv, io["L0_attn_Wv"]), (ident, io["ident"]),
                                     (bq, io["L0_attn_bq"]), (bk, io["L0_attn_bk"]))
            across, across_ready, ACROSS_LAG = q, q_ready, 3
        else:
            source, weights = io["x3"], ((wk, io["basis_T"]), (wv, io["L1_attn_v_wT"]), (ident, io["ident"]))
            across, across_ready, ACROSS_LAG = xnT, xnT_ready, 2
        WEIGHTS = len(weights) * 16

        @block.sync
        def _(sp):
            def load(i, u, n):
                wait(sp, xn_ready, i - 1)
                sp.dma_start(rows[:, u, :, :], rows_of(source, i, ST)).then_inc(x_in[u], 16)
                if isinstance(i, int) and i == 0:
                    for dst, src in weights:
                        sp.dma_start(dst[:, :], src[:, :]).then_inc(w_in, 16)

            def store_across(i, u, n):
                sp.wait_ge(across_ready, i + 1)
                sp.dma_start((io["QT"] if layer == 0 else io["xnT"])[:, bass.ds(i * ST, ST)],
                             across[:, u, :]).then_inc(across_stored[u], 16)

            def store(i, u, n):
                sp.wait_ge(k_ready, i + 1)
                sp.dma_start((io["KT"] if layer == 0 else io["latT"])[:, bass.ds(i * ST, ST)],
                             k[0:R, u, :]).then_inc(stored[u], 16)
                sp.wait_ge(v_ready, i + 1)
                sp.dma_start(rows_of(io["V"], i, ST), v[:, u, :].rearrange("p (j d) -> p j d", d=D)).then_inc(stored[u], 16)

            over_steps(sp, NS, (0, load), (ACROSS_LAG, store_across), (3, store))
            for u in range(2):
                sp.wait_ge(across_stored[u], 16 * (NS // 2))
                sp.wait_ge(stored[u], 32 * (NS // 2))

        @block.vector
        def _(dve):
            def measure_rows(i, u, n):
                dve.wait_ge(x_in[u], n * 16 + 16)
                measure(dve, rows[:, u], i)

            def normalise(i, u, n):
                wait(dve, t_done, i - 1)
                apply(dve, xn[:, u], rows[:, u], i, xn_ready)

            def evacuate(i, u, n):
                wait(dve, stored[u], n * 32)
                dve.wait_ge(k_done, i + 1)
                if layer == 0:
                    dve.tensor_scalar(k[:, u, :], kp[:, u, :], bk[:, 0:1], None, ALU.add).then_inc(k_ready, 1)
                else:
                    dve.tensor_copy(k[0:R, u, :], kp[0:R, u, :]).then_inc(k_ready, 1)
                dve.wait_ge(v_done, i + 1)
                dve.tensor_copy(v[:, u, :], vp[:, u, :]).then_inc(v_ready, 1)

            def scale_bias(i, u, n):
                if layer == 0 and isinstance(i, int) and i == 0:
                    dve.wait_ge(w_in, WEIGHTS)
                    dve.tensor_scalar(bqs[:, :], bq[:, :], scale, None, ALU.mult).then_inc(bias_scaled, 1)

            over_steps(dve, NS, (1, normalise), (0, measure_rows), (1, scale_bias), (2, evacuate))

        @block.gpsimd
        def _(pool):
            set_up(pool)
            over_steps(pool, NS, (0, lambda i, u, n: invert(pool, i)))

        @block.tensor
        def _(pe):
            def transpose(i, u, n):
                pe.wait_ge(xn_ready, i + 1)
                wait(pe, xnT_ready, i - 1)
                for j in range(JT):
                    last = pe.transpose(tp[:, u, j * P:(j + 1) * P], xn[:, u, j, :], ident[:, :])
                last.then_inc(t_done, 1)

            def products(i, u, n):
                pe.wait_ge(xnT_ready, i + 1)
                if layer == 0:
                    wait(pe, q_ready, i - 1)
                    pe.matmul(qp[:, u, :], wq[:, :], xnT[:, u, :], start=True, stop=True).then_inc(q_done, 1)
                wait(pe, k_ready, i - 1)
                pe.matmul(kp[0:R, u, :], wk[:, :], xnT[:, u, :], start=True, stop=True).then_inc(k_done, 1)
                wait(pe, v_ready, i - 1)
                for j in range(JT):
                    last = pe.matmul(vp[:, u, j * P:(j + 1) * P], xnT[:, u, j * P:(j + 1) * P], wv[:, :],
                                     start=True, stop=True)
                last.then_inc(v_done, 1)

            pe.wait_ge(w_in, WEIGHTS)
            over_steps(pe, NS, (2, products), (1, transpose))

        @block.scalar
        def _(act):
            def evacuate_transpose(i, u, n):
                act.wait_ge(t_done, i + 1)
                wait(act, v_done, i - 1)
                if layer == 1:
                    wait(act, across_stored[u], n * 16)
                act.activation(xnT[:, u, :], tp[:, u, :], ACT.Copy).then_inc(xnT_ready, 1)

            def evacuate_q(i, u, n):
                act.wait_ge(bias_scaled, 1)
                act.wait_ge(q_done, i + 1)
                wait(act, across_stored[u], n * 16)
                act.activation(q[:, u, :], qp[:, u, :], ACT.Identity, bias=bqs[:, 0:1], scale=scale).then_inc(q_ready, 1)

            if layer == 0:
                over_steps(act, NS, (2, evacuate_q), (1, evacuate_transpose))
            else:
                over_steps(act, NS, (0, evacuate_transpose))


def tpms_bias(nc, io):
    with phase(nc, "tpms") as (sb, ps, sem, sems, pair, open_block):
        offsets = sb("offsets", [P, H, 3])
        thr, tmp = sb("thr", [P, 1]), sb("tmp", [P, 1])
        inv = sb("inv", [P, 1])
        pos_q, pos_k, pos_z = sb("pos_q", [P, 1]), sb("pos_k", [P, S]), sb("pos_z", [P, S])
        pq = sb("pq", [P, 2, H])
        pk, pz = sb("pk", [P, 2, H, S]), sb("pz", [P, 2, H, S])
        turns_q, turns_k = sb("turns_q", [P, 2, H]), sb("turns_k", [P, 2, H, S])
        val, part = sb("val", [P, H, S]), sb("part", [P, H, S])
        in_done, step, sines = sems("in_done", "step", "sines")
        block = open_block()
        MAGIC = 1.5 * 2.0 ** 23
        TURN_HIGH = 6.28125
        TURN_LOW = 2 * math.pi - TURN_HIGH
        angles = (pq, pk, pz)
        STEPS = 27

        @block.sync
        def _(sp):
            for dst, src in ((offsets[:, :, :], io["L0_attn_phase"].partition_broadcast(P)),
                             (thr[:, :], io["L0_attn_threshold"].partition_broadcast(P)),
                             (tmp[:, :], io["L0_attn_temperature"].partition_broadcast(P)),
                             (pos_q[:, :], io["pos_q"][:, :]), (pos_k[:, :], io["pos_k"][:, :]), (pos_z[:, :], io["pos_z"][:, :])):
                sp.dma_start(dst, src).then_inc(in_done, 16)
            sp.wait_ge(step, STEPS)
            sp.dma_start(io["bias0"][:, :], val[:, :, :].rearrange("p h s -> p (h s)")).then_inc(in_done, 16)
            sp.wait_ge(in_done, 7 * 16)

        @block.vector
        def _(dve):
            count = [0]

            def then(instruction):
                count[0] += 1
                instruction.then_inc(step, 1)
                dve.wait_ge(step, count[0])

            dve.wait_ge(in_done, 6 * 16)
            heads = lambda t: t[:, None, :].broadcast_to([P, H, S])
            keys = lambda n: offsets[:, :, n:n + 1].broadcast_to([P, H, S])
            dve.tensor_scalar(pq[:, 0, :], offsets[:, :, 0], pos_q[:, 0:1], None, ALU.add)
            dve.tensor_tensor(pk[:, 0], keys(1), heads(pos_k), ALU.add)
            then(dve.tensor_tensor(pz[:, 0], keys(2), heads(pos_z), ALU.add))
            for a in angles:
                last = dve.tensor_scalar(a[:, 1], a[:, 0], math.pi / 2, None, ALU.add)
            then(last)
            for a, t in ((pq, turns_q), (pk, turns_k), (pz, turns_k)):
                then(dve.tensor_scalar(t[:], a[:], 1 / (2 * math.pi), MAGIC, ALU.mult, ALU.add))
                then(dve.tensor_scalar(t[:], t[:], MAGIC, None, ALU.subtract))
                then(dve.scalar_tensor_tensor(out=a[:], in0=t[:], scalar=-TURN_HIGH, in1=a[:], op0=ALU.mult, op1=ALU.add))
                then(dve.scalar_tensor_tensor(out=a[:], in0=t[:], scalar=-TURN_LOW, in1=a[:], op0=ALU.mult, op1=ALU.add))
                then(dve.tensor_scalar(a[:], a[:], math.pi, -math.pi, ALU.min, ALU.max))
            then(dve.tensor_scalar(inv[:, :], tmp[:, :], 1e-6, None, ALU.add))
            then(dve.reciprocal(inv[:, :], inv[:, :]))
            dve.wait_ge(sines, 1)
            query = lambda n: pq[:, n, :, None].broadcast_to([P, H, S])
            then(dve.tensor_tensor(val[:], query(0), pk[:, 1], ALU.mult))
            then(dve.tensor_tensor(part[:], pk[:, 0], pz[:, 1], ALU.mult))
            then(dve.tensor_tensor(val[:], val[:], part[:], ALU.add))
            then(dve.tensor_tensor(part[:], query(1), pz[:, 0], ALU.mult))
            then(dve.tensor_tensor(val[:], val[:], part[:], ALU.add))
            then(dve.tensor_scalar(val[:], val[:], thr[:, 0:1], None, ALU.subtract))
            dve.wait_ge(sines, 2)
            then(dve.tensor_scalar(val[:], val[:], 1e-6, None, ALU.add))
            dve.wait_ge(sines, 3)
            then(dve.tensor_scalar(val[:], val[:], 0.3, None, ALU.mult))
            assert count[0] == STEPS

        @block.scalar
        def _(act):
            act.wait_ge(step, 19)
            for a in angles:
                last = act.activation(a[:], a[:], ACT.Sin)
            last.then_inc(sines, 1)
            act.wait_ge(step, 25)
            act.activation(val[:], val[:], ACT.Sigmoid, scale=inv[:, 0:1]).then_inc(sines, 1)
            act.wait_ge(step, 26)
            act.activation(val[:], val[:], ACT.Ln).then_inc(sines, 1)


def narrow_attention(nc, io, name, first):
    with phase(nc, name) as (sb, ps, sem, sems, pair, open_block):
        HP = H // 2
        W = HD + 1
        ident, bias = sb("ident", [P, P]), sb("bias", [P, HK])
        copy_mask = sb("copy_mask", [P, 2])
        qin = sb("qin", [P, 2, TILE])
        vin = sb("vin", [P, 2, 2, D])
        vblock = sb("vblock", [P, 2, 2, HP, 2 * W])
        scored, e, pt = (sb(n, [P, 2, HK]) for n in ("scored", "e", "pt"))
        top, inv = sb("top", [P, 2, H]), sb("inv", [P, 2, H])
        out = sb("out", [P, 2, D])
        if first:
            kin = sb("kin", [P, 2, TILE])
            kblock = sb("kblock", [P, 2, H, TILE])
            head_mask = sb("head_mask", [P, H])
        else:
            kblock = sb("kblock", [P, 2, 2, TILE])
            lat_w = sb("lat_w", [P, HK])
            qT = sb("qT", [P, 2, HP, TILE])
            q_ps = ps("q_ps", [P, HP, TILE])
        SB = 2 if first else 1
        s_ps, pt_ps = ps("s_ps", [P, SB, HK]), ps("pt_ps", [P, HK])
        o_ps = ps("o_ps", [P, ST])
        q_in, k_in, v_in, out_stored = (pair(x) for x in ("q_in", "k_in", "v_in", "out_stored"))
        w_in, cleared, keys_spread_pool, keys_spread_act, keys_spread_dve, vblock_ready, q_done, q_ready, s_done, biased, topped, shifted, e_ready, \
            pt_done, pt_ready, o_done, inverted, out_ready, apart_pool = sems(
                "w_in", "cleared", "keys_spread_pool", "keys_spread_act", "keys_spread_dve", "vblock_ready", "q_done", "q_ready", "s_done", "biased", "topped",
                "shifted", "e_ready", "pt_done", "pt_ready", "o_done", "inverted", "out_ready", "apart_pool")
        block = open_block()
        BY_POOL, BY_ACT, BY_DVE = range(0, 7), range(7, 15), range(15, H)
        WEIGHTS = 16 * 4

        def values(t):
            return o_ps[:, 0:HP * 2 * W].rearrange("p (h w) -> p h w", w=W)

        @block.sync
        def _(sp):
            sp.dma_start(ident[:, :], io["ident"][:, :]).then_inc(w_in, 16)
            sp.dma_start(copy_mask[:, :], io["copy_mask"][:, :]).then_inc(w_in, 16)
            sp.dma_start(bias[:, :], (io["bias0"] if first else io["causal"])[:, :]).then_inc(w_in, 16)
            if first:
                sp.dma_start(head_mask[:, :], io["head_mask"][:, :]).then_inc(w_in, 16)
            else:
                sp.dma_start(lat_w[:, :], io["lat_w"][:, :]).then_inc(w_in, 16)
            sp.wait_ge(cleared, 1)

            def load_queries(i, u, n):
                wait(sp, s_done if first else q_done, i - 1)
                sp.dma_start(qin[:, u, :], io["QT" if first else "xnT"][:, bass.ds(i * TILE, TILE)])\
                    .then_inc(q_in[u], 16)

            def load_keys(i, u, n):
                at = bass.ds(i * TILE, TILE)
                if first:
                    wait(sp, keys_spread_pool, i - 1)
                    wait(sp, keys_spread_act, i - 1)
                    wait(sp, keys_spread_dve, i - 1)
                    sp.dma_start(kin[:, u, :], io["KT"][:, at]).then_inc(k_in[u], 16)
                else:
                    wait(sp, s_done, i - 1)
                    for c in range(2):
                        sp.dma_start(kblock[c * S:(c + 1) * S, u, c, :], io["latT"][:, at]).then_inc(k_in[u], 16)

            def load_values(i, u, n):
                wait(sp, vblock_ready, i - 1)
                for c in range(2):
                    sp.dma_start(vin[c * S:(c + 1) * S, u], io["V"][bass.ds(i * TILE, TILE), :]
                                 .rearrange("(b k) d -> k b d", b=2)).then_inc(v_in[u], 16)

            def store(i, u, n):
                sp.wait_ge(out_ready, i + 1)
                sp.dma_start(io["AO"][bass.ds(i * TILE, TILE), :], out[:, u, :]).then_inc(out_stored[u], 16)

            if first:
                over_steps(sp, NT, (0, load_keys), (0, load_queries), (0, load_values), (4, store))
            else:
                over_steps(sp, NT, (0, load_queries), (1, load_keys), (1, load_values), (4, store))
            for u in range(2):
                sp.wait_ge(out_stored[u], 16 * (NT // 2))

        @block.gpsimd
        def _(pool):
            if not first:
                pool.memset(kblock[:, :, :, :], 0.0)
            pool.memset(vblock[:, :, :, :, :], 0.0).then_inc(cleared, 1)
            pool.wait_ge(cleared, 1)
            for c in range(2):
                last = pool.memset(vblock[c * S:(c + 1) * S, :, :, :, c * W + HD:c * W + W], 1.0)
            last.then_inc(cleared, 1)
            pool.wait_ge(w_in, WEIGHTS)

            pool.wait_ge(cleared, 2)

            def spread_keys(i, u, n):
                pool.wait_ge(k_in[u], n * 16 + 16)
                wait(pool, s_done, i - 1)
                apart(pool, apart_pool)
                for h in BY_POOL:
                    last = pool.tensor_scalar(kblock[:, u, h, :], kin[:, u, :], head_mask[:, h:h + 1], 0.0,
                                              ALU.mult, ALU.add)
                last.then_inc(keys_spread_pool, 1)

            def spread_values(i, u, n):
                pool.wait_ge(v_in[u], n * 32 + 32)
                wait(pool, o_done, i - 1)
                apart(pool, apart_pool)
                for b in range(2):
                    for c in range(2):
                        heads = vin[:, u, b, :].rearrange("p (g c d) -> p g c d", c=2, d=HD)[:, :, c, :]
                        last = pool.tensor_scalar(vblock[:, u, b, :, c * W:c * W + HD], heads, copy_mask[:, c:c + 1], 0.0,
                                                  ALU.mult, ALU.add)
                last.then_inc(vblock_ready, 1)

            if first:
                over_steps(pool, NT, (0, spread_keys), (1, spread_values))
            else:
                over_steps(pool, NT, (0, spread_values))

        @block.tensor
        def _(pe):
            def queries(i, u, n):
                pe.wait_ge(q_in[u], n * 16 + 16)
                wait(pe, q_ready, i)
                for g in range(HP):
                    last = pe.matmul(q_ps[:, g, :], lat_w[:, g * P:(g + 1) * P], qin[:, u, :], start=True, stop=True)
                last.then_inc(q_done, 1)

            def scores(i, u, n):
                if first:
                    pe.wait_ge(q_in[u], n * 16 + 16)
                    pe.wait_ge(keys_spread_pool, i + 1)
                    pe.wait_ge(keys_spread_act, i + 1)
                    pe.wait_ge(keys_spread_dve, i + 1)
                else:
                    pe.wait_ge(q_ready, i + 1)
                    pe.wait_ge(k_in[u], n * 32 + 32)
                wait(pe, biased, i + 1 - SB)
                if first:
                    for half in range(2):
                        for b in range(2):
                            last = pe.matmul(
                                s_ps[b * S:(b + 1) * S, u % SB, half * ST:(half + 1) * ST],
                                qin[:, u, b * S:(b + 1) * S],
                                kblock[:, u, half * HP:(half + 1) * HP, b * S:(b + 1) * S],
                                start=True, stop=True, tile_position=(0, b * S))
                else:
                    for g in range(HP):
                        for b in range(2):
                            last = pe.matmul(
                                s_ps[b * S:(b + 1) * S, u % SB, g * P:(g + 1) * P],
                                qT[:, u, g, b * S:(b + 1) * S],
                                kblock[:, u, :, b * S:(b + 1) * S],
                                start=True, stop=True, tile_position=(0, b * S))
                last.then_inc(s_done, 1)

            def weigh(i, u, n):
                pe.wait_ge(pt_ready, i + 1)
                pe.wait_ge(vblock_ready, i + 1)
                wait(pe, out_ready, i)
                for g in range(HP):
                    for b in range(2):
                        last = pe.matmul(
                            o_ps[b * S:(b + 1) * S, g * 2 * W:(g + 1) * 2 * W],
                            pt[:, u, g * P + b * S:g * P + (b + 1) * S],
                            vblock[:, u, b, g, :],
                            start=True, stop=True, tile_position=(0, b * S))
                last.then_inc(o_done, 1)

            def turn(i, u, n):
                pe.wait_ge(e_ready, i + 1)
                wait(pe, pt_ready, i)
                for g in range(HP):
                    last = pe.transpose(pt_ps[:, g * P:(g + 1) * P], e[:, u, g * P:(g + 1) * P], ident[:, :])
                last.then_inc(pt_done, 1)

            pe.wait_ge(w_in, WEIGHTS)
            pe.wait_ge(cleared, 2)
            if first:
                over_steps(pe, NT, (0, scores), (2, weigh), (1, turn))
            else:
                over_steps(pe, NT, (0, queries), (1, scores), (3, weigh), (2, turn))

        @block.vector
        def _(dve):
            def soften(i, u, n):
                dve.wait_ge(s_done, i + 1)
                wait(dve, e_ready, i - 1)
                dve.tensor_tensor(scored[:, u, :], s_ps[:, u % SB, :], bias[:, :], ALU.add).then_inc(biased, 1)
                dve.wait_ge(biased, i + 1)
                by_head = scored[:, u, :].rearrange("p (h k) -> p h k", k=S)
                dve.tensor_reduce(top[:, u, :], by_head, axis=AX.X, op=ALU.max).then_inc(topped, 1)
                dve.wait_ge(topped, i + 1)
                dve.tensor_tensor(by_head, by_head, top[:, u, :, None].broadcast_to([P, H, S]),
                                  ALU.subtract).then_inc(shifted, 1)

            def spread_keys(i, u, n):
                dve.wait_ge(k_in[u], n * 16 + 16)
                wait(dve, s_done, i - 1)
                for h in BY_DVE:
                    last = dve.tensor_scalar(kblock[:, u, h, :], kin[:, u, :], head_mask[:, h:h + 1], None, ALU.mult)
                last.then_inc(keys_spread_dve, 1)

            def normalise(i, u, n):
                dve.wait_ge(o_done, i + 1)
                wait(dve, out_stored[u], n * 16)
                dve.reciprocal(inv[:, u, :], values(o_ps)[:, :, HD]).then_inc(inverted, 1)
                dve.wait_ge(inverted, i + 1)
                dve.tensor_tensor(out[:, u, :].rearrange("p (h d) -> p h d", d=HD), values(o_ps)[:, :, 0:HD],
                                  inv[:, u, :, None].broadcast_to([P, H, HD]), ALU.mult).then_inc(out_ready, 1)

            dve.wait_ge(w_in, WEIGHTS)
            if first:
                over_steps(dve, NT, (0, spread_keys), (1, soften), (3, normalise))
            else:
                over_steps(dve, NT, (0, soften), (2, normalise))

        @block.scalar
        def _(act):
            def spread_keys(i, u, n):
                act.wait_ge(k_in[u], n * 16 + 16)
                wait(act, s_done, i - 1)
                for h in BY_ACT:
                    last = act.activation(kblock[:, u, h, :], kin[:, u, :], ACT.Copy, scale=head_mask[:, h:h + 1])
                last.then_inc(keys_spread_act, 1)

            def evacuate_queries(i, u, n):
                act.wait_ge(q_done, i + 1)
                wait(act, s_done, i - 1)
                act.activation(qT[:, u], q_ps[:, :, :], ACT.Copy).then_inc(q_ready, 1)

            def exponentials(i, u, n):
                act.wait_ge(shifted, i + 1)
                wait(act, pt_done, i - 1)
                act.activation(e[:, u, :], scored[:, u, :], ACT.Exp).then_inc(e_ready, 1)

            def evacuate_turned(i, u, n):
                act.wait_ge(pt_done, i + 1)
                wait(act, o_done, i - 1)
                act.activation(pt[:, u, :], pt_ps[:, :], ACT.Copy).then_inc(pt_ready, 1)

            if first:
                act.wait_ge(w_in, WEIGHTS)
                over_steps(act, NT, (2, exponentials), (0, spread_keys), (2, evacuate_turned))
            else:
                over_steps(act, NT, (3, evacuate_turned), (0, evacuate_queries), (2, exponentials))


def latent_weights(nc, io):
    with phase(nc, "latents") as (sb, ps, sem, sems, pair, open_block):
        R = io["latent"]
        scale = R ** -0.5
        basis, core, core_t = sb("basis", [R, D]), sb("core", [R, R]), sb("core_t", [R, R])
        heads = sb("heads", [R, H, R])
        mean = sb("mean", [R, R])
        w = sb("w", [P, H * R])
        w_ps = ps("w_ps", [P, H * R])
        loaded, step, product_done, w_ready, stored = sems("loaded", "step", "product_done", "w_ready", "stored")
        block = open_block()
        STEPS = 6

        @block.sync
        def _(sp):
            sp.dma_start(basis[:, :], io["L1_attn_basis_w"][:, :]).then_inc(loaded, 16)
            sp.dma_start(core[:, :], io["L1_attn_core"][:, :]).then_inc(loaded, 16)
            sp.dma_start(core_t[:, :], io["core_T"][:, :]).then_inc(loaded, 16)
            sp.dma_start(heads[:, :, :], io["L1_attn_head_residual"].rearrange("h r s -> r h s")).then_inc(loaded, 16)
            sp.wait_ge(w_ready, 1)
            sp.dma_start(io["lat_w"][:, :], w[:, :]).then_inc(stored, 16)
            sp.wait_ge(stored, 16)

        @block.vector
        def _(dve):
            count = [0]

            def then(instruction):
                count[0] += 1
                instruction.then_inc(step, 1)
                dve.wait_ge(step, count[0])

            dve.wait_ge(loaded, 64)
            then(dve.tensor_reduce(mean[:, :], heads[:, :, :].rearrange("r h s -> r s h"), axis=AX.X, op=ALU.add))
            then(dve.tensor_tensor(core[:, :], core[:, :], core_t[:, :], ALU.add))
            then(dve.tensor_scalar(core[:, :], core[:, :], 0.5, None, ALU.mult))
            then(dve.tensor_tensor(core[:, :], core[:, :], mean[:, :], ALU.subtract))
            then(dve.scalar_tensor_tensor(out=heads[:, :, :], in0=core[:, None, :].broadcast_to([R, H, R]),
                                          scalar=1.0 / H, in1=heads[:, :, :], op0=ALU.mult, op1=ALU.add))
            then(dve.tensor_scalar(heads[:, :, :], heads[:, :, :], scale, None, ALU.mult))
            assert count[0] == STEPS
            dve.wait_ge(product_done, 1)
            dve.tensor_copy(w[:, :], w_ps[:, :]).then_inc(w_ready, 1)

        @block.tensor
        def _(pe):
            pe.wait_ge(step, STEPS)
            for half in range(2):
                last = pe.matmul(w_ps[:, half * ST:(half + 1) * ST], basis[:, :], heads[:, half * 8:half * 8 + 8, :],
                                 start=True, stop=True)
            last.then_inc(product_done, 1)


def close_attention(nc, io, layer):
    with phase(nc, f"close{layer}") as (sb, ps, sem, sems, pair, open_block):
        ident, w = sb("ident", [P, P]), sb("w", [P, D])
        bv, bv_wide, brow, bo = sb("bv", [P, 1]), sb("bv_wide", [P, P]), sb("brow", [P, D]), sb("bo", [P, D])
        ao, rows, x1, out = (sb(n, [P, 2, JT, D]) for n in ("ao", "rows", "x1", "out"))
        aoT = sb("aoT", [P, 2, ST])
        t_ps, y_ps, r_ps = (ps(n, [P, 2, ST]) for n in ("t_ps", "y_ps", "r_ps"))
        b_ps = ps("b_ps", [P, D])
        ctxT, square, r = (sb(n, [P, 2, ST]) for n in ("ctxT", "square", "r"))
        decay = sb("decay", [P, ST])
        xn = sb("xn", [P, 2, JT, D])
        set_up, measure, invert, apply = layer_norm(sb, sems, "ln")
        ao_in, rows_in, ctx_in, stored = (pair(n) for n in ("ao_in", "rows_in", "ctx_in", "stored"))
        w_in, wide_ready, brow_done, brow_ready, t_done, t_ready, y_done, x1_ready, squared, r_ready, r_done, xn_ready, \
            multiplied, out_ready, biased, apart_sp = sems(
                "w_in", "wide_ready", "brow_done", "brow_ready", "t_done", "t_ready", "y_done", "x1_ready", "squared",
                "r_ready", "r_done", "xn_ready", "multiplied", "out_ready", "biased", "apart_sp")
        block = open_block()
        if layer == 0:
            source, target = io["x"], io["x2"]
            weights = ((w, io["L0_attn_Wo"]), (bv, io["L0_attn_bv"]), (bo, io["L0_attn_bo"].partition_broadcast(P)),
                       (ident, io["ident"]), (decay, io["decay"]))
        else:
            source, target = io["x3"], io["x4"]
            weights = ((w, io["L1_attn_o_wT"]), (bv, io["L1_attn_v_b"]), (bo, io["L1_attn_o_b"].partition_broadcast(P)),
                       (ident, io["ident"]))
        WEIGHTS = 16 * len(weights)
        final, final_ready = (out, out_ready) if layer == 0 else (x1, x1_ready)

        @block.sync
        def _(sp):
            for dst, src in weights:
                sp.dma_start(dst[:, :], src if dst is bo else src[:, :]).then_inc(w_in, 16)

            def load(i, u, n):
                if layer == 0:
                    wait(sp, squared, i - 1)
                    apart(sp, apart_sp)
                    sp.dma_start(ctxT[:, u, :], io["ctxT"][:, bass.ds(i * ST, ST)]).then_inc(ctx_in[u], 16)
                wait(sp, t_done, i - 1)
                sp.dma_start(ao[:, u], rows_of(io["AO"], i, ST)).then_inc(ao_in[u], 16)
                wait(sp, x1_ready, i - 1)
                sp.dma_start(rows[:, u], rows_of(source, i, ST)).then_inc(rows_in[u], 16)

            def store(i, u, n):
                sp.wait_ge(final_ready, i + 1)
                sp.dma_start(rows_of(target, i, ST), final[:, u]).then_inc(stored[u], 16)

            over_steps(sp, NS, (0, load), (2, store))
            for u in range(2):
                sp.wait_ge(stored[u], 16 * (NS // 2))

        @block.gpsimd
        def _(pool):
            if layer == 0:
                set_up(pool)

            def add_bias(i, u, n):
                pool.wait_ge(rows_in[u], n * 16 + 16)
                pool.wait_ge(brow_ready, 1)
                pool.tensor_tensor(rows[:, u], rows[:, u], brow[:, None, :].broadcast_to([P, JT, D]),
                                   ALU.add).then_inc(biased, 1)

            if layer == 0:
                over_steps(pool, NS, (0, add_bias), (1, lambda i, u, n: invert(pool, i)))
            else:
                over_steps(pool, NS, (0, add_bias))

        @block.vector
        def _(dve):
            dve.wait_ge(w_in, WEIGHTS)
            dve.tensor_copy(bv_wide[:, :], bv[:, 0:1].broadcast_to([P, P])).then_inc(wide_ready, 1)
            dve.wait_ge(brow_done, 1)
            dve.tensor_tensor(brow[:, :], b_ps[:, :], bo[:, :], ALU.add).then_inc(brow_ready, 1)

            def running(i, u, n):
                dve.wait_ge(squared, i + 1)
                wait(dve, r_done, i - 1)
                dve.tensor_tensor_scan(r[:, u, :], decay[:, :], square[:, u, :], 0.0, ALU.mult, ALU.add).then_inc(r_ready, 1)

            def residual(i, u, n):
                dve.wait_ge(y_done, i + 1)
                dve.wait_ge(biased, i + 1)
                if layer == 1:
                    wait(dve, stored[u], n * 16)
                dve.tensor_tensor(x1[:, u], y_ps[:, u, :].rearrange("p (j d) -> p j d", d=D), rows[:, u],
                                  ALU.add).then_inc(x1_ready, 1)

            def measure_x1(i, u, n):
                dve.wait_ge(x1_ready, i + 1)
                measure(dve, x1[:, u], i)

            def cross(i, u, n):
                apply(dve, xn[:, u], x1[:, u], i, xn_ready)
                dve.wait_ge(xn_ready, i + 1)
                dve.wait_ge(r_done, i + 1)
                wait(dve, stored[u], n * 16)
                dve.tensor_tensor(xn[:, u], r_ps[:, u, :].rearrange("p (j d) -> p j d", d=D), xn[:, u],
                                  ALU.mult).then_inc(multiplied, 1)
                dve.wait_ge(multiplied, i + 1)
                dve.tensor_tensor(out[:, u], x1[:, u], xn[:, u], ALU.add).then_inc(out_ready, 1)

            if layer == 0:
                over_steps(dve, NS, (1, residual), (1, measure_x1), (0, running), (1, cross))
            else:
                over_steps(dve, NS, (0, residual))

        @block.tensor
        def _(pe):
            pe.wait_ge(wide_ready, 1)
            pe.matmul(b_ps[:, :], bv_wide[:, :], w[:, :], start=True, stop=True).then_inc(brow_done, 1)

            def turn(i, u, n):
                pe.wait_ge(ao_in[u], n * 16 + 16)
                wait(pe, t_ready, i - 1)
                for j in range(JT):
                    last = pe.transpose(t_ps[:, u, j * P:(j + 1) * P], ao[:, u, j, :], ident[:, :])
                last.then_inc(t_done, 1)
                if layer == 0:
                    pe.wait_ge(r_ready, i + 1)
                    wait(pe, multiplied, i - 1)
                    for j in range(JT):
                        last = pe.transpose(r_ps[:, u, j * P:(j + 1) * P], r[:, u, j * P:(j + 1) * P], ident[:, :])
                    last.then_inc(r_done, 1)

            def product(i, u, n):
                pe.wait_ge(t_ready, i + 1)
                wait(pe, x1_ready, i - 1)
                for j in range(JT):
                    last = pe.matmul(y_ps[:, u, j * P:(j + 1) * P], aoT[:, u, j * P:(j + 1) * P], w[:, :],
                                     start=True, stop=True)
                last.then_inc(y_done, 1)

            over_steps(pe, NS, (1, product), (0, turn))

        @block.scalar
        def _(act):
            def evacuate(i, u, n):
                act.wait_ge(t_done, i + 1)
                wait(act, y_done, i - 1)
                act.activation(aoT[:, u, :], t_ps[:, u, :], ACT.Copy).then_inc(t_ready, 1)

            def square_context(i, u, n):
                act.wait_ge(ctx_in[u], n * 16 + 16)
                wait(act, r_ready, i - 1)
                act.activation(square[:, u, :], ctxT[:, u, :], ACT.Square).then_inc(squared, 1)

            if layer == 0:
                over_steps(act, NS, (0, square_context), (0, evacuate))
            else:
                over_steps(act, NS, (0, evacuate))


def chain_of(eng, sem, steps, alone):
    at = [0, 0]

    def start(i, done=0):
        at[:] = [done, i * steps]

    def then(instruction, before=False):
        at[0] += 1
        assert at[0] <= steps
        instruction.then_inc(sem, 1)
        eng.wait_ge(sem, at[1] + at[0])
        if before:
            apart(eng, alone)

    return start, then


def moe(nc, io, layer):
    with phase(nc, f"moe{layer}") as (sb, ps, sem, sems, pair, open_block):
        E = 8
        EX = E + 1 if layer == 0 else E
        Y = EX + 1 if layer == 0 else E
        C = 1 if layer == 0 else 2
        R = 3 if layer == 0 else 4
        LATER = 3 if layer == 0 else 2
        LIMIT, ALPHA = 7.0, 1.702
        ident = sb("ident", [P, P])
        gate = sb("gate", [P, E])
        up = sb("up", [P, EX, 4, P])
        down = sb("down", [P, EX, C, D])
        not_first = sb("not_first", [P, JT * E])
        if layer == 0:
            gate_b, up_b, down_b = sb("gate_b", [P, E]), sb("up_b", [P, EX, 4]), sb("down_b", [P, D])
            weights = ((ident[:, :], io["ident"][:, :]), (gate[:, :], io["gate0_T"][:, :]),
                       (down[:, :, 0, :], io["down0"][:, :, :]), (not_first[:, :], io["not_first"][:, :]),
                       (gate_b[:, :], io["gate0_b"].partition_broadcast(P)), (up_b[:, :, :], io["up0_b"][:, :, :]),
                       (down_b[0:EX, :], io["down0_b"][:, :]))
            source, target = io["x2"], io["x3"]
        else:
            weights = ((ident[:, :], io["ident"][:, :]), (gate[:, :], io["gate1_T"][:, :]),
                       (down[:, :, :, :], io["down1"][:, :, :, :]), (not_first[:, :], io["not_first"][:, :]))
            source, target = io["x6"], io["out"]
        WEIGHTS = 16 * len(weights)
        GROUPS = [range(at, min(at + 3, EX)) for at in range(0, EX, 3)]
        rows, xn, acc = (sb(n, [P, 2, JT, D]) for n in ("rows", "xn", "acc"))
        xnT = sb("xnT", [P, 2, ST])
        xnT_high, xnT_low = (sb(n, [P, 2, ST], F32R) for n in ("xnT_high", "xnT_low"))
        up_high, up_low = (sb(n, [P, EX, 4, P], F32R) for n in ("up_high", "up_low"))
        mx, total, share, above_n = (sb(n, [P, JT]) for n in ("mx", "total", "share", "above_n"))
        both = sb("both", [P, JT, 1])
        shifted, ex, score, biased, best, above, level, rank, picked = (
            sb(n, [P, JT, E]) for n in ("shifted", "ex", "score", "biased", "best", "above", "level", "rank", "picked"))
        cw = sb("cw", [P, 2, JT, P])
        cwT = sb("cwT", [P, ST])
        first = sb("first", [P, R, 2, ST])
        prod = sb("prod", [P, R, 2, ST])
        tanh, gated = sb("tanh", [P, R, ST]), sb("gated", [P, R, ST])
        hidden = sb("hidden", [P, R, C, ST])
        t_ps, c_ps = ps("t_ps", [P, ST]), ps("c_ps", [P, ST])
        h_ps, y_ps = ps("h_ps", [P, 4, ST]), ps("y_ps", [P, 2, ST])
        set_up, measure, invert, apply = layer_norm(sb, sems, "ln")
        x_in, acc_in, stored = pair("x_in"), pair("acc_in"), pair("stored")
        w_in, cw_set, xn_ready, t_done, t_ready, logits_done, route, exped, h_done, first_ready, product_ready, \
            gate_clamped, tanh_ready, linear_clamped, linear_ready, gated_ready, hidden_ready, y_done, added, c_done, \
            c_ready, cw_ready, apart_pool, apart_dve, high_ready, low_ready, up_high_ready, up_low_ready = sems(
                "w_in", "cw_set", "xn_ready", "t_done", "t_ready", "logits_done", "route", "exped", "h_done",
                "first_ready", "product_ready", "gate_clamped", "tanh_ready", "linear_clamped", "linear_ready",
                "gated_ready", "hidden_ready", "y_done", "added", "c_done", "c_ready", "cw_ready",
                "apart_pool", "apart_dve", "high_ready", "low_ready", "up_high_ready", "up_low_ready")
        up_in = [sem(f"up_in{g}") for g in range(len(GROUPS))]
        block = open_block()
        ROUTE = 12 if layer == 0 else 10
        EXP_INPUT = 2 if layer == 0 else 4
        LOGITS_READ = 2 if layer == 0 else 1
        wide = lambda t: t[:, :, None].broadcast_to([P, JT, E])

        def across(e):
            made = [(1, EX - 1)] if e == 0 else [(0, e - 1)]
            out = [(0, e - LATER)] if e >= LATER else [(1, EX - LATER + e)]
            if e == LATER - 1:
                out += [(1, y) for y in range(EX, Y)]
            return made, out

        def earlier(i, back):
            return not (back and isinstance(i, int) and i == 0)

        def part_rows(eng, i, u):
            eng.wait_ge(high_ready, i + 1)
            if layer == 0:
                apart(eng, apart_pool)
            eng.wait_ge(t_ready, i + 1)
            if layer == 0:
                apart(eng, apart_pool)
            wait(eng, h_done, (i - 1) * EX * 4)
            eng.tensor_tensor(xnT_low[:, u, :], xnT[:, u, :], xnT_high[:, u, :].bitcast(F32), ALU.subtract)\
                .then_inc(low_ready, 1)

        def part_of(body, experts):
            return lambda i, u, n: [body(i, u, n, e) for e in experts]

        @block.sync
        def _(sp):
            def load(i, u, n):
                wait(sp, xn_ready, i - 1)
                sp.dma_start(rows[:, u], rows_of(source, i, ST)).then_inc(x_in[u], 16)
                if isinstance(i, int) and i == 0:
                    for dst, src in weights:
                        sp.dma_start(dst, src).then_inc(w_in, 16)

            def load_residual(i, u, n):
                wait(sp, stored[u], n * 16)
                sp.dma_start(acc[:, u], rows_of(source, i, ST)).then_inc(acc_in[u], 16)

            def store(i, u, n):
                sp.wait_ge(added, i * Y + Y)
                sp.dma_start(rows_of(target, i, ST), acc[:, u]).then_inc(stored[u], 16)

            def load_up(i, u, n):
                if isinstance(i, int) and i == 0:
                    for group, arrived in zip(GROUPS, up_in):
                        at = slice(group[0], group[-1] + 1)
                        sp.dma_start(up[:, at, :, :], io[f"up{layer}"][:, at, :, :]).then_inc(arrived, 16)

            over_steps(sp, NS, (0, load), (0, load_up), (3, store), (1, load_residual))
            for u in range(2):
                sp.wait_ge(stored[u], 16 * (NS // 2))

        @block.gpsimd
        def _(pool):
            pool.memset(cw[:, :, :, :], 0.0).then_inc(cw_set, 1)
            pool.wait_ge(cw_set, 1)
            pool.memset(cw[:, :, :, E:E + 1], 1.0).then_inc(cw_set, 1)
            set_up(pool)

            def multiply(i, e):
                m = i * EX + e
                pool.wait_ge(gated_ready, m + 1)
                apart(pool, apart_pool)
                pool.wait_ge(linear_ready, m + 1)
                apart(pool, apart_pool)
                wait(pool, y_done, i * Y + e - R + 1 if e >= R else (i - 1) * Y + EX + e - R + 1)
                apart(pool, apart_pool)
                pool.tensor_tensor(hidden[:, e % R, 0, :], gated[:, e % R, :], prod[:, e % R, 1, :], ALU.mult)\
                    .then_inc(hidden_ready, 1)

            def body(i, u, n, e):
                m = i * EX + e
                linear = prod[:, e % R, 1, :]
                pool.wait_ge(product_ready, 2 * m + 2)
                apart(pool, apart_pool)
                pool.tensor_scalar(linear, linear, LIMIT, -LIMIT, ALU.min, ALU.max).then_inc(linear_clamped, 1)
                for back, x in across(e)[0]:
                    if earlier(i, back):
                        multiply(i - back, x)

            def invert_root(i, u, n):
                invert(pool, i)

            if layer == 0:
                over_steps(pool, NS, (2, part_of(body, range(0, 2))), (0, invert_root),
                           (2, part_of(body, range(2, 4))), (1, lambda i, u, n: part_rows(pool, i, u)),
                           (2, part_of(body, range(4, EX))))
                multiply(NS - 1, EX - 1)
            else:
                over_steps(pool, NS, (0, invert_root))

        @block.tensor
        def _(pe):
            def turn(i, u, n):
                pe.wait_ge(xn_ready, i + 1)
                wait(pe, route, (i - 1) * ROUTE + LOGITS_READ)
                for j in range(JT):
                    last = pe.transpose(t_ps[:, j * P:(j + 1) * P], xn[:, u, j, :], ident[:, :])
                last.then_inc(t_done, 1)

            def gate_logits(i, u, n):
                pe.wait_ge(t_ready, i + 1)
                for j in range(JT):
                    last = pe.matmul(t_ps[:, j * E:(j + 1) * E], xnT[:, u, j * P:(j + 1) * P], gate[:, :],
                                     start=True, stop=True)
                last.then_inc(logits_done, 1)

            def outputs(i, u, e):
                m = i * EX + e
                wait(pe, added, i * Y + e - 1)
                if e == EX:
                    pe.wait_ge(c_ready, i + 1)
                else:
                    pe.wait_ge(hidden_ready, m + 1)
                for j in range(JT):
                    at = slice(j * P, (j + 1) * P)
                    if e == EX:
                        last = pe.matmul(y_ps[:, e % 2, at], cwT[0:EX, at], down_b[0:EX, :], start=True, stop=True)
                    else:
                        for c in range(C):
                            last = pe.matmul(y_ps[:, e % 2, at], hidden[:, e % R, c, at], down[:, e, c, :],
                                             start=(c == 0), stop=(c == C - 1))
                last.then_inc(y_done, 1)

            def body(i, u, n, e):
                m = i * EX + e
                if e == 0:
                    pe.wait_ge(low_ready, i + 1)
                if isinstance(i, int) and i == 0:
                    for g, group in enumerate(GROUPS):
                        if e == group[0]:
                            pe.wait_ge(up_high_ready, g + 1)
                            pe.wait_ge(up_low_ready, g + 1)
                for bank in range(4):
                    if bank % 2 == 0:
                        wait(pe, first_ready, 2 * m + bank // 2 - 1)
                        wait(pe, product_ready, 2 * m + bank // 2 - 1)
                    product_of_parts(pe, h_ps[:, bank, :], (up_high[:, e, bank, :], up_low[:, e, bank, :]),
                                     (xnT_high[:, u, :], xnT_low[:, u, :])).then_inc(h_done, 1)
                for back, y in across(e)[1]:
                    if earlier(i, back):
                        outputs(i - back, (u - back) % 2, y)
                if e == 4 and layer == 0:
                    pe.wait_ge(cw_ready, i + 1)
                    wait(pe, c_ready, i)
                    for j in range(JT):
                        last = pe.transpose(c_ps[:, j * P:(j + 1) * P], cw[:, u, j, :], ident[:, :])
                    last.then_inc(c_done, 1)

            pe.wait_ge(w_in, WEIGHTS)
            over_steps(pe, NS, (2, part_of(body, range(0, 2))), (1, turn), (2, part_of(body, range(2, 4))), (1, gate_logits),
                       (2, part_of(body, range(4, EX))))
            for y in range(EX - LATER, Y):
                outputs(NS - 1, (NS - 1) % 2, y)

        @block.scalar
        def _(act):
            def front(i, u, n):
                act.wait_ge(t_done, i + 1)
                wait(act, h_done, (i - 1) * EX * 4)
                act.activation(xnT_high[:, u, :], t_ps[:, :], ACT.Copy).then_inc(high_ready, 1)
                act.activation(xnT[:, u, :], t_ps[:, :], ACT.Copy).then_inc(t_ready, 1)

            def exponentials(i, u, n):
                act.wait_ge(route, i * ROUTE + EXP_INPUT)
                if layer == 0:
                    act.activation(ex[:, :, :], shifted[:, :, :], ACT.Exp).then_inc(exped, 1)
                else:
                    act.activation(ex[:, :, :], shifted[:, :, :], ACT.Tanh, scale=0.5).then_inc(exped, 1)

            def shift_linear(i, e):
                act.wait_ge(linear_clamped, i * EX + e + 1)
                act.activation(prod[:, e % R, 1, :], prod[:, e % R, 1, :], ACT.Copy, bias=0.5, scale=0.5)\
                    .then_inc(linear_ready, 1)

            def body(i, u, n, e):
                m = i * EX + e
                for half in range(2):
                    act.wait_ge(h_done, 4 * m + 2 * half + 1)
                    wait(act, product_ready, 2 * (m - R) + half + 1)
                    if layer == 0:
                        act.activation(first[:, e % R, half, :], h_ps[:, 2 * half, :], ACT.Identity,
                                       bias=up_b[:, e, 2 * half:2 * half + 1]).then_inc(first_ready, 1)
                    else:
                        act.activation(first[:, e % R, half, :], h_ps[:, 2 * half, :], ACT.Silu).then_inc(first_ready, 1)
                if layer == 0:
                    for back, x in across(e)[0]:
                        if earlier(i, back):
                            shift_linear(i - back, x)
                    act.wait_ge(gate_clamped, m + 1)
                    wait(act, gated_ready, m - R + 1)
                    act.activation(tanh[:, e % R, :], prod[:, e % R, 0, :], ACT.Tanh, scale=ALPHA / 2).then_inc(tanh_ready, 1)
                if e == 4 and layer == 0:
                    act.wait_ge(c_done, i + 1)
                    wait(act, y_done, i * Y)
                    act.activation(cwT[:, :], c_ps[:, :], ACT.Copy).then_inc(c_ready, 1)

            act.wait_ge(w_in, WEIGHTS)
            def part_up(i, u, n):
                if isinstance(i, int) and i == 0:
                    for group, arrived in zip(GROUPS, up_in):
                        at = slice(group[0], group[-1] + 1)
                        act.wait_ge(arrived, 16)
                        act.activation(up_high[:, at, :, :].rearrange("p e b f -> p (e b f)"),
                                       up[:, at, :, :].rearrange("p e b f -> p (e b f)"), ACT.Copy).then_inc(up_high_ready, 1)

            over_steps(act, NS, (2, part_of(body, range(0, 2))), (1, front), (2, part_of(body, range(2, 5))), (1, exponentials),
                       (2, part_of(body, range(5, EX))), (1, part_up))
            if layer == 0:
                shift_linear(NS - 1, EX - 1)

        @block.vector
        def _(dve):
            start_chain, then = chain_of(dve, route, ROUTE, apart_dve)

            def measure_rows(i, u, n):
                dve.wait_ge(x_in[u], n * 16 + 16)
                measure(dve, rows[:, u], i)

            def normalise(i, u, n):
                wait(dve, t_done, i - 1)
                apply(dve, xn[:, u], rows[:, u], i, xn_ready)

            def scores(i, u, n):
                start_chain(i)
                logits = t_ps[:, 0:JT * E].rearrange("p (j e) -> p j e", e=E)
                dve.wait_ge(logits_done, i + 1)
                if layer == 0:
                    then(dve.tensor_reduce(mx[:, :], logits, axis=AX.X, op=ALU.max))
                    then(dve.tensor_tensor(shifted[:, :, :], logits, wide(mx), ALU.subtract))
                else:
                    then(dve.tensor_copy(biased[:, :, :], logits), before=True)
                    for j in range(JT):
                        last = dve.max(best[:, j, :], biased[:, j, :])
                    then(last)
                    then(dve.tensor_tensor(both[:, :, :], best[:, :, 0:1], best[:, :, 1:2], ALU.add))
                    then(dve.scalar_tensor_tensor(out=shifted[:, :, :], in0=biased[:, :, :], scalar=2.0,
                                                  in1=both[:, :, :].broadcast_to([P, JT, E]), op0=ALU.mult, op1=ALU.subtract))

            def compare(i, u, n):
                start_chain(i, EXP_INPUT)
                dve.wait_ge(exped, i + 1)
                if layer == 0:
                    then(dve.tensor_reduce(total[:, :], ex[:, :, :], axis=AX.X, op=ALU.add))
                    then(dve.reciprocal(share[:, :], total[:, :]))
                    then(dve.tensor_tensor(score[:, :, :], ex[:, :, :], wide(share), ALU.mult))
                    then(dve.tensor_tensor(biased[:, :, :], score[:, :, :], gate_b[:, None, :].broadcast_to([P, JT, E]),
                                           ALU.add), before=True)
                    for j in range(JT):
                        last = dve.max(best[:, j, :], biased[:, j, :])
                    then(last)
                second = best[:, :, 1:2].broadcast_to([P, JT, E])
                dve.tensor_tensor(above[:, :, :], biased[:, :, :], second, ALU.is_gt)
                then(dve.tensor_tensor(level[:, :, :], biased[:, :, :], second, ALU.is_equal))

            def pick(i, u, n):
                start_chain(i, ROUTE - (4 if layer == 0 else 5))
                dve.tensor_reduce(above_n[:, :], above[:, :, :], axis=AX.X, op=ALU.add)
                then(dve.tensor_tensor_scan(rank[:, :, :].rearrange("p j e -> p (j e)"), not_first[:, :],
                                            level[:, :, :].rearrange("p j e -> p (j e)"), 0.0, ALU.mult, ALU.add))
                then(dve.tensor_tensor(rank[:, :, :], rank[:, :, :], wide(above_n), ALU.add))
                then(dve.scalar_tensor_tensor(out=level[:, :, :], in0=rank[:, :, :], scalar=2.0, in1=level[:, :, :],
                                              op0=ALU.is_le, op1=ALU.mult))
                then(dve.tensor_tensor(picked[:, :, :], above[:, :, :], level[:, :, :], ALU.add))
                dve.wait_ge(cw_set, 2)
                if layer == 0:
                    dve.tensor_tensor(cw[:, u, :, 0:E], picked[:, :, :], score[:, :, :], ALU.mult).then_inc(cw_ready, 1)
                else:
                    then(dve.scalar_tensor_tensor(out=ex[:, :, :], in0=ex[:, :, :], scalar=1.0, in1=picked[:, :, :],
                                                  op0=ALU.add, op1=ALU.mult))
                    dve.tensor_scalar(cw[:, u, :, 0:E], ex[:, :, :], 0.5, None, ALU.mult).then_inc(cw_ready, 1)

            def clamp_gate(i, e):
                m = i * EX + e
                dve.wait_ge(product_ready, 2 * m + 1)
                dve.tensor_scalar(prod[:, e % R, 0, :], prod[:, e % R, 0, :], LIMIT, None, ALU.min).then_inc(gate_clamped, 1)

            def gate(i, e):
                m = i * EX + e
                dve.wait_ge(tanh_ready, m + 1)
                wait(dve, hidden_ready, m - R + 1)
                dve.scalar_tensor_tensor(out=gated[:, e % R, :], in0=tanh[:, e % R, :], scalar=1.0, in1=prod[:, e % R, 0, :],
                                         op0=ALU.add, op1=ALU.mult).then_inc(gated_ready, 1)

            def products(i, u, e):
                m = i * EX + e
                for half in range(2):
                    if half == 1 and layer == 0:
                        clamp_gate(i, e)
                        for back, x in across(e)[0]:
                            if earlier(i, back):
                                gate(i - back, x)
                    dve.wait_ge(first_ready, 2 * m + half + 1)
                    dve.wait_ge(h_done, 4 * m + 2 * half + 2)
                    if layer == 0:
                        wait(dve, hidden_ready, m - R + 1)
                        dve.scalar_tensor_tensor(
                            out=prod[:, e % R, half, :], in0=h_ps[:, 2 * half + 1, :], scalar=up_b[:, e, 2 * half + 1:2 * half + 2],
                            in1=first[:, e % R, half, :], op0=ALU.add, op1=ALU.mult).then_inc(product_ready, 1)
                    else:
                        wait(dve, y_done, m - R + 1)
                        dve.tensor_tensor(hidden[:, e % R, half, :], h_ps[:, 2 * half + 1, :], first[:, e % R, half, :],
                                          ALU.mult).then_inc(product_ready, 1)
                if layer == 1:
                    dve.wait_ge(product_ready, 2 * m + 2)
                    dve.sem_inc(hidden_ready, 1)

            def add(i, u, e, n=NS // 2 - 1):
                dve.wait_ge(y_done, i * Y + e + 1)
                if e == 0:
                    dve.wait_ge(acc_in[u], n * 16 + 16)
                    dve.wait_ge(cw_ready, i + 1)
                else:
                    dve.wait_ge(added, i * Y + e)
                if e == EX:
                    dve.tensor_tensor(acc[:, u], y_ps[:, e % 2, :].rearrange("p (j d) -> p j d", d=D), acc[:, u],
                                      ALU.add).then_inc(added, 1)
                    return
                for j in range(JT):
                    last = dve.scalar_tensor_tensor(
                        out=acc[:, u, j, :], in0=y_ps[:, e % 2, j * P:(j + 1) * P], scalar=cw[:, u, j, e:e + 1],
                        in1=acc[:, u, j, :], op0=ALU.mult, op1=ALU.add)
                last.then_inc(added, 1)

            def body(i, u, n, e):
                products(i, u, e)
                for back, y in across(e)[1]:
                    if earlier(i, back):
                        add(i - back, (u - back) % 2, y, n)

            dve.wait_ge(w_in, WEIGHTS)

            def part_up(i, u, n):
                if isinstance(i, int) and i == 0:
                    for g, group in enumerate(GROUPS):
                        at = slice(group[0], group[-1] + 1)
                        dve.wait_ge(up_high_ready, g + 1)
                        dve.tensor_tensor(up_low[:, at, :, :], up[:, at, :, :], up_high[:, at, :, :].bitcast(F32), ALU.subtract)\
                            .then_inc(up_low_ready, 1)

            low_parts = ((1, lambda i, u, n: part_rows(dve, i, u)),) if layer == 1 else ()
            over_steps(dve, NS, (2, part_of(body, range(0, 2))), (0, measure_rows), (2, part_of(body, range(2, 4))), (0, normalise),
                       *low_parts, (2, part_of(body, range(4, 5))), (1, scores), (2, part_of(body, range(5, 6))), (1, compare),
                       (2, part_of(body, range(6, 7))), (1, pick), (2, part_of(body, range(7, EX))), (1, part_up))
            if layer == 0:
                gate(NS - 1, EX - 1)
            for y in range(EX - LATER, Y):
                add(NS - 1, (NS - 1) % 2, y)


def context_and_gated(nc, io):
    with phase(nc, "gated") as (sb, ps, sem, sems, pair, open_block):
        C, KV = 4, 64
        ident = sb("ident", [P, P])
        gain, offset, cgain, coffset = (sb(n, [P, 1]) for n in ("gain", "offset", "cgain", "coffset"))
        wkv, w1, w2 = sb("wkv", [P, 2 * KV]), sb("w1", [P, 2 * C * P]), sb("w2", [P, C, D])
        rows, ctx, xn, xn2, cn, out = (sb(n, [P, 2, JT, D]) for n in ("rows", "ctx", "xn", "xn2", "cn", "out"))
        xnT, cnT = sb("xnT", [P, 2, ST]), sb("cnT", [P, 2, ST])
        xnT_high, xnT_low = (sb(n, [P, 2, ST], F32R) for n in ("xnT_high", "xnT_low"))
        w1_high, w1_low = (sb(n, [P, 2 * C * P], F32R) for n in ("w1_high", "w1_low"))
        key, value = sb("key", [KV, 2, ST]), sb("value", [P, 2, JT, KV])
        silu, hidden = sb("silu", [P, 2, ST]), sb("hidden", [P, C, ST])
        t_ps, c_ps, k_ps = (ps(n, [P, ST]) for n in ("t_ps", "c_ps", "k_ps"))
        v_ps = c_ps
        h_ps = ps("h_ps", [P, 2, 2, ST])
        y_ps = ps("y_ps", [P, ST])
        norm, norm2, cnorm = (layer_norm(sb, sems, n) for n in ("ln", "ln2", "cln"))
        x_in, ctx_in, out_in, xnT_stored, kv_stored, out_stored = (
            pair(n) for n in ("x_in", "ctx_in", "out_in", "xnT_stored", "kv_stored", "out_stored"))
        w_in, xn_ready, xn2_ready, cn_ready, t_done, t_ready, c_done, c_ready, k_done, k_ready, v_done, v_ready, \
            h_done, silu_ready, hidden_ready, y_done, out_ready, w1_parted, high_ready, low_ready, apart_sp = sems(
                "w_in", "xn_ready", "xn2_ready", "cn_ready", "t_done", "t_ready", "c_done", "c_ready", "k_done",
                "k_ready", "v_done", "v_ready", "h_done", "silu_ready", "hidden_ready", "y_done", "out_ready", "w1_parted",
                "high_ready", "low_ready", "apart_sp")
        block = open_block()
        weights = ((ident[:, :], io["ident"][:, :]), (gain[:, :], io["L1_xattn_ln_g"][:, :]), (offset[:, :], io["L1_xattn_ln_b"][:, :]),
                   (cgain[:, :], io["L1_xattn_cln_g"][:, :]), (coffset[:, :], io["L1_xattn_cln_b"][:, :]),
                   (wkv[:, :], io["xkv"][:, :]), (w1[:, :], io["xw1"][:, :]), (w2[:, :, :], io["xw2"][:, :, :]))
        WEIGHTS = 16 * len(weights)

        @block.sync
        def _(sp):
            def load(i, u, n):
                wait(sp, xn_ready, i - 1)
                sp.dma_start(rows[:, u], rows_of(io["x4"], i, ST)).then_inc(x_in[u], 16)
                wait(sp, cn_ready, i - 1)
                sp.dma_start(ctx[:, u], rows_of(io["ctx"], i, ST)).then_inc(ctx_in[u], 16)
                if isinstance(i, int) and i == 0:
                    for dst, src in weights:
                        sp.dma_start(dst, src).then_inc(w_in, 16)

            def store(i, u, n):
                at = bass.ds(i * ST, ST)
                sp.wait_ge(t_ready, i + 1)
                apart(sp, apart_sp)
                sp.dma_start(io["xnT"][:, at], xnT[:, u, :]).then_inc(xnT_stored[u], 16)
                sp.wait_ge(k_ready, i + 1)
                sp.dma_start(io["kT"][:, at], key[:, u, :]).then_inc(kv_stored[u], 16)
                sp.wait_ge(v_ready, i + 1)
                sp.dma_start(rows_of(io["v"], i, ST), value[:, u]).then_inc(kv_stored[u], 16)

            def store_rows(i, u, n):
                sp.wait_ge(out_ready, i + 1)
                sp.dma_start(rows_of(io["x5"], i, ST), out[:, u]).then_inc(out_stored[u], 16)

            def load_residual(i, u, n):
                wait(sp, out_stored[u], n * 16)
                sp.dma_start(out[:, u], rows_of(io["x4"], i, ST)).then_inc(out_in[u], 16)

            over_steps(sp, NS, (0, load), (3, store_rows), (2, store), (1, load_residual))
            for u in range(2):
                sp.wait_ge(out_stored[u], 16 * (NS // 2))
                sp.wait_ge(xnT_stored[u], 16 * (NS // 2))
                sp.wait_ge(kv_stored[u], 32 * (NS // 2))

        @block.gpsimd
        def _(pool):
            for each in (norm, norm2, cnorm):
                each[0](pool)
            over_steps(pool, NS, *((0, lambda i, u, n, each=each: each[2](pool, i)) for each in (norm, cnorm, norm2)))

        @block.vector
        def _(dve):
            def measure_rows(i, u, n):
                dve.wait_ge(x_in[u], n * 16 + 16)
                norm[1](dve, rows[:, u], i)

            def measure_context(i, u, n):
                dve.wait_ge(ctx_in[u], n * 16 + 16)
                cnorm[1](dve, ctx[:, u], i)

            def normalise(i, u, n):
                norm[3](dve, xn[:, u], rows[:, u], i, xn_ready)

            def measure_again(i, u, n):
                dve.wait_ge(xn_ready, i + 1)
                norm2[1](dve, xn[:, u], i)

            def normalise_context(i, u, n):
                wait(dve, c_done, i - 1)
                cnorm[3](dve, cn[:, u], ctx[:, u], i, cn_ready)

            def normalise_again(i, u, n):
                wait(dve, t_done, i - 1)
                norm2[3](dve, xn2[:, u], xn[:, u], i, xn2_ready)

            def part_rows(i, u, n):
                dve.wait_ge(high_ready, i + 1)
                wait(dve, h_done, (i - 1) * 2 * C)
                dve.tensor_tensor(xnT_low[:, u, :], xnT[:, u, :], xnT_high[:, u, :].bitcast(F32), ALU.subtract)\
                    .then_inc(low_ready, 1)

            def keys_and_values(i, u, n):
                dve.wait_ge(k_done, i + 1)
                wait(dve, kv_stored[u], n * 32)
                dve.tensor_copy(key[:, u, :], k_ps[0:KV, :]).then_inc(k_ready, 1)
                dve.wait_ge(v_done, i + 1)
                dve.tensor_copy(value[:, u], v_ps[:, 0:JT * KV].rearrange("p (j d) -> p j d", d=KV)).then_inc(v_ready, 1)

            def feed_forward(c):
                def stage(i, u, n):
                    dve.wait_ge(h_done, 2 * (i * C + c) + 2)
                    dve.wait_ge(silu_ready, i * C + c + 1)
                    if c == 0:
                        wait(dve, y_done, i)
                    dve.tensor_tensor(hidden[:, c, :], silu[:, c % 2, :], h_ps[:, c % 2, 1, :], ALU.mult)\
                        .then_inc(hidden_ready, 1)
                return stage

            def add(i, u, n):
                dve.wait_ge(out_in[u], n * 16 + 16)
                dve.wait_ge(y_done, i + 1)
                dve.tensor_tensor(out[:, u], y_ps[:, :].rearrange("p (j d) -> p j d", d=D), out[:, u], ALU.add)\
                    .then_inc(out_ready, 1)

            def part_w1(i, u, n):
                if isinstance(i, int) and i == 0:
                    dve.wait_ge(w_in, WEIGHTS)
                    dve.tensor_copy(w1_high[:, :], w1[:, :]).then_inc(w1_parted, 1)
                    dve.wait_ge(w1_parted, 1)
                    dve.tensor_tensor(w1_low[:, :], w1[:, :], w1_high[:, :].bitcast(F32), ALU.subtract).then_inc(w1_parted, 1)

            over_steps(dve, NS, (0, measure_rows), (2, feed_forward(0)), (0, measure_context), (0, normalise),
                       (2, feed_forward(1)), (0, measure_again), (0, normalise_context), (2, feed_forward(2)), (1, part_rows),
                       (2, feed_forward(3)), (1, keys_and_values), (0, normalise_again), (2, add),
                       (0, part_w1))

        @block.tensor
        def _(pe):
            def turn(i, u, n):
                pe.wait_ge(cn_ready, i + 1)
                wait(pe, v_ready, i)
                for j in range(JT):
                    last = pe.transpose(c_ps[:, j * P:(j + 1) * P], cn[:, u, j, :], ident[:, :])
                last.then_inc(c_done, 1)
                pe.wait_ge(xn2_ready, i + 1)
                wait(pe, t_ready, i)
                for j in range(JT):
                    last = pe.transpose(t_ps[:, j * P:(j + 1) * P], xn2[:, u, j, :], ident[:, :])
                last.then_inc(t_done, 1)

            def keys_and_values(i, u, n):
                pe.wait_ge(c_ready, i + 1)
                wait(pe, k_ready, i)
                pe.matmul(k_ps[0:KV, :], wkv[:, 0:KV], cnT[:, u, :], start=True, stop=True).then_inc(k_done, 1)
                for j in range(JT):
                    last = pe.matmul(v_ps[:, j * KV:(j + 1) * KV], cnT[:, u, j * P:(j + 1) * P], wkv[:, KV:2 * KV],
                                     start=True, stop=True)
                last.then_inc(v_done, 1)

            def feed_forward(i, u, n):
                pe.wait_ge(w1_parted, 2)
                pe.wait_ge(low_ready, i + 1)
                for c in range(C):
                    wait(pe, silu_ready, i * C + c - 1)
                    wait(pe, hidden_ready, i * C + c - 1)
                    for part in range(2):
                        f = slice(((1 - part) * C + c) * P, ((1 - part) * C + c + 1) * P)
                        product_of_parts(pe, h_ps[:, c % 2, part, :], (w1_high[:, f], w1_low[:, f]),
                                         (xnT_high[:, u, :], xnT_low[:, u, :])).then_inc(h_done, 1)

            def down(i, u, n):
                pe.wait_ge(hidden_ready, i * C + C)
                wait(pe, out_ready, i)
                for j in range(JT):
                    at = slice(j * P, (j + 1) * P)
                    for c in range(C):
                        last = pe.matmul(y_ps[:, at], hidden[:, c, at], w2[:, c, :], start=(c == 0), stop=(c == C - 1))
                last.then_inc(y_done, 1)

            pe.wait_ge(w_in, WEIGHTS)
            over_steps(pe, NS, (1, turn), (2, feed_forward), (1, keys_and_values), (2, down))

        @block.scalar
        def _(act):
            def evacuate_context(i, u, n):
                act.wait_ge(c_done, i + 1)
                wait(act, v_done, i - 1)
                act.activation(cnT[:, u, :], c_ps[:, :], ACT.Identity, bias=coffset[:, 0:1], scale=cgain[:, 0:1])\
                    .then_inc(c_ready, 1)

            def evacuate_rows(i, u, n):
                act.wait_ge(t_done, i + 1)
                wait(act, low_ready, i - 1)
                wait(act, xnT_stored[u], n * 16)
                act.activation(xnT[:, u, :], t_ps[:, :], ACT.Identity, bias=offset[:, 0:1], scale=gain[:, 0:1])\
                    .then_inc(t_ready, 1)

                act.wait_ge(t_ready, i + 1)
                wait(act, h_done, (i - 1) * 2 * C)
                act.activation(xnT_high[:, u, :], xnT[:, u, :], ACT.Copy).then_inc(high_ready, 1)

            def gates(c):
                def stage(i, u, n):
                    act.wait_ge(h_done, 2 * (i * C + c) + 1)
                    wait(act, hidden_ready, i * C + c - 1)
                    act.activation(silu[:, c % 2, :], h_ps[:, c % 2, 0, :], ACT.Silu).then_inc(silu_ready, 1)
                return stage

            act.wait_ge(w_in, WEIGHTS)
            over_steps(act, NS, (1, evacuate_context), (2, gates(0)), (1, evacuate_rows), *((2, gates(c)) for c in range(1, C)))


def wide_attention(nc, io):
    with phase(nc, "wide") as (sb, ps, sem, sems, pair, open_block):
        HP, KV = H // 2, 64
        ident, wq, wo = sb("ident", [P, P]), sb("wq", [P, HP, P]), sb("wo", [P, HP, D])
        qin = sb("qin", [P, 2, TILE])
        kblock = sb("kblock", [P, 2, 2, TILE])
        vblock = sb("vblock", [P, 2, 2, 2, KV])
        mask = sb("mask", [P, 2, S])
        rows, fin = sb("rows", [P, 2, D]), sb("fin", [P, 2, D])
        qT, oT = sb("qT", [P, 2, HP, TILE]), sb("oT", [P, HP, 2, S])
        scored, e = (sb(n, [P, 2, HK]) for n in ("scored", "e"))
        pt = sb("pt", [P, 2, HP, TILE])
        shifted = sb("shifted", [P, 2, HK])
        top, total, inv = (sb(n, [P, 2, H]) for n in ("top", "total", "inv"))
        a_ps, s_ps, t_ps, o_ps = (ps(n, [P, HK]) for n in ("a_ps", "s_ps", "t_ps", "o_ps"))
        q_in, k_in, v_in, m_in, x_in, stored = (pair(x) for x in ("q_in", "k_in", "v_in", "m_in", "x_in", "stored"))
        w_in, cleared, q_done, q_ready, s_done, masked, topped, shifted_ready, e_ready, pt_done, pt_ready, o_done, summed, \
            inverted, share_ready, ot_ready, y_done, fin_ready = sems(
                "w_in", "cleared", "q_done", "q_ready", "s_done", "masked", "topped", "shifted_ready", "e_ready",
                "pt_done", "pt_ready", "o_done", "summed", "inverted", "share_ready", "ot_ready", "y_done",
                "fin_ready")
        block = open_block()
        scale = KV ** -0.5
        by_head = lambda t: t.rearrange("p (h k) -> p h k", k=S)
        wide = lambda t: t[:, :, None].broadcast_to([P, H, S])

        @block.sync
        def _(sp):
            sp.dma_start(ident[:, :], io["ident"][:, :]).then_inc(w_in, 16)
            sp.dma_start(wq[:, :, :], io["xq"][:, :, :]).then_inc(w_in, 16)
            sp.dma_start(wo[:, :, :], io["xout"][:, :, :]).then_inc(w_in, 16)
            sp.wait_ge(cleared, 1)

            def load_queries(i, u, n):
                wait(sp, q_done, i - 1)
                sp.dma_start(qin[:, u, :], io["xnT"][:, bass.ds(i * TILE, TILE)]).then_inc(q_in[u], 16)

            def load_keys(i, u, n):
                wait(sp, s_done, i - 1)
                for c in range(2):
                    sp.dma_start(kblock[c * S:(c + 1) * S, u, c, :], io["kT"][:, bass.ds(i * TILE, TILE)])\
                        .then_inc(k_in[u], 16)

            def load_mask(i, u, n):
                wait(sp, masked, i - 1)
                sp.dma_start(mask[:, u, :], io["mask"][bass.ds(i * TILE, TILE), :]).then_inc(m_in[u], 16)

            def load_values(i, u, n):
                wait(sp, o_done, i - 1)
                for c in range(2):
                    sp.dma_start(vblock[c * S:(c + 1) * S, u, :, c, :], io["v"][bass.ds(i * TILE, TILE), :]
                                 .rearrange("(b k) d -> k b d", b=2)).then_inc(v_in[u], 16)

            def load_residual(i, u, n):
                wait(sp, fin_ready, i - 1)
                sp.dma_start(rows[:, u, :], io["x5"][bass.ds(i * TILE, TILE), :]).then_inc(x_in[u], 16)

            def store(i, u, n):
                sp.wait_ge(fin_ready, i + 1)
                sp.dma_start(io["x6"][bass.ds(i * TILE, TILE), :], fin[:, u, :]).then_inc(stored[u], 16)

            over_steps(sp, NT, (0, load_queries), (1, load_keys), (1, load_mask), (2, load_values), (3, load_residual), (5, store))
            for u in range(2):
                sp.wait_ge(stored[u], 16 * (NT // 2))

        @block.gpsimd
        def _(pool):
            pool.memset(kblock[:, :, :, :], 0.0)
            pool.memset(vblock[:, :, :, :, :], 0.0).then_inc(cleared, 1)

            def shift(i, u, n):
                pool.wait_ge(topped, i + 1)
                wait(pool, e_ready, i - 1)
                pool.tensor_tensor(by_head(shifted[:, u, :]), by_head(scored[:, u, :]), wide(top[:, u, :]),
                                   ALU.subtract).then_inc(shifted_ready, 1)

            over_steps(pool, NT, (0, shift))

        @block.tensor
        def _(pe):
            def queries(i, u, n):
                pe.wait_ge(q_in[u], n * 16 + 16)
                wait(pe, q_ready, i)
                wait(pe, fin_ready, i - 4)
                for g in range(HP):
                    last = pe.matmul(a_ps[:, g * P:(g + 1) * P], wq[:, g, :], qin[:, u, :], start=True, stop=True)
                last.then_inc(q_done, 1)

            def scores(i, u, n):
                pe.wait_ge(q_ready, i + 1)
                pe.wait_ge(k_in[u], n * 32 + 32)
                wait(pe, masked, i)
                for g in range(HP):
                    for b in range(2):
                        last = pe.matmul(s_ps[b * S:(b + 1) * S, g * P:(g + 1) * P], qT[:, u, g, b * S:(b + 1) * S],
                                         kblock[:, u, :, b * S:(b + 1) * S], start=True, stop=True,
                                         tile_position=(0, b * S))
                last.then_inc(s_done, 1)

            def project(i, u, n):
                pe.wait_ge(ot_ready, i + 1)
                wait(pe, q_ready, at_most(i + 5, NT))
                wait(pe, fin_ready, i)
                for g in range(HP):
                    last = pe.matmul(a_ps[:, 0:D], oT[:, g, :, :].rearrange("p b s -> p (b s)"), wo[:, g, :], start=(g == 0), stop=(g == HP - 1))
                last.then_inc(y_done, 1)

            def weigh(i, u, n):
                pe.wait_ge(pt_ready, i + 1)
                pe.wait_ge(v_in[u], n * 32 + 32)
                wait(pe, ot_ready, i)
                for b in range(2):
                    last = pe.matmul(o_ps[:, b * ST:(b + 1) * ST], vblock[:, u, b, :, :].rearrange("p c d -> p (c d)"),
                                     pt[:, u, :, b * S:(b + 1) * S], start=True, stop=True)
                last.then_inc(o_done, 1)

            def turn_weights(i, u, n):
                pe.wait_ge(share_ready, i + 1)
                wait(pe, pt_ready, i)
                for g in range(HP):
                    last = pe.transpose(t_ps[:, g * P:(g + 1) * P], e[:, u, g * P:(g + 1) * P], ident[:, :])
                last.then_inc(pt_done, 1)

            pe.wait_ge(w_in, 48)
            over_steps(pe, NT, (0, queries), (3, turn_weights), (1, scores), (4, project), (3, weigh))

        @block.vector
        def _(dve):
            def soften(i, u, n):
                dve.wait_ge(s_done, i + 1)
                dve.wait_ge(m_in[u], n * 16 + 16)
                wait(dve, shifted_ready, i - 1)
                dve.tensor_tensor(by_head(scored[:, u, :]), by_head(s_ps[:, :]),
                                  mask[:, u, None, :].broadcast_to([P, H, S]), ALU.add).then_inc(masked, 1)
                dve.wait_ge(masked, i + 1)
                dve.tensor_reduce(top[:, u, :], by_head(scored[:, u, :]), axis=AX.X, op=ALU.max).then_inc(topped, 1)

            def normalise(i, u, n):
                dve.wait_ge(e_ready, i + 1)
                dve.tensor_reduce(total[:, u, :], by_head(e[:, u, :]), axis=AX.X, op=ALU.add).then_inc(summed, 1)
                dve.wait_ge(summed, i + 1)
                dve.reciprocal(inv[:, u, :], total[:, u, :]).then_inc(inverted, 1)
                dve.wait_ge(inverted, i + 1)
                dve.tensor_tensor(by_head(e[:, u, :]), by_head(e[:, u, :]), wide(inv[:, u, :]), ALU.mult)\
                    .then_inc(share_ready, 1)

            def residual(i, u, n):
                dve.wait_ge(y_done, i + 1)
                dve.wait_ge(x_in[u], n * 16 + 16)
                wait(dve, stored[u], n * 16)
                dve.tensor_tensor(fin[:, u, :], a_ps[:, 0:D], rows[:, u, :], ALU.add).then_inc(fin_ready, 1)

            over_steps(dve, NT, (2, normalise), (1, soften), (4, residual))

        @block.scalar
        def _(act):
            def evacuate_weights(i, u, n):
                act.wait_ge(pt_done, i + 1)
                wait(act, o_done, i - 1)
                act.activation(pt[:, u], t_ps[:, :].rearrange("p (g t) -> p g t", t=TILE), ACT.Copy).then_inc(pt_ready, 1)

            def evacuate_queries(i, u, n):
                act.wait_ge(q_done, i + 1)
                wait(act, s_done, i - 1)
                act.activation(qT[:, u], a_ps[:, :].rearrange("p (g t) -> p g t", t=TILE), ACT.Copy, scale=scale)\
                    .then_inc(q_ready, 1)

            def evacuate_outputs(i, u, n):
                act.wait_ge(o_done, i + 1)
                wait(act, y_done, i)
                act.activation(oT[:, :, :, :].rearrange("p g b s -> p b g s"), o_ps[:, :].rearrange("p (b g s) -> p b g s", b=2, s=S),
                               ACT.Copy).then_inc(ot_ready, 1)

            def exponentials(i, u, n):
                act.wait_ge(shifted_ready, i + 1)
                wait(act, pt_done, i - 1)
                act.activation(e[:, u, :], shifted[:, u, :], ACT.Exp).then_inc(e_ready, 1)

            over_steps(act, NT, (4, evacuate_outputs), (2, exponentials), (0, evacuate_queries), (3, evacuate_weights))


SCRATCH = {
    "QT": (D, TOK), "KT": (D, TOK), "V": (TOK, D), "AO": (TOK, D), "bias0": (P, HK), "xnT": (D, TOK),
    "latT": (64, TOK), "lat_w": (P, HK), "x2": (TOK, D), "x3": (TOK, D), "x4": (TOK, D), "x5": (TOK, D),
    "x6": (TOK, D), "kT": (64, TOK), "v": (TOK, 64),
}


def build(nc, io, upto=99):
    io["latent"] = 64
    phases = [lambda: tpms_bias(nc, io), lambda: latent_weights(nc, io), lambda: project(nc, io, 0),
              lambda: narrow_attention(nc, io, "attn0", True), lambda: close_attention(nc, io, 0),
              lambda: moe(nc, io, 0), lambda: project(nc, io, 1),
              lambda: narrow_attention(nc, io, "attn1", False), lambda: close_attention(nc, io, 1),
              lambda: context_and_gated(nc, io), lambda: wide_attention(nc, io), lambda: moe(nc, io, 1)]
    for part in phases[:upto]:
        part()


def constants():
    import numpy as np

    f = np.float32
    token = np.arange(TILE) % S
    pos = (np.arange(S, dtype=f) / f(S) * f(2.0 * math.pi)).astype(f)
    head = np.arange(P)[:, None] // HD == np.arange(H)[None, :]
    seen = token[:, None] >= np.arange(S)[None, :]
    decay = np.where(np.arange(ST) % S == 0, 0.0, 0.9).astype(f)
    first_expert = np.where(np.arange(JT * 8) % 8 == 0, 0.0, 1.0).astype(f)
    return {
        "ident": np.eye(P, dtype=f),
        "pos_q": pos[token][:, None],
        "pos_k": np.broadcast_to(pos, (P, S)),
        "pos_z": ((pos[token][:, None] + pos[None, :]) * f(0.5)).astype(f),
        "head_mask": head.astype(f),
        "copy_mask": (np.arange(P)[:, None] // S == np.arange(2)[None, :]).astype(f),
        "causal": np.tile(np.where(seen, 0.0, -1e30).astype(f), (1, H)),
        "decay": np.broadcast_to(decay, (P, ST)),
        "not_first": np.broadcast_to(first_expert, (P, JT * 8)),
    }


def layouts(x):
    import numpy as np

    col = lambda a: a.reshape(-1, 1)
    both = lambda routed, shared: np.concatenate([g(routed), g(shared)[None]], 0)
    w13 = lambda *n: both(*n).reshape(9, P, 2, D).transpose(3, 0, 2, 1)
    b13 = lambda *n: both(*n).reshape(9, P, 2).transpose(1, 0, 2)
    g = lambda n: x[n]
    return {
        "x": g("x").reshape(TOK, D),
        "ctx": g("ctx_1024").reshape(TOK, D),
        "ctxT": g("ctx_1024").reshape(TOK, D).T,
        "mask": g("mask_BxSxS2_ff0").reshape(TOK, S),
        **{n: g(n) for n in ("L0_attn_Wq", "L0_attn_Wk", "L0_attn_Wv", "L0_attn_Wo", "L0_attn_bo", "L0_attn_phase",
                             "L1_attn_basis_w", "L1_attn_core", "L1_attn_head_residual", "L1_attn_o_b")},
        **{n: col(g(n)) for n in ("L0_attn_bq", "L0_attn_bk", "L0_attn_bv", "L1_attn_v_b", "L1_xattn_ln_g",
                                  "L1_xattn_ln_b", "L1_xattn_cln_g", "L1_xattn_cln_b")},
        "L0_attn_threshold": g("L0_attn_threshold").reshape(1),
        "L0_attn_temperature": g("L0_attn_temperature").reshape(1),
        "basis_T": g("L1_attn_basis_w").T,
        "core_T": g("L1_attn_core").T,
        "L1_attn_v_wT": g("L1_attn_v_w").T,
        "L1_attn_o_wT": g("L1_attn_o_w").T,
        "gate0_T": g("L0_ffn_gate_w").T,
        "gate0_b": g("L0_ffn_gate_b"),
        "up0": np.stack([w13("L0_ffn_w1", "L0_ffn_sw1"), w13("L0_ffn_w3", "L0_ffn_sw3")], 3).reshape(D, 9, 4, P),
        "up0_b": np.stack([b13("L0_ffn_b1", "L0_ffn_sb1"), b13("L0_ffn_b3", "L0_ffn_sb3")], 3).reshape(P, 9, 4),
        "down0": both("L0_ffn_w2", "L0_ffn_sw2").transpose(2, 0, 1),
        "down0_b": both("L0_ffn_b2", "L0_ffn_sb2"),
        "xq": g("L1_xattn_Wq").reshape(D, 8, P),
        "xkv": g("L1_xattn_Wkv"),
        "xout": g("L1_xattn_Wout").reshape(8, P, D).transpose(1, 0, 2),
        "xw1": g("L1_xattn_W1"),
        "xw2": g("L1_xattn_W2").reshape(4, P, D).transpose(1, 0, 2),
        "gate1_T": g("L1_ffn_gate_w").T,
        "up1": g("L1_ffn_w12").reshape(8, 2, 2, P, D).transpose(4, 0, 2, 1, 3).reshape(D, 8, 4, P),
        "down1": g("L1_ffn_w3").reshape(8, D, 2, P).transpose(3, 0, 2, 1),
    }


def kernel(**inputs):
    import numpy as np
    import concourse.bacc as bacc
    from concourse.bass_utils import run_bass_kernel_spmd

    nc = bacc.Bacc("TRN2", target_bir_lowering=False, num_devices=1)
    arrays, io = {}, {}
    for name, a in {**constants(), **layouts({k: np.asarray(v) for k, v in inputs.items()})}.items():
        arrays[f"in_{name}"] = np.ascontiguousarray(a)
        dram = nc.dram_tensor(f"in_{name}", a.shape, mybir.dt.from_np(a.dtype), kind="ExternalInput").ap()
        io[name] = dram
    for name, shape in SCRATCH.items():
        io[name] = nc.dram_tensor(f"scratch_{name}", shape, F32, kind="Internal").ap()
    io["out"] = nc.dram_tensor("out", (TOK, D), F32, kind="ExternalOutput").ap()
    build(nc, io)
    result = run_bass_kernel_spmd(nc, [arrays], core_ids=[0])
    return result.results[0]["out"].reshape(B, S, D)
```

```python
import math
from contextlib import ExitStack, contextmanager, nullcontext

import concourse.bass as bass
from concourse import mybir

F32 = mybir.dt.float32
F32R = mybir.dt.float32r
ALU = mybir.AluOpType
ACT = mybir.ActivationFunctionType
AX = mybir.AxisListType

B, S, D = 128, 64, 128
TOK = B * S
P = 128
TILE = 2 * S
NT = TOK // TILE
ST = 512
NS = TOK // ST
JT = ST // TILE
H = 16
HD = D // H
HK = H * S
EPS = 1e-5


def wait(eng, sem, value):
    if not (isinstance(value, int) and value <= 0):
        eng.wait_ge(sem, value)


def at_most(value, limit):
    return min(value, limit) if isinstance(value, int) else value


def apart(eng, sem):
    eng.sem_inc(sem, 1)


def over_steps(eng, n, *stages, turns=2):
    deepest = max(lag for lag, _ in stages)
    first = -(-(deepest + 2) // turns) * turns

    def step(k):
        for lag, fn in stages:
            if 0 <= k - lag < n:
                fn(k - lag, (k - lag) % turns, (k - lag) // turns)

    for k in range(first):
        step(k)
    with eng.Fori(first // turns, n // turns) as j:
        for p in range(turns):
            for lag, fn in stages:
                fn(j * turns + (p - lag), (p - lag) % turns, j + (p - lag) // turns)
    for k in range(n, n + deepest):
        step(k)


def by_two(fn):
    return lambda i, u, n: fn(i, u % 2, n * 2 + u // 2)


def query_parts(sb, sems, xn_t, weights, wait_for_weights, q_in, q_done):
    xn_high, xn_low = (sb(n, [P, 2, 2 * TILE], F32R) for n in ("xn_high", "xn_low"))
    w_high, w_low = (sb(n, [P, H // 2, P], F32R) for n in ("w_high", "w_low"))
    wq_parted, high_ready, low_ready = sems("wq_parted", "xn_high_ready", "xn_low_ready")
    pairs = H // 4

    def set_up_high(act):
        wait_for_weights(act)
        act.activation(w_high[:, :, :], weights, ACT.Copy).then_inc(wq_parted, 1)

    def set_up_low(dve):
        dve.wait_ge(wq_parted, 1)
        dve.tensor_tensor(w_low[:, :, :], weights, w_high[:, :, :].bitcast(F32), ALU.subtract).then_inc(wq_parted, 1)

    def part_high(act):
        def stage(i, u, n):
            if u % 2 == 0:
                act.wait_ge(q_in[u // 2], n * 16 + 16)
                wait(act, q_done, 4 * n + u - 2)
                act.activation(xn_high[:, u // 2, :], xn_t[:, u // 2, :], ACT.Copy).then_inc(high_ready, 1)
        return stage

    def part_low(dve):
        def stage(i, u, n):
            if u % 2 == 0:
                dve.wait_ge(high_ready, 2 * n + u // 2 + 1)
                wait(dve, q_done, 4 * n + u - 2)
                dve.tensor_tensor(xn_low[:, u // 2, :], xn_t[:, u // 2, :], xn_high[:, u // 2, :].bitcast(F32),
                                  ALU.subtract).then_inc(low_ready, 1)
        return stage

    def products(pe, q_ps, u, n):
        pe.wait_ge(low_ready, 2 * n + u // 2 + 1)
        for g in range(pairs):
            at = (u % 2) * pairs + g
            last = product_of_parts(pe, q_ps[:, g * 2 * TILE:(g + 1) * 2 * TILE], (w_high[:, at, :], w_low[:, at, :]),
                                    (xn_high[:, u // 2, :], xn_low[:, u // 2, :]))
        last.then_inc(q_done, 1)

    return set_up_high, set_up_low, part_high, part_low, products, wq_parted, low_ready


def rows_of(dram, i, size):
    return dram[bass.ds(i * size, size), :].rearrange("(j p) d -> p j d", p=P)


def product_of_parts(pe, out, weights, moving):
    (w_high, w_low), (m_high, m_low) = weights, moving
    pe.matmul(out, w_high, m_high, start=True, stop=False)
    pe.matmul(out, w_high, m_low, start=False, stop=False)
    return pe.matmul(out, w_low, m_high, start=False, stop=True)


@contextmanager
def joint_block(nc):
    taken, blocks = [], []
    with ExitStack() as ctx:
        def open_block():
            if not blocks:
                blocks.append(ctx.enter_context(nc.Block()))
            return blocks[0]

        yield ctx, taken, open_block
    nc.clear_and_free_semaphores(taken)
    nc.all_engine_barrier()


@contextmanager
def phase(nc, name, joint=None):
    with nullcontext(joint) if joint else joint_block(nc) as (ctx, taken, open_block):
        def sem(part):
            taken.append(nc.alloc_semaphore(name=f"{name}_{part}"))
            return taken[-1]

        def sb(part, shape, dtype=F32):
            return ctx.enter_context(nc.sbuf_tensor(f"{name}_{part}", shape, dtype))

        def ps(part, shape):
            return ctx.enter_context(nc.psum_tensor(f"{name}_{part}", shape, F32))

        def sems(*parts):
            return [sem(part) for part in parts]

        def pair(part):
            return [sem(f"{part}{u}") for u in range(2)]

        yield sb, ps, sem, sems, pair, open_block


def layer_norm(sb, sems, name, n=JT):
    stats, moments = sb(f"{name}_stats", [P, n, 6]), sb(f"{name}_moments", [P, n, 2])
    var_eps, rstd, power = (sb(f"{name}_{x}", [P, n]) for x in ("var_eps", "rstd", "power"))
    stats_done, moments_done, eps_added, rstd_done, power_set, apart_dve, apart_pool = sems(*(
        f"{name}_{x}" for x in ("stats_done", "moments_done", "eps_added", "rstd_done", "power_set", "apart_dve",
                                "apart_pool")))

    def set_up(pool):
        pool.memset(power[:, :], -0.5).then_inc(power_set, 1)
        pool.wait_ge(power_set, 1)

    def measure(dve, rows, i):
        for j in range(n):
            last = dve.bn_stats(stats[:, j, :], rows[:, j, :])
        last.then_inc(stats_done, 1)
        dve.wait_ge(stats_done, i + 1)
        apart(dve, apart_dve)
        for j in range(n):
            last = dve.bn_aggr(moments[:, j, :], stats[:, j, :])
        last.then_inc(moments_done, 1)

    def invert(pool, i):
        pool.wait_ge(moments_done, i + 1)
        apart(pool, apart_pool)
        pool.tensor_scalar(var_eps[:, :], moments[:, :, 1], EPS, 0.0, ALU.add, ALU.add).then_inc(eps_added, 1)
        pool.wait_ge(eps_added, i + 1)
        pool.tensor_tensor(rstd[:, :], var_eps[:, :], power[:, :], ALU.pow).then_inc(rstd_done, 1)

    def apply(dve, out, rows, i, done):
        dve.wait_ge(rstd_done, i + 1)
        for j in range(n):
            last = dve.tensor_scalar(out[:, j, :], rows[:, j, :], moments[:, j, 0:1], rstd[:, j:j + 1],
                                     ALU.subtract, ALU.mult)
        last.then_inc(done, 1)

    return set_up, measure, invert, apply


def project(nc, io, layer, joint=None):
    with phase(nc, f"project{layer}", joint) as (sb, ps, sem, sems, pair, open_block):
        R = D if layer == 0 else io["latent"]
        wq, wk, wv, ident = (sb(n, [P, w]) for n, w in (("wq", P), ("wk", R), ("wv", P), ("ident", P)))
        bq, bqs, bk = (sb(n, [P, 1]) for n in ("bq", "bqs", "bk"))
        rows = sb("rows", [P, 2, JT, D])
        xn = sb("xn", [P, 2, JT, D])
        xnT = sb("xnT", [P, 2, ST])
        q, k, v = (sb(n, [P, 2, ST]) for n in ("q", "k", "v"))
        tp, kp, vp = (ps(n, [P, 2, ST]) for n in ("tp", "kp", "vp"))
        if layer == 0:
            qp = ps("qp", [P, 2, ST])
        set_up, measure, invert, apply = layer_norm(sb, sems, "ln")
        x_in, across_stored, stored = pair("x_in"), pair("across_stored"), pair("stored")
        w_in, bias_scaled, xn_ready, t_done, xnT_ready, q_done, k_done, v_done, q_ready, k_ready, v_ready = sems(
            "w_in", "bias_scaled", "xn_ready", "t_done", "xnT_ready", "q_done", "k_done", "v_done",
            "q_ready", "k_ready", "v_ready")
        scale = HD ** -0.5
        block = open_block()
        if layer == 0:
            source, weights = io["x"], ((wq, io["L0_attn_Wq"]), (wk, io["L0_attn_Wk"]), (wv, io["L0_attn_Wv"]), (ident, io["ident"]),
                                     (bq, io["L0_attn_bq"]), (bk, io["L0_attn_bk"]))
            across, across_ready, ACROSS_LAG = q, q_ready, 3
        else:
            source, weights = io["x3"], ((wk, io["basis_T"]), (wv, io["L1_attn_v_wT"]), (ident, io["ident"]))
            across, across_ready, ACROSS_LAG = xnT, xnT_ready, 2
        WEIGHTS = len(weights) * 16

        @block.sync
        def _(sp):
            def load(i, u, n):
                wait(sp, xn_ready, i - 1)
                sp.dma_start(rows[:, u, :, :], rows_of(source, i, ST)).then_inc(x_in[u], 16)
                if isinstance(i, int) and i == 0:
                    for dst, src in weights:
                        sp.dma_start(dst[:, :], src[:, :]).then_inc(w_in, 16)

            def store_across(i, u, n):
                sp.wait_ge(across_ready, i + 1)
                sp.dma_start((io["QT"] if layer == 0 else io["xnT"])[:, bass.ds(i * ST, ST)],
                             across[:, u, :]).then_inc(across_stored[u], 16)

            def store(i, u, n):
                sp.wait_ge(k_ready, i + 1)
                sp.dma_start((io["KT"] if layer == 0 else io["latT"])[:, bass.ds(i * ST, ST)],
                             k[0:R, u, :]).then_inc(stored[u], 16)
                sp.wait_ge(v_ready, i + 1)
                sp.dma_start(rows_of(io["V"], i, ST), v[:, u, :].rearrange("p (j d) -> p j d", d=D)).then_inc(stored[u], 16)

            over_steps(sp, NS, (0, load), (ACROSS_LAG, store_across), (3, store))
            for u in range(2):
                sp.wait_ge(across_stored[u], 16 * (NS // 2))
                sp.wait_ge(stored[u], 32 * (NS // 2))

        @block.vector
        def _(dve):
            def measure_rows(i, u, n):
                dve.wait_ge(x_in[u], n * 16 + 16)
                measure(dve, rows[:, u], i)

            def normalise(i, u, n):
                wait(dve, t_done, i - 1)
                apply(dve, xn[:, u], rows[:, u], i, xn_ready)

            def evacuate(i, u, n):
                wait(dve, stored[u], n * 32)
                dve.wait_ge(k_done, i + 1)
                if layer == 0:
                    dve.tensor_scalar(k[:, u, :], kp[:, u, :], bk[:, 0:1], None, ALU.add).then_inc(k_ready, 1)
                else:
                    dve.tensor_copy(k[0:R, u, :], kp[0:R, u, :]).then_inc(k_ready, 1)
                dve.wait_ge(v_done, i + 1)
                dve.tensor_copy(v[:, u, :], vp[:, u, :]).then_inc(v_ready, 1)

            def scale_bias(i, u, n):
                if layer == 0 and isinstance(i, int) and i == 0:
                    dve.wait_ge(w_in, WEIGHTS)
                    dve.tensor_scalar(bqs[:, :], bq[:, :], scale, None, ALU.mult).then_inc(bias_scaled, 1)

            over_steps(dve, NS, (1, normalise), (0, measure_rows), (1, scale_bias), (2, evacuate))

        @block.gpsimd
        def _(pool):
            set_up(pool)
            over_steps(pool, NS, (0, lambda i, u, n: invert(pool, i)))

        @block.tensor
        def _(pe):
            def transpose(i, u, n):
                pe.wait_ge(xn_ready, i + 1)
                wait(pe, xnT_ready, i - 1)
                for j in range(JT):
                    last = pe.transpose(tp[:, u, j * P:(j + 1) * P], xn[:, u, j, :], ident[:, :])
                last.then_inc(t_done, 1)

            def products(i, u, n):
                pe.wait_ge(xnT_ready, i + 1)
                if layer == 0:
                    wait(pe, q_ready, i - 1)
                    pe.matmul(qp[:, u, :], wq[:, :], xnT[:, u, :], start=True, stop=True).then_inc(q_done, 1)
                wait(pe, k_ready, i - 1)
                pe.matmul(kp[0:R, u, :], wk[:, :], xnT[:, u, :], start=True, stop=True).then_inc(k_done, 1)
                wait(pe, v_ready, i - 1)
                for j in range(JT):
                    last = pe.matmul(vp[:, u, j * P:(j + 1) * P], xnT[:, u, j * P:(j + 1) * P], wv[:, :],
                                     start=True, stop=True)
                last.then_inc(v_done, 1)

            pe.wait_ge(w_in, WEIGHTS)
            over_steps(pe, NS, (2, products), (1, transpose))

        @block.scalar
        def _(act):
            def evacuate_transpose(i, u, n):
                act.wait_ge(t_done, i + 1)
                wait(act, v_done, i - 1)
                if layer == 1:
                    wait(act, across_stored[u], n * 16)
                act.activation(xnT[:, u, :], tp[:, u, :], ACT.Copy).then_inc(xnT_ready, 1)

            def evacuate_q(i, u, n):
                act.wait_ge(bias_scaled, 1)
                act.wait_ge(q_done, i + 1)
                wait(act, across_stored[u], n * 16)
                act.activation(q[:, u, :], qp[:, u, :], ACT.Identity, bias=bqs[:, 0:1], scale=scale).then_inc(q_ready, 1)

            if layer == 0:
                over_steps(act, NS, (2, evacuate_q), (1, evacuate_transpose))
            else:
                over_steps(act, NS, (0, evacuate_transpose))


def tpms_bias(nc, io, joint):
    with phase(nc, "tpms", joint) as (sb, ps, sem, sems, pair, open_block):
        offsets = sb("offsets", [P, H, 3])
        thr, tmp = sb("thr", [P, 1]), sb("tmp", [P, 1])
        inv, quarter = sb("inv", [P, 1]), sb("quarter", [P, 1])
        pos_q, pos_k, pos_z = sb("pos_q", [P, 1]), sb("pos_k", [P, S]), sb("pos_z", [P, S])
        pq = sb("pq", [P, 2, H])
        pk, pz = sb("pk", [P, 2, H, S]), sb("pz", [P, 2, H, S])
        turns_q, turns_k = sb("turns_q", [P, H]), sb("turns_k", [P, H, S])
        val, part = sb("val", [P, H, S]), sb("part", [P, H, S])
        in_done, step, absolutes, sines, stored = sems("in_done", "step", "absolutes", "sines", "stored")
        block = open_block()
        MAGIC = 1.5 * 2.0 ** 23
        TURN_HIGH = 6.28125
        TURN_LOW = 2 * math.pi - TURN_HIGH
        angles = (pq, pk, pz)
        STEPS = 26

        @block.sync
        def _(sp):
            for dst, src in ((offsets[:, :, :], io["L0_attn_phase"].partition_broadcast(P)),
                             (thr[:, :], io["L0_attn_threshold"].partition_broadcast(P)),
                             (tmp[:, :], io["L0_attn_temperature"].partition_broadcast(P)),
                             (pos_q[:, :], io["pos_q"][:, :]), (pos_k[:, :], io["pos_k"][:, :]), (pos_z[:, :], io["pos_z"][:, :])):
                sp.dma_start(dst, src).then_inc(in_done, 16)

        @block.vector
        def _(dve):
            count = [0]

            def then(instruction):
                count[0] += 1
                instruction.then_inc(step, 1)
                dve.wait_ge(step, count[0])

            dve.memset(quarter[:, :], math.pi / 2)
            dve.wait_ge(in_done, 6 * 16)
            heads = lambda t: t[:, None, :].broadcast_to([P, H, S])
            keys = lambda n: offsets[:, :, n:n + 1].broadcast_to([P, H, S])
            dve.tensor_scalar(pq[:, 0, :], offsets[:, :, 0], pos_q[:, 0:1], None, ALU.add)
            dve.tensor_tensor(pk[:, 0], keys(1), heads(pos_k), ALU.add)
            then(dve.tensor_tensor(pz[:, 0], keys(2), heads(pos_z), ALU.add))
            for a, t in ((pq[:, 0], turns_q), (pk[:, 0], turns_k), (pz[:, 0], turns_k)):
                then(dve.tensor_scalar(t[:], a, 1 / (2 * math.pi), MAGIC, ALU.mult, ALU.add))
                then(dve.tensor_scalar(t[:], t[:], MAGIC, None, ALU.subtract))
                then(dve.scalar_tensor_tensor(out=a, in0=t[:], scalar=-TURN_HIGH, in1=a, op0=ALU.mult, op1=ALU.add))
                then(dve.scalar_tensor_tensor(out=a, in0=t[:], scalar=-TURN_LOW, in1=a, op0=ALU.mult, op1=ALU.add))
                then(dve.tensor_scalar(a, a, math.pi, -math.pi, ALU.min, ALU.max))
            then(dve.tensor_scalar(inv[:, :], tmp[:, :], 1e-6, None, ALU.add))
            then(dve.reciprocal(inv[:, :], inv[:, :]))
            dve.wait_ge(sines, 1)
            query = lambda n: pq[:, n, :, None].broadcast_to([P, H, S])
            then(dve.tensor_tensor(val[:], query(0), pk[:, 1], ALU.mult))
            then(dve.tensor_tensor(part[:], pk[:, 0], pz[:, 1], ALU.mult))
            then(dve.tensor_tensor(val[:], val[:], part[:], ALU.add))
            then(dve.tensor_tensor(part[:], query(1), pz[:, 0], ALU.mult))
            then(dve.tensor_tensor(val[:], val[:], part[:], ALU.add))
            then(dve.tensor_scalar(val[:], val[:], thr[:, 0:1], None, ALU.subtract))
            dve.wait_ge(sines, 2)
            then(dve.tensor_scalar(val[:], val[:], 1e-6, None, ALU.add))
            dve.wait_ge(sines, 3)
            then(dve.tensor_scalar(val[:], val[:], 0.3, None, ALU.mult))
            assert count[0] == STEPS

        @block.scalar
        def _(act):
            for at, a in enumerate(angles):
                act.wait_ge(step, 6 + 5 * at)
                act.activation(a[:, 1], a[:, 0], ACT.Abs).then_inc(absolutes, 1)
                act.activation(a[:, 0], a[:, 0], ACT.Sin).then_inc(absolutes, 1)
                act.wait_ge(absolutes, 2 * at + 2)
                last = act.activation(a[:, 1], a[:, 1], ACT.Sin, bias=quarter[:, 0:1], scale=-1.0)
            last.then_inc(sines, 1)
            act.wait_ge(step, 24)
            act.activation(val[:], val[:], ACT.Sigmoid, scale=inv[:, 0:1]).then_inc(sines, 1)
            act.wait_ge(step, 25)
            act.activation(val[:], val[:], ACT.Ln).then_inc(sines, 1)
            act.wait_ge(step, STEPS)
            act.dma_start(io["bias0"][:, :], val[:, :, :].rearrange("p h s -> p (h s)")).then_inc(stored, 16)
            act.wait_ge(stored, 16)


def narrow_attention(nc, io, name, first):
    with phase(nc, name) as (sb, ps, sem, sems, pair, open_block):
        HP = H // 2
        W = HD + 1
        ident, bias = sb("ident", [P, P]), sb("bias", [P, HK])
        copy_mask = sb("copy_mask", [P, 2])
        vin = sb("vin", [P, 2, 2, D])
        vblock = sb("vblock", [P, 2, 2, HP, 2 * W])
        scored, e, pt = (sb(n, [P, 2, HK]) for n in ("scored", "e", "pt"))
        top, inv = sb("top", [P, 2, H]), sb("inv", [P, 2, H])
        out = sb("out", [P, 2, D])
        if first:
            qin, kin = sb("qin", [P, 2, TILE]), sb("kin", [P, 2, TILE])
            kblock = sb("kblock", [P, 2, H, TILE])
            head_mask = sb("head_mask", [P, H])
        else:
            kblock = sb("kblock", [P, 2, 2, TILE])
            lat_w = sb("lat_w", [P, HK])
            qin = sb("qin", [P, 2, 2 * TILE])
            qT = sb("qT", [P, 2, HP, 2 * TILE])
            q_ps = ps("q_ps", [P, HK])
        SB = 2 if first else 1
        s_ps, pt_ps = ps("s_ps", [P, SB, HK]), ps("pt_ps", [P, HK])
        o_ps = ps("o_ps", [P, ST])
        q_in, k_in, v_in, out_stored = (pair(x) for x in ("q_in", "k_in", "v_in", "out_stored"))
        w_in, cleared, keys_spread_pool, keys_spread_act, keys_spread_dve, vblock_ready, q_done, q_ready, s_done, biased, topped, shifted, e_ready, \
            pt_done, pt_ready, o_done, inverted, out_ready, apart_pool = sems(
                "w_in", "cleared", "keys_spread_pool", "keys_spread_act", "keys_spread_dve", "vblock_ready", "q_done", "q_ready", "s_done", "biased", "topped",
                "shifted", "e_ready", "pt_done", "pt_ready", "o_done", "inverted", "out_ready", "apart_pool")
        if not first:
            set_up_high, set_up_low, part_high, part_low, query_products, wq_parted, low_ready = query_parts(
                sb, sems, qin, lat_w[:, :].rearrange("p (g c) -> p g c", c=P), lambda act: act.wait_ge(w_in, 64), q_in, q_done)
        block = open_block()
        BY_POOL, BY_ACT, BY_DVE = range(0, 7), range(7, 15), range(15, H)
        WEIGHTS = 16 * 4

        def values(t):
            return o_ps[:, 0:HP * 2 * W].rearrange("p (h w) -> p h w", w=W)

        @block.sync
        def _(sp):
            sp.dma_start(ident[:, :], io["ident"][:, :]).then_inc(w_in, 16)
            sp.dma_start(copy_mask[:, :], io["copy_mask"][:, :]).then_inc(w_in, 16)
            sp.dma_start(bias[:, :], (io["bias0"] if first else io["causal"])[:, :]).then_inc(w_in, 16)
            if first:
                sp.dma_start(head_mask[:, :], io["head_mask"][:, :]).then_inc(w_in, 16)
            else:
                sp.dma_start(lat_w[:, :], io["lat_w"][:, :]).then_inc(w_in, 16)
            sp.wait_ge(cleared, 1)

            def load_queries(i, u, n):
                wait(sp, s_done, i - 1)
                sp.dma_start(qin[:, u, :], io["QT"][:, bass.ds(i * TILE, TILE)]).then_inc(q_in[u], 16)

            def load_pair(i, u, n):
                if u % 2 == 0:
                    wait(sp, low_ready, 2 * n + u // 2 - 1)
                    sp.dma_start(qin[:, u // 2, :], io["xnT"][:, bass.ds(i * TILE, 2 * TILE)]).then_inc(q_in[u // 2], 16)

            def load_keys(i, u, n):
                at = bass.ds(i * TILE, TILE)
                if first:
                    wait(sp, keys_spread_pool, i - 1)
                    wait(sp, keys_spread_act, i - 1)
                    wait(sp, keys_spread_dve, i - 1)
                    sp.dma_start(kin[:, u, :], io["KT"][:, at]).then_inc(k_in[u], 16)
                else:
                    wait(sp, s_done, i - 1)
                    for c in range(2):
                        sp.dma_start(kblock[c * S:(c + 1) * S, u, c, :], io["latT"][:, at]).then_inc(k_in[u], 16)

            def load_values(i, u, n):
                wait(sp, vblock_ready, i - 1)
                for c in range(2):
                    sp.dma_start(vin[c * S:(c + 1) * S, u], io["V"][bass.ds(i * TILE, TILE), :]
                                 .rearrange("(b k) d -> k b d", b=2)).then_inc(v_in[u], 16)

            def store(i, u, n):
                sp.wait_ge(out_ready, i + 1)
                sp.dma_start(io["AO"][bass.ds(i * TILE, TILE), :], out[:, u, :]).then_inc(out_stored[u], 16)

            if first:
                over_steps(sp, NT, (0, load_keys), (0, load_queries), (0, load_values), (4, store))
            else:
                over_steps(sp, NT, (0, load_pair), (2, by_two(load_keys)), (2, by_two(load_values)), (6, by_two(store)), turns=4)
            for u in range(2):
                sp.wait_ge(out_stored[u], 16 * (NT // 2))

        @block.gpsimd
        def _(pool):
            if not first:
                pool.memset(kblock[:, :, :, :], 0.0)
            pool.memset(vblock[:, :, :, :, :], 0.0).then_inc(cleared, 1)
            pool.wait_ge(cleared, 1)
            for c in range(2):
                last = pool.memset(vblock[c * S:(c + 1) * S, :, :, :, c * W + HD:c * W + W], 1.0)
            last.then_inc(cleared, 1)
            pool.wait_ge(w_in, WEIGHTS)

            pool.wait_ge(cleared, 2)

            def spread_keys(i, u, n):
                pool.wait_ge(k_in[u], n * 16 + 16)
                wait(pool, s_done, i - 1)
                apart(pool, apart_pool)
                for h in BY_POOL:
                    last = pool.tensor_scalar(kblock[:, u, h, :], kin[:, u, :], head_mask[:, h:h + 1], 0.0,
                                              ALU.mult, ALU.add)
                last.then_inc(keys_spread_pool, 1)

            def spread_values(i, u, n):
                pool.wait_ge(v_in[u], n * 32 + 32)
                wait(pool, o_done, i - 1)
                apart(pool, apart_pool)
                for b in range(2):
                    for c in range(2):
                        heads = vin[:, u, b, :].rearrange("p (g c d) -> p g c d", c=2, d=HD)[:, :, c, :]
                        last = pool.tensor_scalar(vblock[:, u, b, :, c * W:c * W + HD], heads, copy_mask[:, c:c + 1], 0.0,
                                                  ALU.mult, ALU.add)
                last.then_inc(vblock_ready, 1)

            if first:
                over_steps(pool, NT, (0, spread_keys), (1, spread_values))
            else:
                over_steps(pool, NT, (0, spread_values))

        @block.tensor
        def _(pe):
            def queries(i, u, n):
                wait(pe, q_ready, i)
                query_products(pe, q_ps, u, n)

            def scores_of_pair(i, u, n):
                v, u, n = u // 2, u % 2, 2 * n + u // 2
                pe.wait_ge(q_ready, 2 * n + 2)
                pe.wait_ge(k_in[u], n * 32 + 32)
                wait(pe, biased, i)
                for g in range(HP):
                    for b in range(2):
                        last = pe.matmul(
                            s_ps[b * S:(b + 1) * S, 0, g * P:(g + 1) * P],
                            qT[:, v, g, u * TILE + b * S:u * TILE + (b + 1) * S],
                            kblock[:, u, :, b * S:(b + 1) * S],
                            start=True, stop=True, tile_position=(0, b * S))
                last.then_inc(s_done, 1)

            def scores(i, u, n):
                pe.wait_ge(q_in[u], n * 16 + 16)
                pe.wait_ge(keys_spread_pool, i + 1)
                pe.wait_ge(keys_spread_act, i + 1)
                pe.wait_ge(keys_spread_dve, i + 1)
                wait(pe, biased, i - 1)
                for half in range(2):
                    for b in range(2):
                        last = pe.matmul(
                            s_ps[b * S:(b + 1) * S, u, half * ST:(half + 1) * ST],
                            qin[:, u, b * S:(b + 1) * S],
                            kblock[:, u, half * HP:(half + 1) * HP, b * S:(b + 1) * S],
                            start=True, stop=True, tile_position=(0, b * S))
                last.then_inc(s_done, 1)

            def weigh(i, u, n):
                pe.wait_ge(pt_ready, i + 1)
                pe.wait_ge(vblock_ready, i + 1)
                wait(pe, out_ready, i)
                for g in range(HP):
                    for b in range(2):
                        last = pe.matmul(
                            o_ps[b * S:(b + 1) * S, g * 2 * W:(g + 1) * 2 * W],
                            pt[:, u, g * P + b * S:g * P + (b + 1) * S],
                            vblock[:, u, b, g, :],
                            start=True, stop=True, tile_position=(0, b * S))
                last.then_inc(o_done, 1)

            def turn(i, u, n):
                pe.wait_ge(e_ready, i + 1)
                wait(pe, pt_ready, i)
                for g in range(HP):
                    last = pe.transpose(pt_ps[:, g * P:(g + 1) * P], e[:, u, g * P:(g + 1) * P], ident[:, :])
                last.then_inc(pt_done, 1)

            pe.wait_ge(w_in, WEIGHTS)
            pe.wait_ge(cleared, 2)
            if first:
                over_steps(pe, NT, (0, scores), (2, weigh), (1, turn))
            else:
                pe.wait_ge(wq_parted, 2)
                over_steps(pe, NT, (1, queries), (3, scores_of_pair), (5, by_two(weigh)), (4, by_two(turn)), turns=4)

        @block.vector
        def _(dve):
            def soften(i, u, n):
                dve.wait_ge(s_done, i + 1)
                wait(dve, e_ready, i - 1)
                dve.tensor_tensor(scored[:, u, :], s_ps[:, u % SB, :], bias[:, :], ALU.add).then_inc(biased, 1)
                dve.wait_ge(biased, i + 1)
                by_head = scored[:, u, :].rearrange("p (h k) -> p h k", k=S)
                dve.tensor_reduce(top[:, u, :], by_head, axis=AX.X, op=ALU.max).then_inc(topped, 1)
                dve.wait_ge(topped, i + 1)
                dve.tensor_tensor(by_head, by_head, top[:, u, :, None].broadcast_to([P, H, S]),
                                  ALU.subtract).then_inc(shifted, 1)

            def spread_keys(i, u, n):
                dve.wait_ge(k_in[u], n * 16 + 16)
                wait(dve, s_done, i - 1)
                for h in BY_DVE:
                    last = dve.tensor_scalar(kblock[:, u, h, :], kin[:, u, :], head_mask[:, h:h + 1], None, ALU.mult)
                last.then_inc(keys_spread_dve, 1)

            def normalise(i, u, n):
                dve.wait_ge(o_done, i + 1)
                wait(dve, out_stored[u], n * 16)
                dve.reciprocal(inv[:, u, :], values(o_ps)[:, :, HD]).then_inc(inverted, 1)
                dve.wait_ge(inverted, i + 1)
                dve.tensor_tensor(out[:, u, :].rearrange("p (h d) -> p h d", d=HD), values(o_ps)[:, :, 0:HD],
                                  inv[:, u, :, None].broadcast_to([P, H, HD]), ALU.mult).then_inc(out_ready, 1)

            dve.wait_ge(w_in, WEIGHTS)
            if first:
                over_steps(dve, NT, (0, spread_keys), (1, soften), (3, normalise))
            else:
                set_up_low(dve)
                over_steps(dve, NT, (0, part_low(dve)), (3, by_two(soften)), (5, by_two(normalise)), turns=4)

        @block.scalar
        def _(act):
            def spread_keys(i, u, n):
                act.wait_ge(k_in[u], n * 16 + 16)
                wait(act, s_done, i - 1)
                for h in BY_ACT:
                    last = act.activation(kblock[:, u, h, :], kin[:, u, :], ACT.Copy, scale=head_mask[:, h:h + 1])
                last.then_inc(keys_spread_act, 1)

            def evacuate_queries(i, u, n):
                act.wait_ge(q_done, i + 1)
                wait(act, s_done, 4 * n + 2 * (u // 2) - 2)
                half = slice((u % 2) * (HP // 2), (u % 2 + 1) * (HP // 2))
                act.activation(qT[:, u // 2, half, :], q_ps[:, :].rearrange("p (g t) -> p g t", t=2 * TILE), ACT.Copy)\
                    .then_inc(q_ready, 1)

            def exponentials(i, u, n):
                act.wait_ge(shifted, i + 1)
                wait(act, pt_done, i - 1)
                act.activation(e[:, u, :], scored[:, u, :], ACT.Exp).then_inc(e_ready, 1)

            def evacuate_turned(i, u, n):
                act.wait_ge(pt_done, i + 1)
                wait(act, o_done, i - 1)
                act.activation(pt[:, u, :], pt_ps[:, :], ACT.Copy).then_inc(pt_ready, 1)

            if first:
                act.wait_ge(w_in, WEIGHTS)
                over_steps(act, NT, (2, exponentials), (0, spread_keys), (2, evacuate_turned))
            else:
                set_up_high(act)
                over_steps(act, NT, (0, part_high(act)), (5, by_two(evacuate_turned)), (1, evacuate_queries),
                           (4, by_two(exponentials)), turns=4)


def latent_weights(nc, io, joint):
    with phase(nc, "latents", joint) as (sb, ps, sem, sems, pair, open_block):
        R = io["latent"]
        scale = R ** -0.5
        basis, core, core_t = sb("basis", [R, D]), sb("core", [R, R]), sb("core_t", [R, R])
        heads = sb("heads", [R, H, R])
        mean = sb("mean", [R, R])
        w = sb("w", [P, H * R])
        w_ps = ps("w_ps", [P, H * R])
        loaded, step, product_done, w_ready, stored = sems("loaded", "step", "product_done", "w_ready", "stored")
        block = open_block()
        STEPS = 6

        @block.sync
        def _(sp):
            sp.dma_start(basis[:, :], io["L1_attn_basis_w"][:, :]).then_inc(loaded, 16)
            sp.dma_start(core[:, :], io["L1_attn_core"][:, :]).then_inc(loaded, 16)
            sp.dma_start(core_t[:, :], io["core_T"][:, :]).then_inc(loaded, 16)
            sp.dma_start(heads[:, :, :], io["L1_attn_head_residual"].rearrange("h r s -> r h s")).then_inc(loaded, 16)

        @block.vector
        def _(dve):
            count = [0]

            def then(instruction):
                count[0] += 1
                instruction.then_inc(step, 1)
                dve.wait_ge(step, count[0])

            dve.wait_ge(loaded, 64)
            then(dve.tensor_reduce(mean[:, :], heads[:, :, :].rearrange("r h s -> r s h"), axis=AX.X, op=ALU.add))
            then(dve.tensor_tensor(core[:, :], core[:, :], core_t[:, :], ALU.add))
            then(dve.tensor_scalar(core[:, :], core[:, :], 0.5, None, ALU.mult))
            then(dve.tensor_tensor(core[:, :], core[:, :], mean[:, :], ALU.subtract))
            then(dve.scalar_tensor_tensor(out=heads[:, :, :], in0=core[:, None, :].broadcast_to([R, H, R]),
                                          scalar=1.0 / H, in1=heads[:, :, :], op0=ALU.mult, op1=ALU.add))
            then(dve.tensor_scalar(heads[:, :, :], heads[:, :, :], scale, None, ALU.mult))
            assert count[0] == STEPS
            dve.wait_ge(product_done, 1)
            dve.tensor_copy(w[:, :], w_ps[:, :]).then_inc(w_ready, 1)

        @block.tensor
        def _(pe):
            pe.wait_ge(step, STEPS)
            for half in range(2):
                last = pe.matmul(w_ps[:, half * ST:(half + 1) * ST], basis[:, :], heads[:, half * 8:half * 8 + 8, :],
                                 start=True, stop=True)
            last.then_inc(product_done, 1)

        @block.scalar
        def _(act):
            act.wait_ge(w_ready, 1)
            act.dma_start(io["lat_w"][:, :], w[:, :]).then_inc(stored, 16)
            act.wait_ge(stored, 16)


def close_attention(nc, io, layer):
    with phase(nc, f"close{layer}") as (sb, ps, sem, sems, pair, open_block):
        ident, w = sb("ident", [P, P]), sb("w", [P, D])
        bv, bv_wide, brow, bo = sb("bv", [P, 1]), sb("bv_wide", [P, P]), sb("brow", [P, D]), sb("bo", [P, D])
        ao, rows, x1, out = (sb(n, [P, 2, JT, D]) for n in ("ao", "rows", "x1", "out"))
        aoT = sb("aoT", [P, 2, ST])
        t_ps, y_ps, r_ps = (ps(n, [P, 2, ST]) for n in ("t_ps", "y_ps", "r_ps"))
        b_ps = ps("b_ps", [P, D])
        ctxT, square, r = (sb(n, [P, 2, ST]) for n in ("ctxT", "square", "r"))
        decay = sb("decay", [P, ST])
        xn = sb("xn", [P, 2, JT, D])
        set_up, measure, invert, apply = layer_norm(sb, sems, "ln")
        ao_in, rows_in, ctx_in, stored = (pair(n) for n in ("ao_in", "rows_in", "ctx_in", "stored"))
        w_in, wide_ready, brow_done, brow_ready, t_done, t_ready, y_done, x1_ready, squared, r_ready, r_done, xn_ready, \
            multiplied, out_ready, biased, apart_sp = sems(
                "w_in", "wide_ready", "brow_done", "brow_ready", "t_done", "t_ready", "y_done", "x1_ready", "squared",
                "r_ready", "r_done", "xn_ready", "multiplied", "out_ready", "biased", "apart_sp")
        block = open_block()
        if layer == 0:
            source, target = io["x"], io["x2"]
            weights = ((w, io["L0_attn_Wo"]), (bv, io["L0_attn_bv"]), (bo, io["L0_attn_bo"].partition_broadcast(P)),
                       (ident, io["ident"]), (decay, io["decay"]))
        else:
            source, target = io["x3"], io["x4"]
            weights = ((w, io["L1_attn_o_wT"]), (bv, io["L1_attn_v_b"]), (bo, io["L1_attn_o_b"].partition_broadcast(P)),
                       (ident, io["ident"]))
        WEIGHTS = 16 * len(weights)
        final, final_ready = (out, out_ready) if layer == 0 else (x1, x1_ready)

        @block.sync
        def _(sp):
            for dst, src in weights:
                sp.dma_start(dst[:, :], src if dst is bo else src[:, :]).then_inc(w_in, 16)

            def load(i, u, n):
                if layer == 0:
                    wait(sp, squared, i - 1)
                    apart(sp, apart_sp)
                    sp.dma_start(ctxT[:, u, :], io["ctxT"][:, bass.ds(i * ST, ST)]).then_inc(ctx_in[u], 16)
                wait(sp, t_done, i - 1)
                sp.dma_start(ao[:, u], rows_of(io["AO"], i, ST)).then_inc(ao_in[u], 16)
                wait(sp, x1_ready, i - 1)
                sp.dma_start(rows[:, u], rows_of(source, i, ST)).then_inc(rows_in[u], 16)

            def store(i, u, n):
                sp.wait_ge(final_ready, i + 1)
                sp.dma_start(rows_of(target, i, ST), final[:, u]).then_inc(stored[u], 16)

            over_steps(sp, NS, (0, load), (2, store))
            for u in range(2):
                sp.wait_ge(stored[u], 16 * (NS // 2))

        @block.gpsimd
        def _(pool):
            if layer == 0:
                set_up(pool)

            def add_bias(i, u, n):
                pool.wait_ge(rows_in[u], n * 16 + 16)
                pool.wait_ge(brow_ready, 1)
                pool.tensor_tensor(rows[:, u], rows[:, u], brow[:, None, :].broadcast_to([P, JT, D]),
                                   ALU.add).then_inc(biased, 1)

            if layer == 0:
                over_steps(pool, NS, (0, add_bias), (1, lambda i, u, n: invert(pool, i)))
            else:
                over_steps(pool, NS, (0, add_bias))

        @block.vector
        def _(dve):
            dve.wait_ge(w_in, WEIGHTS)
            dve.tensor_copy(bv_wide[:, :], bv[:, 0:1].broadcast_to([P, P])).then_inc(wide_ready, 1)
            dve.wait_ge(brow_done, 1)
            dve.tensor_tensor(brow[:, :], b_ps[:, :], bo[:, :], ALU.add).then_inc(brow_ready, 1)

            def running(i, u, n):
                dve.wait_ge(squared, i + 1)
                wait(dve, r_done, i - 1)
                dve.tensor_tensor_scan(r[:, u, :], decay[:, :], square[:, u, :], 0.0, ALU.mult, ALU.add).then_inc(r_ready, 1)

            def residual(i, u, n):
                dve.wait_ge(y_done, i + 1)
                dve.wait_ge(biased, i + 1)
                if layer == 1:
                    wait(dve, stored[u], n * 16)
                dve.tensor_tensor(x1[:, u], y_ps[:, u, :].rearrange("p (j d) -> p j d", d=D), rows[:, u],
                                  ALU.add).then_inc(x1_ready, 1)

            def measure_x1(i, u, n):
                dve.wait_ge(x1_ready, i + 1)
                measure(dve, x1[:, u], i)

            def cross(i, u, n):
                apply(dve, xn[:, u], x1[:, u], i, xn_ready)
                dve.wait_ge(xn_ready, i + 1)
                dve.wait_ge(r_done, i + 1)
                wait(dve, stored[u], n * 16)
                dve.tensor_tensor(xn[:, u], r_ps[:, u, :].rearrange("p (j d) -> p j d", d=D), xn[:, u],
                                  ALU.mult).then_inc(multiplied, 1)
                dve.wait_ge(multiplied, i + 1)
                dve.tensor_tensor(out[:, u], x1[:, u], xn[:, u], ALU.add).then_inc(out_ready, 1)

            if layer == 0:
                over_steps(dve, NS, (1, residual), (1, measure_x1), (0, running), (1, cross))
            else:
                over_steps(dve, NS, (0, residual))

        @block.tensor
        def _(pe):
            pe.wait_ge(wide_ready, 1)
            pe.matmul(b_ps[:, :], bv_wide[:, :], w[:, :], start=True, stop=True).then_inc(brow_done, 1)

            def turn(i, u, n):
                pe.wait_ge(ao_in[u], n * 16 + 16)
                wait(pe, t_ready, i - 1)
                for j in range(JT):
                    last = pe.transpose(t_ps[:, u, j * P:(j + 1) * P], ao[:, u, j, :], ident[:, :])
                last.then_inc(t_done, 1)
                if layer == 0:
                    pe.wait_ge(r_ready, i + 1)
                    wait(pe, multiplied, i - 1)
                    for j in range(JT):
                        last = pe.transpose(r_ps[:, u, j * P:(j + 1) * P], r[:, u, j * P:(j + 1) * P], ident[:, :])
                    last.then_inc(r_done, 1)

            def product(i, u, n):
                pe.wait_ge(t_ready, i + 1)
                wait(pe, x1_ready, i - 1)
                for j in range(JT):
                    last = pe.matmul(y_ps[:, u, j * P:(j + 1) * P], aoT[:, u, j * P:(j + 1) * P], w[:, :],
                                     start=True, stop=True)
                last.then_inc(y_done, 1)

            over_steps(pe, NS, (1, product), (0, turn))

        @block.scalar
        def _(act):
            def evacuate(i, u, n):
                act.wait_ge(t_done, i + 1)
                wait(act, y_done, i - 1)
                act.activation(aoT[:, u, :], t_ps[:, u, :], ACT.Copy).then_inc(t_ready, 1)

            def square_context(i, u, n):
                act.wait_ge(ctx_in[u], n * 16 + 16)
                wait(act, r_ready, i - 1)
                act.activation(square[:, u, :], ctxT[:, u, :], ACT.Square).then_inc(squared, 1)

            if layer == 0:
                over_steps(act, NS, (0, square_context), (0, evacuate))
            else:
                over_steps(act, NS, (0, evacuate))


def chain_of(eng, sem, steps, alone):
    at = [0, 0]

    def start(i, done=0):
        at[:] = [done, i * steps]

    def then(instruction, before=False):
        at[0] += 1
        assert at[0] <= steps
        instruction.then_inc(sem, 1)
        eng.wait_ge(sem, at[1] + at[0])
        if before:
            apart(eng, alone)

    return start, then


def moe(nc, io, layer):
    with phase(nc, f"moe{layer}") as (sb, ps, sem, sems, pair, open_block):
        E = 8
        EX = E + 1 if layer == 0 else E
        Y = EX + 1 if layer == 0 else E
        C = 1 if layer == 0 else 2
        R = 3 if layer == 0 else 4
        LATER = 3 if layer == 0 else 2
        ADD_LATER = LATER + 1 if layer == 0 else LATER
        LIMIT, ALPHA = 7.0, 1.702
        ident = sb("ident", [P, P])
        gate = sb("gate", [P, E])
        up = sb("up", [P, EX, 4, P])
        down = sb("down", [P, EX, C, D])
        not_first = sb("not_first", [P, JT * E])
        if layer == 0:
            gate_b, up_b, down_b = sb("gate_b", [P, E]), sb("up_b", [P, EX, 4]), sb("down_b", [P, D])
            weights = ((ident[:, :], io["ident"][:, :]), (gate[:, :], io["gate0_T"][:, :]),
                       (down[:, :, 0, :], io["down0"][:, :, :]), (not_first[:, :], io["not_first"][:, :]),
                       (gate_b[:, :], io["gate0_b"].partition_broadcast(P)), (up_b[:, :, :], io["up0_b"][:, :, :]),
                       (down_b[0:EX, :], io["down0_b"][:, :]))
            source, target = io["x2"], io["x3"]
        else:
            weights = ((ident[:, :], io["ident"][:, :]), (gate[:, :], io["gate1_T"][:, :]),
                       (down[:, :, :, :], io["down1"][:, :, :, :]), (not_first[:, :], io["not_first"][:, :]))
            source, target = io["x6"], io["out"]
        WEIGHTS = 16 * len(weights)
        GROUPS = [range(at, min(at + 3, EX)) for at in range(0, EX, 3)]
        rows, xn, acc = (sb(n, [P, 2, JT, D]) for n in ("rows", "xn", "acc"))
        xnT = sb("xnT", [P, 2, ST])
        xnT_high, xnT_low = (sb(n, [P, 2, ST], F32R) for n in ("xnT_high", "xnT_low"))
        up_high, up_low = (sb(n, [P, EX, 4, P], F32R) for n in ("up_high", "up_low"))
        mx, total, share, above_n = (sb(n, [P, JT]) for n in ("mx", "total", "share", "above_n"))
        both = sb("both", [P, JT, 1])
        shifted, ex, score, biased, best, above, level, rank, picked = (
            sb(n, [P, JT, E]) for n in ("shifted", "ex", "score", "biased", "best", "above", "level", "rank", "picked"))
        cw = sb("cw", [P, 2, JT, P])
        cwT = sb("cwT", [P, ST])
        first = sb("first", [P, R, 2, ST])
        prod = sb("prod", [P, R, 2, ST])
        tanh, gated = sb("tanh", [P, R, ST]), sb("gated", [P, R, ST])
        hidden = sb("hidden", [P, R, C, ST])
        W = Y // 2
        weighed = sb("weighed", [P, W, JT, D])
        t_ps, c_ps = ps("t_ps", [P, ST]), ps("c_ps", [P, ST])
        h_ps, y_ps = ps("h_ps", [P, 4, ST]), ps("y_ps", [P, 2, ST])
        set_up, measure, invert, apply = layer_norm(sb, sems, "ln")
        x_in, acc_in, stored = pair("x_in"), pair("acc_in"), pair("stored")
        w_in, cw_set, xn_ready, t_done, t_ready, logits_done, route, exped, h_done, first_ready, product_ready, \
            gate_clamped, tanh_ready, linear_clamped, linear_ready, gated_ready, hidden_ready, y_done, added, c_done, \
            c_ready, cw_ready, apart_pool, apart_dve, high_ready, low_ready, up_high_ready, up_low_ready, weighed_ready = sems(
                "w_in", "cw_set", "xn_ready", "t_done", "t_ready", "logits_done", "route", "exped", "h_done",
                "first_ready", "product_ready", "gate_clamped", "tanh_ready", "linear_clamped", "linear_ready",
                "gated_ready", "hidden_ready", "y_done", "added", "c_done", "c_ready", "cw_ready",
                "apart_pool", "apart_dve", "high_ready", "low_ready", "up_high_ready", "up_low_ready", "weighed_ready")
        up_in = [sem(f"up_in{g}") for g in range(len(GROUPS))]
        block = open_block()
        ROUTE = 12 if layer == 0 else 10
        EXP_INPUT = 2 if layer == 0 else 4
        LOGITS_READ = 2 if layer == 0 else 1
        wide = lambda t: t[:, :, None].broadcast_to([P, JT, E])

        def before(e):
            return (1, EX - 1) if e == 0 else (0, e - 1)

        def outputs_beside(e, later):
            out = [(0, e - later)] if e >= later else [(1, EX - later + e)]
            return out + ([(1, y) for y in range(EX, Y)] if e == later - 1 else [])

        def earlier(i, back):
            return not (back and isinstance(i, int) and i == 0)

        def part_rows(eng, i, u):
            eng.wait_ge(high_ready, i + 1)
            if layer == 0:
                apart(eng, apart_pool)
            eng.wait_ge(t_ready, i + 1)
            if layer == 0:
                apart(eng, apart_pool)
            wait(eng, h_done, (i - 1) * EX * 4)
            eng.tensor_tensor(xnT_low[:, u, :], xnT[:, u, :], xnT_high[:, u, :].bitcast(F32), ALU.subtract)\
                .then_inc(low_ready, 1)

        def part_of(body, experts):
            return lambda i, u, n: [body(i, u, n, e) for e in experts]

        @block.sync
        def _(sp):
            def load(i, u, n):
                wait(sp, xn_ready, i - 1)
                sp.dma_start(rows[:, u], rows_of(source, i, ST)).then_inc(x_in[u], 16)
                if isinstance(i, int) and i == 0:
                    for dst, src in weights:
                        sp.dma_start(dst, src).then_inc(w_in, 16)

            def load_residual(i, u, n):
                wait(sp, stored[u], n * 16)
                sp.dma_start(acc[:, u], rows_of(source, i, ST)).then_inc(acc_in[u], 16)

            def store(i, u, n):
                sp.wait_ge(added, i * Y + Y)
                sp.dma_start(rows_of(target, i, ST), acc[:, u]).then_inc(stored[u], 16)

            def load_up(i, u, n):
                if isinstance(i, int) and i == 0:
                    for group, arrived in zip(GROUPS, up_in):
                        at = slice(group[0], group[-1] + 1)
                        sp.dma_start(up[:, at, :, :], io[f"up{layer}"][:, at, :, :]).then_inc(arrived, 16)

            over_steps(sp, NS, (0, load), (0, load_up), (3, store), (1, load_residual))
            for u in range(2):
                sp.wait_ge(stored[u], 16 * (NS // 2))

        @block.gpsimd
        def _(pool):
            pool.memset(cw[:, :, :, :], 0.0).then_inc(cw_set, 1)
            pool.wait_ge(cw_set, 1)
            pool.memset(cw[:, :, :, E:E + 1], 1.0).then_inc(cw_set, 1)
            set_up(pool)

            def multiply(i, e):
                m = i * EX + e
                pool.wait_ge(gated_ready, m + 1)
                apart(pool, apart_pool)
                pool.wait_ge(linear_ready, m + 1)
                apart(pool, apart_pool)
                wait(pool, y_done, i * Y + e - R + 1 if e >= R else (i - 1) * Y + EX + e - R + 1)
                apart(pool, apart_pool)
                pool.tensor_tensor(hidden[:, e % R, 0, :], gated[:, e % R, :], prod[:, e % R, 1, :], ALU.mult)\
                    .then_inc(hidden_ready, 1)

            def body(i, u, n, e):
                m = i * EX + e
                linear = prod[:, e % R, 1, :]
                pool.wait_ge(product_ready, 2 * m + 2)
                apart(pool, apart_pool)
                pool.tensor_scalar(linear, linear, LIMIT, -LIMIT, ALU.min, ALU.max).then_inc(linear_clamped, 1)
                back, x = before(e)
                if earlier(i, back):
                    multiply(i - back, x)

            def invert_root(i, u, n):
                invert(pool, i)

            if layer == 0:
                over_steps(pool, NS, (2, part_of(body, range(0, 2))), (0, invert_root),
                           (2, part_of(body, range(2, 4))), (1, lambda i, u, n: part_rows(pool, i, u)),
                           (2, part_of(body, range(4, EX))))
                multiply(NS - 1, EX - 1)
            else:
                over_steps(pool, NS, (0, invert_root))

        @block.tensor
        def _(pe):
            def turn(i, u, n):
                pe.wait_ge(xn_ready, i + 1)
                wait(pe, route, (i - 1) * ROUTE + LOGITS_READ)
                for j in range(JT):
                    last = pe.transpose(t_ps[:, j * P:(j + 1) * P], xn[:, u, j, :], ident[:, :])
                last.then_inc(t_done, 1)

            def gate_logits(i, u, n):
                pe.wait_ge(t_ready, i + 1)
                for j in range(JT):
                    last = pe.matmul(t_ps[:, j * E:(j + 1) * E], xnT[:, u, j * P:(j + 1) * P], gate[:, :],
                                     start=True, stop=True)
                last.then_inc(logits_done, 1)

            def outputs(i, u, e):
                m = i * EX + e
                wait(pe, weighed_ready if layer == 0 else added, i * Y + e - 1)
                if e == EX:
                    pe.wait_ge(c_ready, i + 1)
                else:
                    pe.wait_ge(hidden_ready, m + 1)
                for j in range(JT):
                    at = slice(j * P, (j + 1) * P)
                    if e == EX:
                        last = pe.matmul(y_ps[:, e % 2, at], cwT[0:EX, at], down_b[0:EX, :], start=True, stop=True)
                    else:
                        for c in range(C):
                            last = pe.matmul(y_ps[:, e % 2, at], hidden[:, e % R, c, at], down[:, e, c, :],
                                             start=(c == 0), stop=(c == C - 1))
                last.then_inc(y_done, 1)

            def body(i, u, n, e):
                m = i * EX + e
                if e == 0:
                    pe.wait_ge(low_ready, i + 1)
                if isinstance(i, int) and i == 0:
                    for g, group in enumerate(GROUPS):
                        if e == group[0]:
                            pe.wait_ge(up_high_ready, g + 1)
                            pe.wait_ge(up_low_ready, g + 1)
                for bank in range(4):
                    if bank % 2 == 0:
                        wait(pe, first_ready, 2 * m + bank // 2 - 1)
                        wait(pe, product_ready, 2 * m + bank // 2 - 1)
                    product_of_parts(pe, h_ps[:, bank, :], (up_high[:, e, bank, :], up_low[:, e, bank, :]),
                                     (xnT_high[:, u, :], xnT_low[:, u, :])).then_inc(h_done, 1)
                for back, y in outputs_beside(e, LATER):
                    if earlier(i, back):
                        outputs(i - back, (u - back) % 2, y)
                if e == 4 and layer == 0:
                    pe.wait_ge(cw_ready, i + 1)
                    wait(pe, c_ready, i)
                    for j in range(JT):
                        last = pe.transpose(c_ps[:, j * P:(j + 1) * P], cw[:, u, j, :], ident[:, :])
                    last.then_inc(c_done, 1)

            pe.wait_ge(w_in, WEIGHTS)
            over_steps(pe, NS, (2, part_of(body, range(0, 2))), (1, turn), (2, part_of(body, range(2, 4))), (1, gate_logits),
                       (2, part_of(body, range(4, EX))))
            for y in range(EX - LATER, Y):
                outputs(NS - 1, (NS - 1) % 2, y)

        @block.scalar
        def _(act):
            def front(i, u, n):
                act.wait_ge(t_done, i + 1)
                wait(act, h_done, (i - 1) * EX * 4)
                act.activation(xnT_high[:, u, :], t_ps[:, :], ACT.Copy).then_inc(high_ready, 1)
                act.activation(xnT[:, u, :], t_ps[:, :], ACT.Copy).then_inc(t_ready, 1)

            def exponentials(i, u, n):
                act.wait_ge(route, i * ROUTE + EXP_INPUT)
                if layer == 0:
                    act.activation(ex[:, :, :], shifted[:, :, :], ACT.Exp).then_inc(exped, 1)
                else:
                    act.activation(ex[:, :, :], shifted[:, :, :], ACT.Tanh, scale=0.5).then_inc(exped, 1)

            def shift_linear(i, e):
                act.wait_ge(linear_clamped, i * EX + e + 1)
                act.activation(prod[:, e % R, 1, :], prod[:, e % R, 1, :], ACT.Copy, bias=0.5, scale=0.5)\
                    .then_inc(linear_ready, 1)

            def weigh(i, u, e):
                act.wait_ge(y_done, i * Y + e + 1)
                if e == 0:
                    act.wait_ge(cw_ready, i + 1)
                wait(act, added, i * Y + e + 1 - W)
                if e == EX:
                    last = act.activation(weighed[:, e % W], y_ps[:, e % 2, :].rearrange("p (j d) -> p j d", d=D), ACT.Copy)
                else:
                    for j in range(JT):
                        last = act.activation(weighed[:, e % W, j, :], y_ps[:, e % 2, j * P:(j + 1) * P], ACT.Copy,
                                              scale=cw[:, u, j, e:e + 1])
                last.then_inc(weighed_ready, 1)

            def body(i, u, n, e):
                m = i * EX + e
                for half in range(2):
                    act.wait_ge(h_done, 4 * m + 2 * half + 1)
                    wait(act, product_ready, 2 * (m - R) + half + 1)
                    if layer == 0:
                        act.activation(first[:, e % R, half, :], h_ps[:, 2 * half, :], ACT.Identity,
                                       bias=up_b[:, e, 2 * half:2 * half + 1]).then_inc(first_ready, 1)
                    else:
                        act.activation(first[:, e % R, half, :], h_ps[:, 2 * half, :], ACT.Silu).then_inc(first_ready, 1)
                if layer == 0:
                    back, x = before(e)
                    if earlier(i, back):
                        shift_linear(i - back, x)
                    act.wait_ge(gate_clamped, m + 1)
                    wait(act, gated_ready, m - R + 1)
                    act.activation(tanh[:, e % R, :], prod[:, e % R, 0, :], ACT.Tanh, scale=ALPHA / 2).then_inc(tanh_ready, 1)
                    for back, y in outputs_beside(e, LATER):
                        if earlier(i, back):
                            weigh(i - back, (u - back) % 2, y)
                if e == 4 and layer == 0:
                    act.wait_ge(c_done, i + 1)
                    wait(act, y_done, i * Y)
                    act.activation(cwT[:, :], c_ps[:, :], ACT.Copy).then_inc(c_ready, 1)

            act.wait_ge(w_in, WEIGHTS)
            def part_up(i, u, n):
                if isinstance(i, int) and i == 0:
                    for group, arrived in zip(GROUPS, up_in):
                        at = slice(group[0], group[-1] + 1)
                        act.wait_ge(arrived, 16)
                        act.activation(up_high[:, at, :, :].rearrange("p e b f -> p (e b f)"),
                                       up[:, at, :, :].rearrange("p e b f -> p (e b f)"), ACT.Copy).then_inc(up_high_ready, 1)

            over_steps(act, NS, (2, part_of(body, range(0, 2))), (1, front), (2, part_of(body, range(2, 5))), (1, exponentials),
                       (2, part_of(body, range(5, EX))), (1, part_up))
            if layer == 0:
                shift_linear(NS - 1, EX - 1)
                for y in range(EX - LATER, Y):
                    weigh(NS - 1, (NS - 1) % 2, y)

        @block.vector
        def _(dve):
            start_chain, then = chain_of(dve, route, ROUTE, apart_dve)

            def measure_rows(i, u, n):
                dve.wait_ge(x_in[u], n * 16 + 16)
                measure(dve, rows[:, u], i)

            def normalise(i, u, n):
                wait(dve, t_done, i - 1)
                apply(dve, xn[:, u], rows[:, u], i, xn_ready)

            def scores(i, u, n):
                start_chain(i)
                logits = t_ps[:, 0:JT * E].rearrange("p (j e) -> p j e", e=E)
                dve.wait_ge(logits_done, i + 1)
                if layer == 0:
                    then(dve.tensor_reduce(mx[:, :], logits, axis=AX.X, op=ALU.max))
                    then(dve.tensor_tensor(shifted[:, :, :], logits, wide(mx), ALU.subtract))
                else:
                    then(dve.tensor_copy(biased[:, :, :], logits), before=True)
                    for j in range(JT):
                        last = dve.max(best[:, j, :], biased[:, j, :])
                    then(last)
                    then(dve.tensor_tensor(both[:, :, :], best[:, :, 0:1], best[:, :, 1:2], ALU.add))
                    then(dve.scalar_tensor_tensor(out=shifted[:, :, :], in0=biased[:, :, :], scalar=2.0,
                                                  in1=both[:, :, :].broadcast_to([P, JT, E]), op0=ALU.mult, op1=ALU.subtract))

            def compare(i, u, n):
                start_chain(i, EXP_INPUT)
                dve.wait_ge(exped, i + 1)
                if layer == 0:
                    then(dve.tensor_reduce(total[:, :], ex[:, :, :], axis=AX.X, op=ALU.add))
                    then(dve.reciprocal(share[:, :], total[:, :]))
                    then(dve.tensor_tensor(score[:, :, :], ex[:, :, :], wide(share), ALU.mult))
                    then(dve.tensor_tensor(biased[:, :, :], score[:, :, :], gate_b[:, None, :].broadcast_to([P, JT, E]),
                                           ALU.add), before=True)
                    for j in range(JT):
                        last = dve.max(best[:, j, :], biased[:, j, :])
                    then(last)
                second = best[:, :, 1:2].broadcast_to([P, JT, E])
                dve.tensor_tensor(above[:, :, :], biased[:, :, :], second, ALU.is_gt)
                then(dve.tensor_tensor(level[:, :, :], biased[:, :, :], second, ALU.is_equal))

            def pick(i, u, n):
                start_chain(i, ROUTE - (4 if layer == 0 else 5))
                dve.tensor_reduce(above_n[:, :], above[:, :, :], axis=AX.X, op=ALU.add)
                then(dve.tensor_tensor_scan(rank[:, :, :].rearrange("p j e -> p (j e)"), not_first[:, :],
                                            level[:, :, :].rearrange("p j e -> p (j e)"), 0.0, ALU.mult, ALU.add))
                then(dve.tensor_tensor(rank[:, :, :], rank[:, :, :], wide(above_n), ALU.add))
                then(dve.scalar_tensor_tensor(out=level[:, :, :], in0=rank[:, :, :], scalar=2.0, in1=level[:, :, :],
                                              op0=ALU.is_le, op1=ALU.mult))
                then(dve.tensor_tensor(picked[:, :, :], above[:, :, :], level[:, :, :], ALU.add))
                dve.wait_ge(cw_set, 2)
                if layer == 0:
                    dve.tensor_tensor(cw[:, u, :, 0:E], picked[:, :, :], score[:, :, :], ALU.mult).then_inc(cw_ready, 1)
                else:
                    then(dve.scalar_tensor_tensor(out=ex[:, :, :], in0=ex[:, :, :], scalar=1.0, in1=picked[:, :, :],
                                                  op0=ALU.add, op1=ALU.mult))
                    dve.tensor_scalar(cw[:, u, :, 0:E], ex[:, :, :], 0.5, None, ALU.mult).then_inc(cw_ready, 1)

            def clamp_gate(i, e):
                m = i * EX + e
                dve.wait_ge(product_ready, 2 * m + 1)
                dve.tensor_scalar(prod[:, e % R, 0, :], prod[:, e % R, 0, :], LIMIT, None, ALU.min).then_inc(gate_clamped, 1)

            def gate(i, e):
                m = i * EX + e
                dve.wait_ge(tanh_ready, m + 1)
                wait(dve, hidden_ready, m - R + 1)
                dve.scalar_tensor_tensor(out=gated[:, e % R, :], in0=tanh[:, e % R, :], scalar=1.0, in1=prod[:, e % R, 0, :],
                                         op0=ALU.add, op1=ALU.mult).then_inc(gated_ready, 1)

            def products(i, u, e):
                m = i * EX + e
                for half in range(2):
                    if half == 1 and layer == 0:
                        clamp_gate(i, e)
                    dve.wait_ge(first_ready, 2 * m + half + 1)
                    dve.wait_ge(h_done, 4 * m + 2 * half + 2)
                    if layer == 0:
                        wait(dve, hidden_ready, m - R + 1)
                        dve.scalar_tensor_tensor(
                            out=prod[:, e % R, half, :], in0=h_ps[:, 2 * half + 1, :], scalar=up_b[:, e, 2 * half + 1:2 * half + 2],
                            in1=first[:, e % R, half, :], op0=ALU.add, op1=ALU.mult).then_inc(product_ready, 1)
                    else:
                        wait(dve, y_done, m - R + 1)
                        dve.tensor_tensor(hidden[:, e % R, half, :], h_ps[:, 2 * half + 1, :], first[:, e % R, half, :],
                                          ALU.mult).then_inc(product_ready, 1)
                if layer == 0:
                    back, x = before(e)
                    if earlier(i, back):
                        gate(i - back, x)
                else:
                    dve.wait_ge(product_ready, 2 * m + 2)
                    dve.sem_inc(hidden_ready, 1)

            def add(i, u, e, n=NS // 2 - 1):
                if e == 0:
                    dve.wait_ge(acc_in[u], n * 16 + 16)
                    dve.wait_ge(cw_ready, i + 1)
                else:
                    dve.wait_ge(added, i * Y + e)
                if layer == 0:
                    dve.wait_ge(weighed_ready, i * Y + e + 1)
                    dve.tensor_tensor(acc[:, u], weighed[:, e % W], acc[:, u], ALU.add).then_inc(added, 1)
                    return
                dve.wait_ge(y_done, i * Y + e + 1)
                for j in range(JT):
                    last = dve.scalar_tensor_tensor(
                        out=acc[:, u, j, :], in0=y_ps[:, e % 2, j * P:(j + 1) * P], scalar=cw[:, u, j, e:e + 1],
                        in1=acc[:, u, j, :], op0=ALU.mult, op1=ALU.add)
                last.then_inc(added, 1)

            def body(i, u, n, e):
                products(i, u, e)
                for back, y in outputs_beside(e, ADD_LATER):
                    if earlier(i, back):
                        add(i - back, (u - back) % 2, y, n)

            dve.wait_ge(w_in, WEIGHTS)

            def part_up(i, u, n):
                if isinstance(i, int) and i == 0:
                    for g, group in enumerate(GROUPS):
                        at = slice(group[0], group[-1] + 1)
                        dve.wait_ge(up_high_ready, g + 1)
                        dve.tensor_tensor(up_low[:, at, :, :], up[:, at, :, :], up_high[:, at, :, :].bitcast(F32), ALU.subtract)\
                            .then_inc(up_low_ready, 1)

            low_parts = ((1, lambda i, u, n: part_rows(dve, i, u)),) if layer == 1 else ()
            over_steps(dve, NS, (2, part_of(body, range(0, 2))), (0, measure_rows), (2, part_of(body, range(2, 4))), (0, normalise),
                       *low_parts, (2, part_of(body, range(4, 5))), (1, scores), (2, part_of(body, range(5, 6))), (1, compare),
                       (2, part_of(body, range(6, 7))), (1, pick), (2, part_of(body, range(7, EX))), (1, part_up))
            if layer == 0:
                gate(NS - 1, EX - 1)
            for y in range(EX - ADD_LATER, Y):
                add(NS - 1, (NS - 1) % 2, y)


def context_and_gated(nc, io):
    with phase(nc, "gated") as (sb, ps, sem, sems, pair, open_block):
        C, KV = 4, 64
        ident = sb("ident", [P, P])
        gain, offset, cgain, coffset = (sb(n, [P, 1]) for n in ("gain", "offset", "cgain", "coffset"))
        wkv, w1, w2 = sb("wkv", [P, 2 * KV]), sb("w1", [P, 2 * C * P]), sb("w2", [P, C, D])
        rows, ctx, xn, xn2, cn, out = (sb(n, [P, 2, JT, D]) for n in ("rows", "ctx", "xn", "xn2", "cn", "out"))
        xnT, cnT = sb("xnT", [P, 2, ST]), sb("cnT", [P, 2, ST])
        xnT_high, xnT_low = (sb(n, [P, 2, ST], F32R) for n in ("xnT_high", "xnT_low"))
        w1_high, w1_low = (sb(n, [P, 2 * C * P], F32R) for n in ("w1_high", "w1_low"))
        key, value = sb("key", [KV, 2, ST]), sb("value", [P, 2, JT, KV])
        silu, hidden = sb("silu", [P, 2, ST]), sb("hidden", [P, C, ST])
        t_ps, c_ps, k_ps = (ps(n, [P, ST]) for n in ("t_ps", "c_ps", "k_ps"))
        v_ps = c_ps
        h_ps = ps("h_ps", [P, 2, 2, ST])
        y_ps = ps("y_ps", [P, ST])
        norm, norm2, cnorm = (layer_norm(sb, sems, n) for n in ("ln", "ln2", "cln"))
        x_in, ctx_in, out_in, xnT_stored, kv_stored, out_stored = (
            pair(n) for n in ("x_in", "ctx_in", "out_in", "xnT_stored", "kv_stored", "out_stored"))
        w_in, xn_ready, xn2_ready, cn_ready, t_done, t_ready, c_done, c_ready, k_done, k_ready, v_done, v_ready, \
            h_done, silu_ready, hidden_ready, y_done, out_ready, w1_parted, high_ready, low_ready, apart_sp = sems(
                "w_in", "xn_ready", "xn2_ready", "cn_ready", "t_done", "t_ready", "c_done", "c_ready", "k_done",
                "k_ready", "v_done", "v_ready", "h_done", "silu_ready", "hidden_ready", "y_done", "out_ready", "w1_parted",
                "high_ready", "low_ready", "apart_sp")
        block = open_block()
        weights = ((ident[:, :], io["ident"][:, :]), (gain[:, :], io["L1_xattn_ln_g"][:, :]), (offset[:, :], io["L1_xattn_ln_b"][:, :]),
                   (cgain[:, :], io["L1_xattn_cln_g"][:, :]), (coffset[:, :], io["L1_xattn_cln_b"][:, :]),
                   (wkv[:, :], io["xkv"][:, :]), (w1[:, :], io["xw1"][:, :]), (w2[:, :, :], io["xw2"][:, :, :]))
        WEIGHTS = 16 * len(weights)

        @block.sync
        def _(sp):
            def load(i, u, n):
                wait(sp, xn_ready, i - 1)
                sp.dma_start(rows[:, u], rows_of(io["x4"], i, ST)).then_inc(x_in[u], 16)
                wait(sp, cn_ready, i - 1)
                sp.dma_start(ctx[:, u], rows_of(io["ctx"], i, ST)).then_inc(ctx_in[u], 16)
                if isinstance(i, int) and i == 0:
                    for dst, src in weights:
                        sp.dma_start(dst, src).then_inc(w_in, 16)

            def store(i, u, n):
                at = bass.ds(i * ST, ST)
                sp.wait_ge(t_ready, i + 1)
                apart(sp, apart_sp)
                sp.dma_start(io["xnT"][:, at], xnT[:, u, :]).then_inc(xnT_stored[u], 16)
                sp.wait_ge(k_ready, i + 1)
                sp.dma_start(io["kT"][:, at], key[:, u, :]).then_inc(kv_stored[u], 16)
                sp.wait_ge(v_ready, i + 1)
                sp.dma_start(rows_of(io["v"], i, ST), value[:, u]).then_inc(kv_stored[u], 16)

            def store_rows(i, u, n):
                sp.wait_ge(out_ready, i + 1)
                sp.dma_start(rows_of(io["x5"], i, ST), out[:, u]).then_inc(out_stored[u], 16)

            def load_residual(i, u, n):
                wait(sp, out_stored[u], n * 16)
                sp.dma_start(out[:, u], rows_of(io["x4"], i, ST)).then_inc(out_in[u], 16)

            over_steps(sp, NS, (0, load), (3, store_rows), (2, store), (1, load_residual))
            for u in range(2):
                sp.wait_ge(out_stored[u], 16 * (NS // 2))
                sp.wait_ge(xnT_stored[u], 16 * (NS // 2))
                sp.wait_ge(kv_stored[u], 32 * (NS // 2))

        @block.gpsimd
        def _(pool):
            for each in (norm, norm2, cnorm):
                each[0](pool)
            over_steps(pool, NS, *((0, lambda i, u, n, each=each: each[2](pool, i)) for each in (norm, cnorm, norm2)))

        @block.vector
        def _(dve):
            def measure_rows(i, u, n):
                dve.wait_ge(x_in[u], n * 16 + 16)
                norm[1](dve, rows[:, u], i)

            def measure_context(i, u, n):
                dve.wait_ge(ctx_in[u], n * 16 + 16)
                cnorm[1](dve, ctx[:, u], i)

            def normalise(i, u, n):
                norm[3](dve, xn[:, u], rows[:, u], i, xn_ready)

            def measure_again(i, u, n):
                dve.wait_ge(xn_ready, i + 1)
                norm2[1](dve, xn[:, u], i)

            def normalise_context(i, u, n):
                wait(dve, c_done, i - 1)
                cnorm[3](dve, cn[:, u], ctx[:, u], i, cn_ready)

            def normalise_again(i, u, n):
                wait(dve, t_done, i - 1)
                norm2[3](dve, xn2[:, u], xn[:, u], i, xn2_ready)

            def part_rows(i, u, n):
                dve.wait_ge(high_ready, i + 1)
                wait(dve, h_done, (i - 1) * 2 * C)
                dve.tensor_tensor(xnT_low[:, u, :], xnT[:, u, :], xnT_high[:, u, :].bitcast(F32), ALU.subtract)\
                    .then_inc(low_ready, 1)

            def keys_and_values(i, u, n):
                dve.wait_ge(k_done, i + 1)
                wait(dve, kv_stored[u], n * 32)
                dve.tensor_copy(key[:, u, :], k_ps[0:KV, :]).then_inc(k_ready, 1)
                dve.wait_ge(v_done, i + 1)
                dve.tensor_copy(value[:, u], v_ps[:, 0:JT * KV].rearrange("p (j d) -> p j d", d=KV)).then_inc(v_ready, 1)

            def feed_forward(c):
                def stage(i, u, n):
                    dve.wait_ge(h_done, 2 * (i * C + c) + 2)
                    dve.wait_ge(silu_ready, i * C + c + 1)
                    if c == 0:
                        wait(dve, y_done, i)
                    dve.tensor_tensor(hidden[:, c, :], silu[:, c % 2, :], h_ps[:, c % 2, 1, :], ALU.mult)\
                        .then_inc(hidden_ready, 1)
                return stage

            def add(i, u, n):
                dve.wait_ge(out_in[u], n * 16 + 16)
                dve.wait_ge(y_done, i + 1)
                dve.tensor_tensor(out[:, u], y_ps[:, :].rearrange("p (j d) -> p j d", d=D), out[:, u], ALU.add)\
                    .then_inc(out_ready, 1)

            def part_w1(i, u, n):
                if isinstance(i, int) and i == 0:
                    dve.wait_ge(w_in, WEIGHTS)
                    dve.tensor_copy(w1_high[:, :], w1[:, :]).then_inc(w1_parted, 1)
                    dve.wait_ge(w1_parted, 1)
                    dve.tensor_tensor(w1_low[:, :], w1[:, :], w1_high[:, :].bitcast(F32), ALU.subtract).then_inc(w1_parted, 1)

            over_steps(dve, NS, (0, measure_rows), (2, feed_forward(0)), (0, measure_context), (0, normalise),
                       (2, feed_forward(1)), (0, measure_again), (0, normalise_context), (2, feed_forward(2)), (1, part_rows),
                       (2, feed_forward(3)), (1, keys_and_values), (0, normalise_again), (2, add),
                       (0, part_w1))

        @block.tensor
        def _(pe):
            def turn(i, u, n):
                pe.wait_ge(cn_ready, i + 1)
                wait(pe, v_ready, i)
                for j in range(JT):
                    last = pe.transpose(c_ps[:, j * P:(j + 1) * P], cn[:, u, j, :], ident[:, :])
                last.then_inc(c_done, 1)
                pe.wait_ge(xn2_ready, i + 1)
                wait(pe, t_ready, i)
                for j in range(JT):
                    last = pe.transpose(t_ps[:, j * P:(j + 1) * P], xn2[:, u, j, :], ident[:, :])
                last.then_inc(t_done, 1)

            def keys_and_values(i, u, n):
                pe.wait_ge(c_ready, i + 1)
                wait(pe, k_ready, i)
                pe.matmul(k_ps[0:KV, :], wkv[:, 0:KV], cnT[:, u, :], start=True, stop=True).then_inc(k_done, 1)
                for j in range(JT):
                    last = pe.matmul(v_ps[:, j * KV:(j + 1) * KV], cnT[:, u, j * P:(j + 1) * P], wkv[:, KV:2 * KV],
                                     start=True, stop=True)
                last.then_inc(v_done, 1)

            def feed_forward(i, u, n):
                pe.wait_ge(w1_parted, 2)
                pe.wait_ge(low_ready, i + 1)
                for c in range(C):
                    wait(pe, silu_ready, i * C + c - 1)
                    wait(pe, hidden_ready, i * C + c - 1)
                    for part in range(2):
                        f = slice(((1 - part) * C + c) * P, ((1 - part) * C + c + 1) * P)
                        product_of_parts(pe, h_ps[:, c % 2, part, :], (w1_high[:, f], w1_low[:, f]),
                                         (xnT_high[:, u, :], xnT_low[:, u, :])).then_inc(h_done, 1)

            def down(i, u, n):
                pe.wait_ge(hidden_ready, i * C + C)
                wait(pe, out_ready, i)
                for j in range(JT):
                    at = slice(j * P, (j + 1) * P)
                    for c in range(C):
                        last = pe.matmul(y_ps[:, at], hidden[:, c, at], w2[:, c, :], start=(c == 0), stop=(c == C - 1))
                last.then_inc(y_done, 1)

            pe.wait_ge(w_in, WEIGHTS)
            over_steps(pe, NS, (1, turn), (2, feed_forward), (1, keys_and_values), (2, down))

        @block.scalar
        def _(act):
            def evacuate_context(i, u, n):
                act.wait_ge(c_done, i + 1)
                wait(act, v_done, i - 1)
                act.activation(cnT[:, u, :], c_ps[:, :], ACT.Identity, bias=coffset[:, 0:1], scale=cgain[:, 0:1])\
                    .then_inc(c_ready, 1)

            def evacuate_rows(i, u, n):
                act.wait_ge(t_done, i + 1)
                wait(act, low_ready, i - 1)
                wait(act, xnT_stored[u], n * 16)
                act.activation(xnT[:, u, :], t_ps[:, :], ACT.Identity, bias=offset[:, 0:1], scale=gain[:, 0:1])\
                    .then_inc(t_ready, 1)

                act.wait_ge(t_ready, i + 1)
                wait(act, h_done, (i - 1) * 2 * C)
                act.activation(xnT_high[:, u, :], xnT[:, u, :], ACT.Copy).then_inc(high_ready, 1)

            def gates(c):
                def stage(i, u, n):
                    act.wait_ge(h_done, 2 * (i * C + c) + 1)
                    wait(act, hidden_ready, i * C + c - 1)
                    act.activation(silu[:, c % 2, :], h_ps[:, c % 2, 0, :], ACT.Silu).then_inc(silu_ready, 1)
                return stage

            act.wait_ge(w_in, WEIGHTS)
            over_steps(act, NS, (1, evacuate_context), (2, gates(0)), (1, evacuate_rows), *((2, gates(c)) for c in range(1, C)))


def wide_attention(nc, io):
    with phase(nc, "wide") as (sb, ps, sem, sems, pair, open_block):
        HP, KV = H // 2, 64
        ident, wq, wo = sb("ident", [P, P]), sb("wq", [P, HP, P]), sb("wo", [P, HP, D])
        qin = sb("qin", [P, 2, 2 * TILE])
        kblock = sb("kblock", [P, 2, 2, TILE])
        vblock = sb("vblock", [P, 2, 2, 2, KV])
        mask = sb("mask", [P, 2, S])
        rows, fin = sb("rows", [P, 2, D]), sb("fin", [P, 2, D])
        qT, oT = sb("qT", [P, 2, HP, 2 * TILE]), sb("oT", [P, HP, 2, S])
        scored, e = (sb(n, [P, 2, HK]) for n in ("scored", "e"))
        pt_high, pt_low = (sb(n, [P, 2, HP, TILE], F32R) for n in ("pt_high", "pt_low"))
        v_high, v_low = (sb(n, [P, 2, 2, 2 * KV], F32R) for n in ("v_high", "v_low"))
        shifted = sb("shifted", [P, 2, HK])
        top, total, inv = (sb(n, [P, 2, H]) for n in ("top", "total", "inv"))
        a_ps, s_ps, t_ps, o_ps = (ps(n, [P, HK]) for n in ("a_ps", "s_ps", "t_ps", "o_ps"))
        q_in, k_in, v_in, m_in, x_in, stored = (pair(x) for x in ("q_in", "k_in", "v_in", "m_in", "x_in", "stored"))
        w_in, cleared, q_done, q_ready, s_done, masked, topped, shifted_ready, e_ready, pt_done, pt_ready, o_done, summed, \
            inverted, share_ready, ot_ready, y_done, fin_ready, pt_low_ready, v_high_ready, v_low_ready, apart_pool = sems(
                "w_in", "cleared", "q_done", "q_ready", "s_done", "masked", "topped", "shifted_ready", "e_ready",
                "pt_done", "pt_ready", "o_done", "summed", "inverted", "share_ready", "ot_ready", "y_done",
                "fin_ready", "pt_low_ready", "v_high_ready", "v_low_ready", "apart_pool")
        set_up_high, set_up_low, part_high, part_low, query_products, wq_parted, low_ready = query_parts(
            sb, sems, qin, wq[:, :, :], lambda act: act.wait_ge(w_in, 48), q_in, q_done)
        block = open_block()
        scale = KV ** -0.5
        by_head = lambda t: t.rearrange("p (h k) -> p h k", k=S)
        wide = lambda t: t[:, :, None].broadcast_to([P, H, S])

        @block.sync
        def _(sp):
            sp.dma_start(ident[:, :], io["ident"][:, :]).then_inc(w_in, 16)
            sp.dma_start(wq[:, :, :], io["xq"][:, :, :]).then_inc(w_in, 16)
            sp.dma_start(wo[:, :, :], io["xout"][:, :, :]).then_inc(w_in, 16)
            sp.wait_ge(cleared, 1)

            def load_queries(i, u, n):
                if u % 2 == 0:
                    wait(sp, low_ready, 2 * n + u // 2 - 1)
                    sp.dma_start(qin[:, u // 2, :], io["xnT"][:, bass.ds(i * TILE, 2 * TILE)]).then_inc(q_in[u // 2], 16)

            def load_keys(i, u, n):
                wait(sp, s_done, i - 1)
                for c in range(2):
                    sp.dma_start(kblock[c * S:(c + 1) * S, u, c, :], io["kT"][:, bass.ds(i * TILE, TILE)])\
                        .then_inc(k_in[u], 16)

            def load_mask(i, u, n):
                wait(sp, masked, i - 1)
                sp.dma_start(mask[:, u, :], io["mask"][bass.ds(i * TILE, TILE), :]).then_inc(m_in[u], 16)

            def load_values(i, u, n):
                wait(sp, v_low_ready, i - 1)
                for c in range(2):
                    sp.dma_start(vblock[c * S:(c + 1) * S, u, :, c, :], io["v"][bass.ds(i * TILE, TILE), :]
                                 .rearrange("(b k) d -> k b d", b=2)).then_inc(v_in[u], 16)

            def load_residual(i, u, n):
                wait(sp, fin_ready, i - 1)
                sp.dma_start(rows[:, u, :], io["x5"][bass.ds(i * TILE, TILE), :]).then_inc(x_in[u], 16)

            def store(i, u, n):
                sp.wait_ge(fin_ready, i + 1)
                sp.dma_start(io["x6"][bass.ds(i * TILE, TILE), :], fin[:, u, :]).then_inc(stored[u], 16)

            over_steps(sp, NT, (0, load_queries), (2, by_two(load_keys)), (2, by_two(load_mask)), (4, by_two(load_values)),
                       (6, by_two(load_residual)), (8, by_two(store)), turns=4)
            for u in range(2):
                sp.wait_ge(stored[u], 16 * (NT // 2))

        @block.gpsimd
        def _(pool):
            pool.memset(kblock[:, :, :, :], 0.0)
            pool.memset(vblock[:, :, :, :, :], 0.0).then_inc(cleared, 1)

            def shift(i, u, n):
                pool.wait_ge(topped, i + 1)
                wait(pool, e_ready, i - 1)
                pool.tensor_tensor(by_head(shifted[:, u, :]), by_head(scored[:, u, :]), wide(top[:, u, :]),
                                   ALU.subtract).then_inc(shifted_ready, 1)

            def part_values(i, u, n):
                pool.wait_ge(v_high_ready, i + 1)
                apart(pool, apart_pool)
                pool.wait_ge(v_in[u], n * 32 + 32)
                apart(pool, apart_pool)
                wait(pool, o_done, i - 1)
                pool.tensor_tensor(v_low[:, u], vblock[:, u, :, :, :].rearrange("p b c d -> p b (c d)"),
                                   v_high[:, u].bitcast(F32), ALU.subtract).then_inc(v_low_ready, 1)

            over_steps(pool, NT, (0, shift), (2, part_values))

        @block.tensor
        def _(pe):
            def queries(i, u, n):
                wait(pe, q_ready, i)
                wait(pe, fin_ready, i - 6)
                query_products(pe, a_ps, u, n)

            def scores(i, u, n):
                v, u, n = u // 2, u % 2, 2 * n + u // 2
                pe.wait_ge(q_ready, 2 * n + 2)
                pe.wait_ge(k_in[u], n * 32 + 32)
                wait(pe, masked, i)
                for g in range(HP):
                    for b in range(2):
                        last = pe.matmul(s_ps[b * S:(b + 1) * S, g * P:(g + 1) * P], qT[:, v, g, u * TILE + b * S:u * TILE + (b + 1) * S],
                                         kblock[:, u, :, b * S:(b + 1) * S], start=True, stop=True,
                                         tile_position=(0, b * S))
                last.then_inc(s_done, 1)

            def project(i, u, n):
                pe.wait_ge(ot_ready, i + 1)
                wait(pe, q_ready, at_most(i + 7, NT))
                wait(pe, fin_ready, i)
                for g in range(HP):
                    last = pe.matmul(a_ps[:, 0:D], oT[:, g, :, :].rearrange("p b s -> p (b s)"), wo[:, g, :], start=(g == 0), stop=(g == HP - 1))
                last.then_inc(y_done, 1)

            def weigh(i, u, n):
                pe.wait_ge(pt_ready, i + 1)
                pe.wait_ge(pt_low_ready, i + 1)
                pe.wait_ge(v_low_ready, i + 1)
                wait(pe, ot_ready, i)
                for b in range(2):
                    at = slice(b * S, (b + 1) * S)
                    last = product_of_parts(pe, o_ps[:, b * ST:(b + 1) * ST], (v_high[:, u, b, :], v_low[:, u, b, :]),
                                            (pt_high[:, u, :, at], pt_low[:, u, :, at]))
                last.then_inc(o_done, 1)

            def turn_weights(i, u, n):
                pe.wait_ge(share_ready, i + 1)
                wait(pe, pt_low_ready, i)
                for g in range(HP):
                    last = pe.transpose(t_ps[:, g * P:(g + 1) * P], e[:, u, g * P:(g + 1) * P], ident[:, :])
                last.then_inc(pt_done, 1)

            pe.wait_ge(w_in, 48)
            pe.wait_ge(wq_parted, 2)
            over_steps(pe, NT, (1, queries), (6, by_two(turn_weights)), (3, scores), (7, by_two(project)), (6, by_two(weigh)),
                       turns=4)

        @block.vector
        def _(dve):
            def mask_scores(i, u, n):
                dve.wait_ge(s_done, i + 1)
                dve.wait_ge(m_in[u], n * 16 + 16)
                wait(dve, shifted_ready, i - 1)
                dve.tensor_tensor(by_head(scored[:, u, :]), by_head(s_ps[:, :]),
                                  mask[:, u, None, :].broadcast_to([P, H, S]), ALU.add).then_inc(masked, 1)

            def find_top(i, u, n):
                dve.wait_ge(masked, i + 1)
                dve.tensor_reduce(top[:, u, :], by_head(scored[:, u, :]), axis=AX.X, op=ALU.max).then_inc(topped, 1)

            def normalise(i, u, n):
                dve.wait_ge(e_ready, i + 1)
                dve.tensor_reduce(total[:, u, :], by_head(e[:, u, :]), axis=AX.X, op=ALU.add).then_inc(summed, 1)
                dve.wait_ge(summed, i + 1)
                dve.reciprocal(inv[:, u, :], total[:, u, :]).then_inc(inverted, 1)
                dve.wait_ge(inverted, i + 1)
                dve.tensor_tensor(by_head(e[:, u, :]), by_head(e[:, u, :]), wide(inv[:, u, :]), ALU.mult)\
                    .then_inc(share_ready, 1)

            def residual(i, u, n):
                dve.wait_ge(y_done, i + 1)
                dve.wait_ge(x_in[u], n * 16 + 16)
                wait(dve, stored[u], n * 16)
                dve.tensor_tensor(fin[:, u, :], a_ps[:, 0:D], rows[:, u, :], ALU.add).then_inc(fin_ready, 1)

            def part_weights(i, u, n):
                dve.wait_ge(pt_ready, i + 1)
                wait(dve, o_done, i - 1)
                dve.tensor_tensor(pt_low[:, u], t_ps[:, :].rearrange("p (g t) -> p g t", t=TILE),
                                  pt_high[:, u].bitcast(F32), ALU.subtract).then_inc(pt_low_ready, 1)

            set_up_low(dve)
            over_steps(dve, NT, (5, by_two(normalise)), (0, part_low(dve)), (6, by_two(part_weights)),
                       (3, by_two(mask_scores)), (7, by_two(residual)), (3, by_two(find_top)), turns=4)

        @block.scalar
        def _(act):
            def evacuate_weights(i, u, n):
                act.wait_ge(pt_done, i + 1)
                wait(act, o_done, i - 1)
                act.activation(pt_high[:, u], t_ps[:, :].rearrange("p (g t) -> p g t", t=TILE), ACT.Copy).then_inc(pt_ready, 1)

            def evacuate_queries(i, u, n):
                act.wait_ge(q_done, i + 1)
                wait(act, s_done, 4 * n + 2 * (u // 2) - 2)
                half = slice((u % 2) * (HP // 2), (u % 2 + 1) * (HP // 2))
                act.activation(qT[:, u // 2, half, :], a_ps[:, :].rearrange("p (g t) -> p g t", t=2 * TILE), ACT.Copy,
                               scale=scale).then_inc(q_ready, 1)

            def evacuate_outputs(i, u, n):
                act.wait_ge(o_done, i + 1)
                wait(act, y_done, i)
                act.activation(oT[:, :, :, :].rearrange("p g b s -> p b g s"), o_ps[:, :].rearrange("p (b g s) -> p b g s", b=2, s=S),
                               ACT.Copy).then_inc(ot_ready, 1)

            def exponentials(i, u, n):
                act.wait_ge(shifted_ready, i + 1)
                wait(act, pt_done, i - 1)
                act.activation(e[:, u, :], shifted[:, u, :], ACT.Exp).then_inc(e_ready, 1)

            def part_values(i, u, n):
                act.wait_ge(v_in[u], n * 32 + 32)
                wait(act, o_done, i - 1)
                act.activation(v_high[:, u], vblock[:, u, :, :, :].rearrange("p b c d -> p b (c d)"), ACT.Copy)\
                    .then_inc(v_high_ready, 1)

            set_up_high(act)
            over_steps(act, NT, (7, by_two(evacuate_outputs)), (0, part_high(act)), (1, evacuate_queries),
                       (6, by_two(evacuate_weights)), (4, by_two(exponentials)), (5, by_two(part_values)), turns=4)


SCRATCH = {
    "QT": (D, TOK), "KT": (D, TOK), "V": (TOK, D), "AO": (TOK, D), "bias0": (P, HK), "xnT": (D, TOK),
    "latT": (64, TOK), "lat_w": (P, HK), "x2": (TOK, D), "x3": (TOK, D), "x4": (TOK, D), "x5": (TOK, D),
    "x6": (TOK, D), "kT": (64, TOK), "v": (TOK, 64),
}


def first_projection(nc, io):
    with joint_block(nc) as joint:
        tpms_bias(nc, io, joint)
        project(nc, io, 0, joint)


def second_projection(nc, io):
    with joint_block(nc) as joint:
        latent_weights(nc, io, joint)
        project(nc, io, 1, joint)


def build(nc, io, upto=99):
    io["latent"] = 64
    phases = [lambda: first_projection(nc, io),
              lambda: narrow_attention(nc, io, "attn0", True), lambda: close_attention(nc, io, 0),
              lambda: moe(nc, io, 0), lambda: second_projection(nc, io),
              lambda: narrow_attention(nc, io, "attn1", False), lambda: close_attention(nc, io, 1),
              lambda: context_and_gated(nc, io), lambda: wide_attention(nc, io), lambda: moe(nc, io, 1)]
    for part in phases[:upto]:
        part()


def constants():
    import numpy as np

    f = np.float32
    token = np.arange(TILE) % S
    pos = (np.arange(S, dtype=f) / f(S) * f(2.0 * math.pi)).astype(f)
    head = np.arange(P)[:, None] // HD == np.arange(H)[None, :]
    seen = token[:, None] >= np.arange(S)[None, :]
    decay = np.where(np.arange(ST) % S == 0, 0.0, 0.9).astype(f)
    first_expert = np.where(np.arange(JT * 8) % 8 == 0, 0.0, 1.0).astype(f)
    return {
        "ident": np.eye(P, dtype=f),
        "pos_q": pos[token][:, None],
        "pos_k": np.broadcast_to(pos, (P, S)),
        "pos_z": ((pos[token][:, None] + pos[None, :]) * f(0.5)).astype(f),
        "head_mask": head.astype(f),
        "copy_mask": (np.arange(P)[:, None] // S == np.arange(2)[None, :]).astype(f),
        "causal": np.tile(np.where(seen, 0.0, -1e30).astype(f), (1, H)),
        "decay": np.broadcast_to(decay, (P, ST)),
        "not_first": np.broadcast_to(first_expert, (P, JT * 8)),
    }


def layouts(x):
    import numpy as np

    col = lambda a: a.reshape(-1, 1)
    both = lambda routed, shared: np.concatenate([g(routed), g(shared)[None]], 0)
    w13 = lambda *n: both(*n).reshape(9, P, 2, D).transpose(3, 0, 2, 1)
    b13 = lambda *n: both(*n).reshape(9, P, 2).transpose(1, 0, 2)
    g = lambda n: x[n]
    return {
        "x": g("x").reshape(TOK, D),
        "ctx": g("ctx_1024").reshape(TOK, D),
        "ctxT": g("ctx_1024").reshape(TOK, D).T,
        "mask": g("mask_BxSxS2_ff0").reshape(TOK, S),
        **{n: g(n) for n in ("L0_attn_Wq", "L0_attn_Wk", "L0_attn_Wv", "L0_attn_Wo", "L0_attn_bo", "L0_attn_phase",
                             "L1_attn_basis_w", "L1_attn_core", "L1_attn_head_residual", "L1_attn_o_b")},
        **{n: col(g(n)) for n in ("L0_attn_bq", "L0_attn_bk", "L0_attn_bv", "L1_attn_v_b", "L1_xattn_ln_g",
                                  "L1_xattn_ln_b", "L1_xattn_cln_g", "L1_xattn_cln_b")},
        "L0_attn_threshold": g("L0_attn_threshold").reshape(1),
        "L0_attn_temperature": g("L0_attn_temperature").reshape(1),
        "basis_T": g("L1_attn_basis_w").T,
        "core_T": g("L1_attn_core").T,
        "L1_attn_v_wT": g("L1_attn_v_w").T,
        "L1_attn_o_wT": g("L1_attn_o_w").T,
        "gate0_T": g("L0_ffn_gate_w").T,
        "gate0_b": g("L0_ffn_gate_b"),
        "up0": np.stack([w13("L0_ffn_w1", "L0_ffn_sw1"), w13("L0_ffn_w3", "L0_ffn_sw3")], 3).reshape(D, 9, 4, P),
        "up0_b": np.stack([b13("L0_ffn_b1", "L0_ffn_sb1"), b13("L0_ffn_b3", "L0_ffn_sb3")], 3).reshape(P, 9, 4),
        "down0": both("L0_ffn_w2", "L0_ffn_sw2").transpose(2, 0, 1),
        "down0_b": both("L0_ffn_b2", "L0_ffn_sb2"),
        "xq": g("L1_xattn_Wq").reshape(D, 8, P),
        "xkv": g("L1_xattn_Wkv"),
        "xout": g("L1_xattn_Wout").reshape(8, P, D).transpose(1, 0, 2),
        "xw1": g("L1_xattn_W1"),
        "xw2": g("L1_xattn_W2").reshape(4, P, D).transpose(1, 0, 2),
        "gate1_T": g("L1_ffn_gate_w").T,
        "up1": g("L1_ffn_w12").reshape(8, 2, 2, P, D).transpose(4, 0, 2, 1, 3).reshape(D, 8, 4, P),
        "down1": g("L1_ffn_w3").reshape(8, D, 2, P).transpose(3, 0, 2, 1),
    }


def kernel(**inputs):
    import numpy as np
    import concourse.bacc as bacc
    from concourse.bass_utils import run_bass_kernel_spmd

    nc = bacc.Bacc("TRN2", target_bir_lowering=False, num_devices=1)
    arrays, io = {}, {}
    for name, a in {**constants(), **layouts({k: np.asarray(v) for k, v in inputs.items()})}.items():
        arrays[f"in_{name}"] = np.ascontiguousarray(a)
        dram = nc.dram_tensor(f"in_{name}", a.shape, mybir.dt.from_np(a.dtype), kind="ExternalInput").ap()
        io[name] = dram
    for name, shape in SCRATCH.items():
        io[name] = nc.dram_tensor(f"scratch_{name}", shape, F32, kind="Internal").ap()
    io["out"] = nc.dram_tensor("out", (TOK, D), F32, kind="ExternalOutput").ap()
    build(nc, io)
    result = run_bass_kernel_spmd(nc, [arrays], core_ids=[0])
    return result.results[0]["out"].reshape(B, S, D)
```
